# Optimizing a Trainium2 kernel written in Bass

```python
import numpy as np
import jax
import jax.numpy as jnp

def _softmax(x, axis=-1):
    return jax.nn.softmax(x, axis=axis)

def _gelu(x):
    return jax.nn.gelu(x, approximate=True)

def _silu(x):
    return jax.nn.silu(x)

def _sigmoid(x):
    return jax.nn.sigmoid(x)

def _layernorm(x, axis=-1, eps=1e-05):
    m = jnp.mean(x, axis=axis, keepdims=True)
    v = jnp.var(x, axis=axis, keepdims=True)
    return (x - m) / jnp.sqrt(v + eps)

def _scatter_add(tgt, idx, src, axis=0):
    return tgt.at[idx].add(src)

def _segment_sum(src, seg, n):
    return jax.ops.segment_sum(src, seg, n)
kernel_name = 'mk_conv_preact_d2_conv_nhwc1024_r4_466555'

def setup_inputs(seed: int=0):
    np.random.seed(seed)
    _w = jnp.asarray

    def _rec_inputs():
        import jax
        import jax.numpy as jnp
        _gk = jax.random.key(seed)
        x = -0.000125 + 0.9999 * jax.random.normal(jax.random.fold_in(_gk, 1), (32, 16, 16, 256), jnp.float32)
        return x
    x = _rec_inputs()

    def _L0_conv_setup():
        import math
        import jax, jax.numpy as jnp
        import numpy as np
        WIN = 8
        SHIFT = 4
        HEADS = 16
        LOG100 = math.log(100.0)

        def _rel_position_index(wh, ww):
            ch, cw = np.meshgrid(np.arange(wh), np.arange(ww), indexing='ij')
            coords = np.stack([ch.ravel(), cw.ravel()])
            rel = (coords[:, :, None] - coords[:, None, :]).transpose(1, 2, 0)
            rel[:, :, 0] += wh - 1
            rel[:, :, 1] += ww - 1
            rel[:, :, 0] *= 2 * ww - 1
            return rel.sum(-1).ravel()

        def _coords_table(wh, ww):
            rh = np.arange(-(wh - 1), wh, dtype=np.float32)
            rw = np.arange(-(ww - 1), ww, dtype=np.float32)
            t = np.stack(np.meshgrid(rh, rw, indexing='ij'), axis=-1)[None]
            t[..., 0] /= wh - 1
            t[..., 1] /= ww - 1
            t *= 8.0
            return np.sign(t) * np.log2(np.abs(t) + 1.0) / 3.0

        def _shift_mask(H, W, win, shift):
            m = np.zeros((H, W), np.int32)
            cnt = 0
            for hs in ((0, -win), (-win, -shift), (-shift, None)):
                for ws in ((0, -win), (-win, -shift), (-shift, None)):
                    m[hs[0]:hs[1], ws[0]:ws[1]] = cnt
                    cnt += 1
            nW = H // win * (W // win)
            m = m.reshape(H // win, win, W // win, win).transpose(0, 2, 1, 3).reshape(nW, win * win)
            return m[:, None, :] != m[:, :, None]
        key = jax.random.key(seed)
        ks = jax.random.split(key, 11)
        D, HID = (256, 128)
        s = 0.02
        return {'x': jax.random.normal(ks[0], (32, 16, 16, D), jnp.float32), 'Wq': jax.random.normal(ks[1], (D, D), jnp.float32) * s, 'Wk': jax.random.normal(ks[2], (D, D), jnp.float32) * s, 'Wv': jax.random.normal(ks[3], (D, D), jnp.float32) * s, 'bv': jax.random.normal(ks[4], (D,), jnp.float32) * s, 'Wo': jax.random.normal(ks[5], (D, D), jnp.float32) * s, 'bo': jax.random.normal(ks[6], (D,), jnp.float32) * s, 'logit_scale': jnp.full((HEADS, 1, 1), jnp.log(10.0), jnp.float32), 'cpb_w1': jax.random.normal(ks[7], (HID, 2), jnp.float32) * 0.5, 'cpb_b1': jax.random.normal(ks[8], (HID,), jnp.float32) * 0.1, 'cpb_w2': jax.random.normal(ks[9], (HEADS, HID), jnp.float32) * 0.1}
    _L0_conv_all = _L0_conv_setup()
    _L0_conv_in = {k: v for k, v in _L0_conv_all.items() if k in ('Wq', 'Wk', 'Wv', 'bv', 'Wo', 'bo', 'logit_scale', 'cpb_w1', 'cpb_b1', 'cpb_w2')}
    del _L0_conv_all

    def _L1_conv_setup():
        import jax, jax.numpy as jnp
        import numpy as np
        EMBED_DIM = 256
        NUM_HEADS = 16
        LB_HEADS = 8
        LA_HEADS = 8
        HEAD_DIM = EMBED_DIM // NUM_HEADS

        def _masked_attention(xf, Wq, Wk, Wv, lookahead):
            q = jnp.einsum('bnd,hed->bhne', xf, Wq)
            k = jnp.einsum('bnd,hed->bhne', xf, Wk)
            v = jnp.einsum('bnd,hed->bhne', xf, Wv)
            scale = 1.0 / jnp.sqrt(jnp.asarray(q.shape[-1], q.dtype))
            s = jnp.einsum('bhqe,bhke->bhqk', q, k) * scale
            n = s.shape[-1]
            i = jnp.arange(n)
            mask = i[:, None] <= i[None, :] if lookahead else i[:, None] >= i[None, :]
            s = jnp.where(mask, s, jnp.finfo(s.dtype).min)
            p = jax.nn.softmax(s, axis=-1)
            return jnp.einsum('bhqk,bhke->bhqe', p, v)
        key = jax.random.key(seed)
        ks = jax.random.split(key, 8)
        B, T, F, D = (2, 16, 32, EMBED_DIM)

        def xavier(k, shape):
            fan_out, fan_in = (shape[-2], shape[-1])
            lim = float(np.sqrt(6.0 / (fan_in + fan_out)))
            return jax.random.uniform(k, shape, jnp.float32, -lim, lim)
        return {'x': jax.random.normal(ks[0], (B, T, F, D), jnp.float32), 'Wq_lb': xavier(ks[1], (LB_HEADS, HEAD_DIM, D)), 'Wk_lb': xavier(ks[2], (LB_HEADS, HEAD_DIM, D)), 'Wv_lb': xavier(ks[3], (LB_HEADS, HEAD_DIM, D)), 'Wq_la': xavier(ks[4], (LA_HEADS, HEAD_DIM, D)), 'Wk_la': xavier(ks[5], (LA_HEADS, HEAD_DIM, D)), 'Wv_la': xavier(ks[6], (LA_HEADS, HEAD_DIM, D)), 'Wo': xavier(ks[7], (D, D))}
    _L1_conv_all = _L1_conv_setup()
    _L1_conv_in = {k: v for k, v in _L1_conv_all.items() if k in ('Wq_lb', 'Wk_lb', 'Wv_lb', 'Wq_la', 'Wk_la', 'Wv_la', 'Wo')}
    del _L1_conv_all
    return {'x': x, 'L0_conv_Wq': _L0_conv_in['Wq'], 'L0_conv_Wk': _L0_conv_in['Wk'], 'L0_conv_Wv': _L0_conv_in['Wv'], 'L0_conv_bv': _L0_conv_in['bv'], 'L0_conv_Wo': _L0_conv_in['Wo'], 'L0_conv_bo': _L0_conv_in['bo'], 'L0_conv_logit_scale': _L0_conv_in['logit_scale'], 'L0_conv_cpb_w1': _L0_conv_in['cpb_w1'], 'L0_conv_cpb_b1': _L0_conv_in['cpb_b1'], 'L0_conv_cpb_w2': _L0_conv_in['cpb_w2'], 'L1_conv_Wq_lb': _L1_conv_in['Wq_lb'], 'L1_conv_Wk_lb': _L1_conv_in['Wk_lb'], 'L1_conv_Wv_lb': _L1_conv_in['Wv_lb'], 'L1_conv_Wq_la': _L1_conv_in['Wq_la'], 'L1_conv_Wk_la': _L1_conv_in['Wk_la'], 'L1_conv_Wv_la': _L1_conv_in['Wv_la'], 'L1_conv_Wo': _L1_conv_in['Wo']}

def reference(x, L0_conv_Wq, L0_conv_Wk, L0_conv_Wv, L0_conv_bv, L0_conv_Wo, L0_conv_bo, L0_conv_logit_scale, L0_conv_cpb_w1, L0_conv_cpb_b1, L0_conv_cpb_w2, L1_conv_Wq_lb, L1_conv_Wk_lb, L1_conv_Wv_lb, L1_conv_Wq_la, L1_conv_Wk_la, L1_conv_Wv_la, L1_conv_Wo):
    import jax
    import jax.numpy as jnp

    def _L0_conv_ref(x, Wq, Wk, Wv, bv, Wo, bo, logit_scale, cpb_w1, cpb_b1, cpb_w2):
        import math
        import jax, jax.numpy as jnp
        import numpy as np
        WIN = 8
        SHIFT = 4
        HEADS = 16
        LOG100 = math.log(100.0)

        def _rel_position_index(wh, ww):
            ch, cw = np.meshgrid(np.arange(wh), np.arange(ww), indexing='ij')
            coords = np.stack([ch.ravel(), cw.ravel()])
            rel = (coords[:, :, None] - coords[:, None, :]).transpose(1, 2, 0)
            rel[:, :, 0] += wh - 1
            rel[:, :, 1] += ww - 1
            rel[:, :, 0] *= 2 * ww - 1
            return rel.sum(-1).ravel()

        def _coords_table(wh, ww):
            rh = np.arange(-(wh - 1), wh, dtype=np.float32)
            rw = np.arange(-(ww - 1), ww, dtype=np.float32)
            t = np.stack(np.meshgrid(rh, rw, indexing='ij'), axis=-1)[None]
            t[..., 0] /= wh - 1
            t[..., 1] /= ww - 1
            t *= 8.0
            return np.sign(t) * np.log2(np.abs(t) + 1.0) / 3.0

        def _shift_mask(H, W, win, shift):
            m = np.zeros((H, W), np.int32)
            cnt = 0
            for hs in ((0, -win), (-win, -shift), (-shift, None)):
                for ws in ((0, -win), (-win, -shift), (-shift, None)):
                    m[hs[0]:hs[1], ws[0]:ws[1]] = cnt
                    cnt += 1
            nW = H // win * (W // win)
            m = m.reshape(H // win, win, W // win, win).transpose(0, 2, 1, 3).reshape(nW, win * win)
            return m[:, None, :] != m[:, :, None]
        B, H, W, D = x.shape
        N = WIN * WIN
        d = D // HEADS
        nWh, nWw = (H // WIN, W // WIN)
        nW = nWh * nWw
        xs = jnp.roll(x, (-SHIFT, -SHIFT), axis=(1, 2))
        xw = xs.reshape(B, nWh, WIN, nWw, WIN, D).transpose(0, 1, 3, 2, 4, 5)
        xw = xw.reshape(B * nW, N, D)
        q = (xw @ Wq.T).reshape(-1, N, HEADS, d).transpose(0, 2, 1, 3)
        k = (xw @ Wk.T).reshape(-1, N, HEADS, d).transpose(0, 2, 1, 3)
        v = (xw @ Wv.T + bv).reshape(-1, N, HEADS, d).transpose(0, 2, 1, 3)
        qn = q / jnp.maximum(jnp.linalg.norm(q, axis=-1, keepdims=True), 1e-12)
        kn = k / jnp.maximum(jnp.linalg.norm(k, axis=-1, keepdims=True), 1e-12)
        scale = jnp.exp(jnp.minimum(logit_scale, LOG100))
        logits = jnp.einsum('bhnd,bhmd->bhnm', qn, kn) * scale
        table = jnp.asarray(_coords_table(WIN, WIN))
        hcpb = jax.nn.relu(table @ cpb_w1.T + cpb_b1) @ cpb_w2.T
        tab = hcpb.reshape(-1, HEADS)
        idx = jnp.asarray(_rel_position_index(WIN, WIN))
        bias = tab[idx].reshape(N, N, HEADS).transpose(2, 0, 1)[None]
        logits = logits + 16.0 * jax.nn.sigmoid(bias)
        mask = jnp.asarray(_shift_mask(H, W, WIN, SHIFT))
        lg = logits.reshape(B, nW, HEADS, N, N)
        lg = jnp.where(mask[None, :, None], -jnp.inf, lg)
        logits = lg.reshape(B * nW, HEADS, N, N)
        scores = jax.nn.softmax(logits, axis=-1)
        o = jnp.einsum('bhnm,bhmd->bhnd', scores, v)
        o = o.transpose(0, 2, 1, 3).reshape(B * nW, N, D)
        z = o @ Wo.T + bo
        z = z.reshape(B, nWh, nWw, WIN, WIN, D).transpose(0, 1, 3, 2, 4, 5).reshape(B, H, W, D)
        return jnp.roll(z, (SHIFT, SHIFT), axis=(1, 2))

    def _L1_conv_ref(x, Wq_lb, Wk_lb, Wv_lb, Wq_la, Wk_la, Wv_la, Wo):
        import jax, jax.numpy as jnp
        import numpy as np
        EMBED_DIM = 256
        NUM_HEADS = 16
        LB_HEADS = 8
        LA_HEADS = 8
        HEAD_DIM = EMBED_DIM // NUM_HEADS

        def _masked_attention(xf, Wq, Wk, Wv, lookahead):
            q = jnp.einsum('bnd,hed->bhne', xf, Wq)
            k = jnp.einsum('bnd,hed->bhne', xf, Wk)
            v = jnp.einsum('bnd,hed->bhne', xf, Wv)
            scale = 1.0 / jnp.sqrt(jnp.asarray(q.shape[-1], q.dtype))
            s = jnp.einsum('bhqe,bhke->bhqk', q, k) * scale
            n = s.shape[-1]
            i = jnp.arange(n)
            mask = i[:, None] <= i[None, :] if lookahead else i[:, None] >= i[None, :]
            s = jnp.where(mask, s, jnp.finfo(s.dtype).min)
            p = jax.nn.softmax(s, axis=-1)
            return jnp.einsum('bhqk,bhke->bhqe', p, v)
        B, T, F, D = x.shape
        xf = x.reshape(B, T * F, D)
        o_lb = _masked_attention(xf, Wq_lb, Wk_lb, Wv_lb, lookahead=False)
        o_la = _masked_attention(xf, Wq_la, Wk_la, Wv_la, lookahead=True)
        o = jnp.concatenate([o_lb, o_la], axis=1)
        o = o.reshape(B, T * F, D)
        out = jnp.einsum('bnd,od->bno', o, Wo)
        return out.reshape(B, T, F, D)

    def _gn(v, G=32, eps=1e-05):
        B_, H_, W_, C_ = v.shape
        g = v.reshape(B_, H_, W_, G, C_ // G)
        m = jnp.mean(g, axis=(1, 2, 4), keepdims=True)
        s = jnp.var(g, axis=(1, 2, 4), keepdims=True)
        return ((g - m) / jnp.sqrt(s + eps)).reshape(v.shape)

    def _ln_c(v, eps=1e-06):
        m = jnp.mean(v, axis=-1, keepdims=True)
        s = jnp.var(v, axis=-1, keepdims=True)
        return (v - m) / jnp.sqrt(s + eps)

    def _ln_t(v, eps=1e-05):
        m = jnp.mean(v, axis=-1, keepdims=True)
        s = jnp.var(v, axis=-1, keepdims=True)
        return (v - m) / jnp.sqrt(s + eps)

    def _to_tokens(v):
        B_, H_, W_, C_ = v.shape
        return v.reshape(B_, H_ * W_, C_)

    def _from_tokens(t, like):
        return t.reshape(like.shape)
    x = x + _L0_conv_ref(_gn(x), L0_conv_Wq, L0_conv_Wk, L0_conv_Wv, L0_conv_bv, L0_conv_Wo, L0_conv_bo, L0_conv_logit_scale, L0_conv_cpb_w1, L0_conv_cpb_b1, L0_conv_cpb_w2)
    x = x + _L1_conv_ref(_gn(x), L1_conv_Wq_lb, L1_conv_Wk_lb, L1_conv_Wv_lb, L1_conv_Wq_la, L1_conv_Wk_la, L1_conv_Wv_la, L1_conv_Wo)
    return x

_drawn_inputs = setup_inputs


def setup_inputs(seed=0):
    import zlib

    import numpy as np

    out = dict(_drawn_inputs(seed))
    spreads = {'L0_conv_logit_scale': (2.3025851249694824, 0.2)}
    factors = {'L0_conv_bv': 5.748, 'L0_conv_cpb_b1': 8.0}
    for name, (base, spread) in spreads.items():
        noise = np.random.default_rng([zlib.crc32(name.encode()), seed]).standard_normal(out[name].shape)
        drawn = base * np.exp(spread * noise) if base else spread * noise
        out[name] = jnp.asarray(drawn.astype(out[name].dtype))
    for name, factor in factors.items():
        out[name] = (out[name] * factor).astype(out[name].dtype)
    return out
```

```python
import math
from contextlib import ExitStack

import numpy as np

import concourse.bass as bass
from concourse import mybir

F32 = mybir.dt.float32
BF16 = mybir.dt.bfloat16
I32 = mybir.dt.int32
ALU = mybir.AluOpType
ACT = mybir.ActivationFunctionType
AX_X = mybir.AxisListType.X

P = 128
SIDE = 16
TOKENS = SIDE * SIDE
WIN = 8
WTOK = WIN * WIN
SHIFT = 4
CH = 256
CT = CH // P
HEADS = 16
DIM = CH // HEADS
TILE_HEADS = P // DIM
GROUP = CH // 32
TT = TOKENS // P
COL = 32
QUADS = P // COL
HIDDEN = 128
LOG100 = math.log(100.0)
EPS = 1e-5
NORM_MIN = 1e-12
MASKED = -1e30
RSQRT_SEED = 1597463007.0


class Image:

    def __init__(self, pair, offset):
        self.pair, self.offset = pair, offset
        self.k = offset % 2

    def plus(self, n):
        return Image(self.pair, self.offset + n)

    def among(self, images):
        return not isinstance(self.pair, int) or self.pair * 2 + self.offset < images

    def index(self, n=0):
        return self.pair * 2 + (self.offset + n)

    def count(self, per, n=None):
        return self.pair * (2 * per) + (self.offset * per + (per if n is None else n))

    def dmas(self, n):
        return self.pair * (16 * n) + 16 * n * (self.offset // 2 + 1)


def wait(eng, sem, value):
    if not (isinstance(value, int) and value <= 0):
        eng.wait_ge(sem, value)


def wait_alone(eng, sem, value):
    if not (isinstance(value, int) and value <= 0):
        eng.wait_ge(sem, value)
        if not isinstance(value, int):
            eng.nop(nofuse=True)


def pipeline(eng, images, stages, lags):
    low, high = lags
    first_pair = (2 - low + 1) // 2
    last_pair = (images - 1 - high - 1) // 2
    pairs = range(first_pair, last_pair + 1)

    def step(s):
        for stage, lag, *past in stages:
            if 0 <= s + lag < images + len(past):
                stage(Image(0, s + lag))

    if len(pairs) < 2:
        for s in range(-high, images - low):
            step(s)
        return
    for s in range(-high, 2 * pairs[0]):
        step(s)
    with eng.Fori(pairs[0], pairs[-1] + 1) as pair:
        for k in range(2):
            for stage, lag, *_ in stages:
                stage(Image(pair, k + lag))
    for s in range(2 * pairs[-1] + 2, images - low):
        step(s)


def window_rows():
    t, ww, rr, c = np.meshgrid(np.arange(2), np.arange(2), np.arange(WIN), np.arange(WIN), indexing="ij")
    right, left = (ww == 1) & (c >= WIN - SHIFT), (ww == 1) & (c < WIN - SHIFT)
    low, high = (t == 1) & (rr >= WIN - SHIFT), (t == 1) & (rr < WIN - SHIFT)
    queries = np.stack([right, left, low, high]).reshape(4, TOKENS).astype(np.float32) * MASKED
    keys = np.stack([left, right, high, low]).reshape(4, TOKENS).astype(np.float32)
    return queries, keys


def relative_points():
    rows, cols = np.meshgrid(np.arange(WIN), np.arange(WIN), indexing="ij")
    at = np.stack([rows.ravel(), cols.ravel()]).astype(np.float32)
    rel = (at[:, :, None] - at[:, None, :]) / np.float32(WIN - 1) * np.float32(8.0)
    rel = np.sign(rel) * np.log2(np.abs(rel) + np.float32(1.0)) / np.float32(3.0)
    return rel.astype(np.float32).reshape(2, WTOK * WTOK)


def build_network(nc, xr, out, given):
    images = xr.shape[1]
    scratch = nc.dram_tensor("scratch_heads", [2, HEADS, TOKENS, DIM], F32).ap()

    with ExitStack() as shared:
        def sb(name, shape, dt=F32, ctx=shared):
            return ctx.enter_context(nc.sbuf_tensor(name, shape, dt))

        X = sb("X", [P, images + 1, CT, TOKENS])
        stats2 = sb("stats2", [P, images, CT, 6])
        probs = [sb(f"probs{k}", [P, 6144]) for k in range(2)]
        qx = [sb(f"qx{k}", [P, HEADS, TOKENS]) for k in range(2)]
        kx = sb("kx", [P, HEADS, TOKENS], BF16)
        xh = [sb(f"xh{k}", [P, CT, TOKENS]) for k in range(2)]
        qk = [sb(f"qk{k}", [P, 4, TOKENS]) for k in range(2)]
        qkb = sb("qkb", [P, 4, TOKENS], BF16)
        ident = sb("ident", [P, P])
        gavg = sb("gavg", [P, P])
        A = [shared.enter_context(nc.psum_tensor(f"psA{n}", [P, 512], F32)) for n in range(3)]
        C = [shared.enter_context(nc.psum_tensor(f"psC{n}", [P, 1024], F32)) for n in range(2)]
        E = shared.enter_context(nc.psum_tensor("psE", [P, 512], F32))
        B = [C[1][:, 0:512], C[1][:, 512:1024]]

        with ExitStack() as ctx:
            layer0(nc, ctx, images, xr, given, X, stats2, probs, qx, kx, xh, qk, qkb, ident, gavg, A, B, C, E)
        with ExitStack() as ctx:
            layer1(nc, ctx, images, out, given, scratch, X, stats2, probs, qx, kx, xh, qk, qkb, ident, gavg, A, C, E)


def layer0(nc, ctx, images, xr, given, X, stats2, probs, qx, kx, xh, qk, qkb, ident, gavg, A, B, C, E):
    def sb(name, shape, dt=F32):
        return ctx.enter_context(nc.sbuf_tensor(name, shape, dt))

    def sem(name):
        return ctx.enter_context(nc.semaphore(name))

    prob = [p[:, 0:TT * HEADS * WTOK].rearrange("p (t h q) -> p t h q", t=TT, h=HEADS) for p in probs]
    sq = probs[0][:, 2048:3072].rearrange("p (t c) -> p t c", t=TT)
    qkn = probs[0][:, 3072:4096].rearrange("p (t c) -> p t c", t=TT)
    aux_q = [probs[0][COL * k:COL * k + 5, 4096:6144].bitcast(BF16).rearrange("p (h t) -> p h t", h=HEADS)
             for k in range(2)]
    zb = probs[1][:, 2048:2560].rearrange("p (c t) -> p c t", c=CT)
    rd = probs[1][:, 2560:3072]
    wop = probs[1][:, 3072:5120].rearrange("p (ww g o) -> p ww g o", ww=2, g=QUADS)
    wqk = probs[1][:, 5120:6144].rearrange("p (c o) -> p c o", c=CT)
    hidden = probs[0][:, 0:WTOK * WTOK]
    e_bias = [probs[1][:, n * 1024:(n + 1) * 1024] for n in range(3)]
    wo = xh[0]
    wv = sb("wv0", [P, CT, CH])
    bv = sb("bv0", [P, CT])
    bo = sb("bo0", [P, CT])
    bz = sb("bz0", [P, CT])
    scale = sb("scale0", [P, HEADS])
    ones_win = sb("ones_win", [P, COL])
    pt = qx[1][0:2, :, :].rearrange("p h t -> p (h t)")
    w1 = sb("cpb_w1", [2, HIDDEN])
    b1 = sb("cpb_b1", [HIDDEN, 1])
    w2 = sb("cpb_w2", [HIDDEN, HEADS])
    ebias = sb("ebias", [P, HEADS, WTOK])
    aux_rows = sb("aux_k", [COL + 5, TOKENS], BF16)
    aux_k = [aux_rows[COL * k:COL * k + 5, :] for k in range(2)]
    rs = sb("rs", [P, 66])
    rs_half = sb("rs_half", [P, 66])
    rs_bits = sb("rs_bits", [P, 66], I32)
    rs_y = sb("rs_y", [P, 66])
    rs_t = sb("rs_t", [P, 66])
    shift = sb("shift", [P, CT])
    minus_mean = sb("minus_mean", [P, CT])
    three_halves = sb("three_halves", [P, 1])
    bn = sb("bn", [P, CT, 6])
    mm = sb("mm", [P, 2 * CT])
    gs = sb("gs", [P, CT, 2])
    gm = sb("gm", [P, CT])
    cm = sb("cm", [P, TT, HEADS])
    ct = [sb(f"ct{k}", [HEADS, TOKENS], BF16) for k in range(2)]
    vw = [sb(f"vw{k}", [P, TT, HEADS, 2, DIM]) for k in range(2)]
    ot = sb("ot", [P, TT, QUADS, WTOK])

    c_in, p_hid, a_hid, p_tab, a_tab, d_tab, a_tab2, tab_in, z_in, p_bz, d_bz = (
        sem(n) for n in ("c_in", "p_hid", "a_hid", "p_tab", "a_tab", "d_tab", "a_tab2", "tab_in", "z_in",
                         "p_bz", "d_bz"))
    loads = [(ident, given["ident"]), (gavg, given["gavg"]), (ones_win, given["ones_win"]), (pt, given["points"]),
             (w1, given["cpb_w1"]), (b1, given["cpb_b1"]), (w2, given["cpb_w2"]), (wqk, given["wqk0"]), (wv, given["wv0"]),
             (wo, given["wo0"]), (wop, given["wop0"]), (bv, given["bv0"]), (bo, given["bo0"]), (aux_k[0], given["aux_k"]), (aux_k[1], given["aux_k"]),
             (aux_q[0], given["aux_q"]), (aux_q[1], given["aux_q"]), (scale, given["scale0"])]

    with nc.Block() as block:
        @block.sync
        def _(sp):
            for dst, src in loads:
                sp.dma_start(dst if isinstance(dst, bass.AP) else dst[:], src).then_inc(c_in, 16)
            sp.wait_ge(a_tab2, 1)
            sp.dma_start(ebias[WTOK:P, :, :], ebias[0:WTOK, :, :]).then_inc(tab_in, 16)
            sp.wait_ge(tab_in, 16)

        @block.gpsimd
        def _(pool):
            for k in range(2):
                if k:
                    pool.wait_ge(p_hid, 8)
                nc.gpsimd.memset(qx[k][:], 0.0)
                nc.gpsimd.memset(vw[k][:], 0.0)
            nc.gpsimd.memset(kx[:].bitcast(F32), 0.0)
            nc.gpsimd.memset(three_halves[:], 1.5)
            nc.gpsimd.memset(rs[:], 1.0).then_inc(z_in, 1)
            pool.wait_ge(z_in, 1)

        @block.tensor
        def _(pe):
            pe.wait_ge(c_in, 16 * len(loads))
            for n in range(8):
                if n >= 3:
                    pe.wait_ge(a_hid, n - 2)
                nc.tensor.matmul(A[n % 3][:], w1[:], pt[:, 512 * n:512 * n + 512],
                                 start=True, stop=True).then_inc(p_hid, 1)
            pe.wait_ge(a_hid, 8)
            for q in range(WTOK):
                last = nc.tensor.matmul(C[0][0:WTOK, q * HEADS:(q + 1) * HEADS],
                                        hidden[:, q * WTOK:(q + 1) * WTOK], w2[:], start=True, stop=True)
            last.then_inc(p_tab, 1)
            for o in range(CT):
                for c in range(CT):
                    last = nc.tensor.matmul(E[:, o:o + 1], wo[:, c, o * P:(o + 1) * P], bv[:, c:c + 1],
                                            start=(c == 0), stop=(c == CT - 1))
            last.then_inc(p_bz, 1)

        @block.scalar
        def _(act):
            for n in range(8):
                act.wait_ge(p_hid, n + 1)
                nc.scalar.activation(hidden[:, 512 * n:512 * n + 512], A[n % 3][:], ACT.Relu,
                                     bias=b1[:, 0:1]).then_inc(a_hid, 1)
            act.wait_ge(p_tab, 1)
            nc.scalar.activation(e_bias[0][0:WTOK, :], C[0][0:WTOK, :], ACT.Exp, scale=-1.0).then_inc(a_tab, 1)
            act.wait_ge(d_tab, 2)
            nc.scalar.activation(ebias[0:WTOK, :, :].rearrange("p h q -> p q h"),
                                 e_bias[2][0:WTOK, :].rearrange("p (q h) -> p q h", h=HEADS),
                                 ACT.Exp, scale=16.0).then_inc(a_tab2, 1)
            act.wait_ge(d_bz, 2)
            nc.scalar.activation(scale[:], scale[:], ACT.Exp).then_inc(a_tab2, 1)

        @block.vector
        def _(dve):
            dve.wait_ge(a_tab, 1)
            nc.vector.tensor_scalar(e_bias[1][0:WTOK, :], e_bias[0][0:WTOK, :], 1.0, None,
                                    ALU.add).then_inc(d_tab, 1)
            dve.wait_ge(d_tab, 1)
            nc.vector.reciprocal(e_bias[2][0:WTOK, :], e_bias[1][0:WTOK, :]).then_inc(d_tab, 1)
            dve.wait_ge(p_bz, 1)
            nc.vector.tensor_tensor(bz[:], E[:, 0:CT], bo[:], ALU.add).then_inc(d_bz, 1)
            nc.vector.tensor_scalar(scale[:], scale[:], LOG100, None, ALU.min).then_inc(d_bz, 1)

    x_in = [sem(f"x_in{k}") for k in range(2)]
    kx_in = [sem(f"kx_in{k}") for k in range(2)]
    qx_in = [sem(f"qx_in{k}") for k in range(2)]
    c_row = [sem(f"c_row{k}") for k in range(2)]
    pv_done, proj_qk, proj_v, max_ready, s_ready, z_ready, turned, c_turned, g_ready = (
        sem(n) for n in ("pv_done", "proj_qk", "proj_v", "max_ready", "s_ready", "z_ready", "turned",
                         "c_turned", "g_ready"))
    squared, exp_done, z_out, qk_out, c_out, xh_done, v_out = (
        sem(n) for n in ("squared", "exp_done", "z_out", "qk_out", "c_out", "xh_done", "v_out"))
    r_done, o_done, sum_done, gn_chain, rs_ready, max_done, qkn_done, x1_done, cast_done, stats = (
        sem(n) for n in ("r_done", "o_done", "sum_done", "gn_chain", "rs_ready", "max_done", "qkn_done",
                         "x1_done", "cast_done", "stats"))
    newton, biased = sem("newton"), sem("biased")
    LAGS = (-1, 6)
    NEWTON = 14

    def win(t, ww):
        return slice(t * P + ww * WTOK, t * P + (ww + 1) * WTOK)

    with nc.Block() as block:
        @block.sync
        def _(sp):
            def load(i):
                wait_alone(sp, stats, i.plus(-2).count(4, 1))
                src = xr.rearrange("(c p) i t -> p c i t", p=P)[:, :, bass.ds(i.index(), 1), :]
                sp.dma_start(X[:, bass.ds(i.index(1), 1), :, :].rearrange("p i c t -> p c (i t)"),
                             src.rearrange("p c i t -> p c (i t)")).then_inc(x_in[i.k], 16)

            def spread_k(i):
                wait_alone(sp, cast_done, i.count(1))
                wait_alone(sp, max_ready, i.plus(-1).count(4))
                for h in range(TILE_HEADS):
                    rows = slice(h * DIM, (h + 1) * DIM)
                    sp.dma_start(kx[rows, h::TILE_HEADS, :], qkb[rows, 2:4, :]).then_inc(kx_in[i.k], 16)

            def spread_q(i):
                wait_alone(sp, qk_out, i.count(2))
                wait_alone(sp, s_ready, i.plus(-2).count(2))
                for h in range(TILE_HEADS):
                    rows = slice(h * DIM, (h + 1) * DIM)
                    sp.dma_start(qx[i.k][rows, h::TILE_HEADS, :], qk[i.k][rows, 0:2, :]).then_inc(qx_in[i.k], 16)

            def row_c(i):
                wait_alone(sp, c_out, i.count(1))
                wait_alone(sp, s_ready, i.plus(-2).count(2))
                sp.dma_start(aux_q[i.k][4:5, :, :], ct[i.k][:, :]).then_inc(c_row[i.k], 16)

            pipeline(sp, images, [(row_c, 1), (spread_k, 2), (spread_q, 2), (load, 6)], LAGS)

        @block.tensor
        def _(pe):
            def weigh(i):
                wait(pe, biased, i.count(2))
                wait(pe, v_out, i.count(2))
                if i.plus(1).among(images):
                    wait(pe, max_done, i.plus(1).count(4))
                for stationary, bank in ((None, B[0]), (ones_win, B[1])):
                    for t in range(TT):
                        for g in range(QUADS):
                            for c in range(QUADS):
                                h = g * QUADS + c
                                v = ones_win[:, :] if stationary is not None else vw[i.k][:, t, h, :, :]
                                at = (t * QUADS + g) * WTOK
                                last = nc.tensor.matmul(bank[COL * c:COL * c + COL, at:at + WTOK], v,
                                                        prob[i.k][:, t, h, :], start=True, stop=True,
                                                        tile_position=(0, COL * c))
                last.then_inc(pv_done, 1)

            def project(i):
                wait(pe, xh_done, i.count(4))
                wait(pe, qk_out, i.plus(-1).count(2))
                for t in range(TT):
                    for c in range(CT):
                        last = nc.tensor.matmul(A[t][:], xh[i.k][:, c, t * P:(t + 1) * P], wqk[:, c, :],
                                                start=(c == 0), stop=(c == CT - 1))
                    last.then_inc(proj_qk, 1)

            def project_v(i):
                wait(pe, c_out, i.plus(-1).count(1))
                for t in range(TT):
                    for c in range(CT):
                        last = nc.tensor.matmul(A[2][:, t * CH:(t + 1) * CH], xh[i.k][:, c, t * P:(t + 1) * P],
                                                wv[:, c, :], start=(c == 0), stop=(c == CT - 1))
                last.then_inc(proj_v, 1)

            def maxima(i):
                wait(pe, kx_in[i.k], i.dmas(TILE_HEADS))
                for t in range(TT):
                    for g in range(CT):
                        n = t * CT + g
                        if n < 2:
                            wait(pe, o_done, i.plus(-2).count(1))
                        else:
                            wait(pe, max_done, i.count(4, n - 1))
                        for masks in range(2):
                            for ww in range(2):
                                keys = aux_k[i.k][0:4, win(t, ww)].unsqueeze(1).to_broadcast([4, TILE_HEADS, WTOK])
                                lhs = aux_q[i.k][0:4, 0, win(t, ww)] if masks else qkb[:, g, win(t, ww)]
                                rhs = keys if masks else kx[:, g * TILE_HEADS:(g + 1) * TILE_HEADS, win(t, ww)]
                                last = nc.tensor.matmul(B[n % 2][WTOK * ww:WTOK * (ww + 1), :], lhs, rhs,
                                                        start=not masks, stop=bool(masks), skip_group_check=True)
                        last.then_inc(max_ready, 1)

            def scores(i, t):
                wait(pe, qx_in[i.k], i.dmas(TILE_HEADS))
                wait(pe, c_row[i.k], i.dmas(1))
                wait(pe, exp_done, i.count(2, t - 1 + 1) if t else i.plus(-1).count(2))
                for g in range(CT):
                    heads = slice(g * TILE_HEADS, (g + 1) * TILE_HEADS)
                    for aux in range(2):
                        for ww in range(2):
                            lhs = aux_k[i.k][0:5, win(t, ww)] if aux else qk[i.k][:, 2 + g, win(t, ww)]
                            rhs = aux_q[i.k][0:5, heads, win(t, ww)] if aux else qx[i.k][:, heads, win(t, ww)]
                            last = nc.tensor.matmul(C[0][WTOK * ww:WTOK * (ww + 1), g * 512:(g + 1) * 512],
                                                    lhs, rhs, start=not aux, stop=bool(aux), skip_group_check=True)
                last.then_inc(s_ready, 1)

            def output(i):
                wait(pe, o_done, i.count(1))
                if i.plus(4).among(images):
                    wait(pe, gn_chain, i.plus(4).count(4, 1))
                wait(pe, z_out, i.plus(-1).count(2))
                for o in range(CT):
                    for ww in range(2):
                        dst = E[:, o * TOKENS:(o + 1) * TOKENS].rearrange("p (t rr ww c) -> p ww t rr c", t=TT, rr=WIN, ww=2)
                        for g in range(QUADS):
                            last = nc.tensor.matmul(dst[:, ww], wop[:, ww, g, o * P:(o + 1) * P],
                                                    ot[:, :, g, :].rearrange("p t (rr c) -> p t rr c", rr=WIN),
                                                    start=(g == 0), stop=(g == QUADS - 1))
                last.then_inc(z_ready, 1)

            def turn(i):
                for t in range(TT):
                    wait(pe, qkn_done, i.count(2, t + 1))
                    for n in range(4):
                        last = nc.tensor.transpose(A[t][:, n * P:(n + 1) * P], qkn[:, t, n * P:(n + 1) * P],
                                                   ident[:, :])
                    last.then_inc(turned, 1)

            def turn_c(i):
                wait(pe, max_done, i.count(4))
                wait(pe, v_out, i.count(2))
                for t in range(TT):
                    last = nc.tensor.transpose(A[2][0:HEADS, t * P:(t + 1) * P], cm[:, t, :], ident[:, :])
                last.then_inc(c_turned, 1)

            def groups(i):
                wait(pe, stats, i.count(4))
                wait(pe, z_out, i.plus(-5).count(2))
                nc.tensor.matmul(E[:, 0:4 * CT], gavg[:, :], bn[:, :, :].rearrange("p c (h s) -> p (c h) s", s=3)[:, :, 1:3],
                                 start=True, stop=True).then_inc(g_ready, 1)

            pipeline(pe, images, [(weigh, -1), (project, 2), (project_v, 1), (maxima, 1), (lambda i: scores(i, 0), 0),
                                  (output, -1), (lambda i: scores(i, 1), 0), (turn, 2), (turn_c, 1),
                                  (groups, 4)], LAGS)

        @block.scalar
        def _(act):
            def square(i):
                wait(act, sum_done, i.plus(-1).count(2))
                for t in range(TT):
                    wait(act, proj_qk, i.count(2, t + 1))
                    nc.scalar.activation(sq[:, t, :], A[t][:], ACT.Square).then_inc(squared, 1)

            def copy_v(i):
                wait(act, proj_v, i.count(1))
                wait(act, pv_done, i.plus(-2).count(1))
                for ww in range(2):
                    rows = slice(ww * WTOK, (ww + 1) * WTOK)
                    nc.scalar.activation(vw[i.k][rows, :, :, ww, :],
                                         A[2][rows, :].rearrange("p (t h e) -> p t h e", t=TT, h=HEADS),
                                         ACT.Copy).then_inc(v_out, 1)

            def exponent(i, t):
                wait(act, s_ready, i.count(2, t + 1))
                wait(act, pv_done, i.plus(-2).count(1))
                nc.scalar.activation(prob[i.k][:, t, :, :].rearrange("p h q -> p (h q)"), C[0][:, :],
                                     ACT.Exp).then_inc(exp_done, 1)

            def copy_z(i):
                wait(act, z_ready, i.count(1))
                wait(act, x1_done, i.plus(-1).count(4))
                for o in range(CT):
                    nc.scalar.activation(zb[:, o, :], E[:, o * TOKENS:(o + 1) * TOKENS], ACT.Identity,
                                         bias=bz[:, o:o + 1]).then_inc(z_out, 1)

            def copy_qk(i):
                wait(act, qx_in[i.k], i.plus(-2).dmas(TILE_HEADS))
                wait(act, s_ready, i.plus(-2).count(2))
                wait(act, cast_done, i.plus(-2).count(1))
                for t in range(TT):
                    wait(act, turned, i.count(2, t + 1))
                    nc.scalar.activation(qk[i.k][:, :, t * P:(t + 1) * P],
                                         A[t][:].rearrange("p (n t) -> p n t", n=4), ACT.Copy).then_inc(qk_out, 1)

            def copy_c(i):
                wait(act, c_turned, i.count(1))
                wait(act, c_row[i.k], i.plus(-2).dmas(1))
                nc.scalar.activation(ct[i.k][:, :], A[2][0:HEADS, 0:TOKENS], ACT.Copy, scale=-1.0).then_inc(c_out, 1)

            def normalize(i):
                wait(act, newton, i.count(NEWTON))
                wait(act, proj_v, i.plus(-2).count(1))
                for c in range(CT):
                    src = X[:, bass.ds(i.index(1), 1), c, :].rearrange("p i (t rr ww c) -> p (i t) rr ww c", t=TT, rr=WIN, ww=2)
                    dst = xh[i.k][:, c, :].rearrange("p (t ww rr c) -> p t rr ww c", t=TT, ww=2, rr=WIN)
                    for ww in range(2):
                        nc.scalar.activation(dst[:, :, :, ww, :], src[:, :, :, ww, :], ACT.Identity,
                                             bias=shift[:, c:c + 1], scale=rs_y[:, 64 + c:65 + c]).then_inc(xh_done, 1)

            pipeline(act, images, [(square, 2), (copy_v, 1), (lambda i: exponent(i, 0), 0), (normalize, 3),
                                   (copy_z, -1), (lambda i: exponent(i, 1), 0), (copy_qk, 2), (copy_c, 1)], LAGS)

        @block.vector
        def _(dve):
            def outputs(i):
                wait(dve, pv_done, i.count(1))
                wait(dve, o_done, i.plus(-1).count(1))
                nc.vector.reciprocal(rd[:, :], B[1]).then_inc(r_done, 1)
                wait(dve, r_done, i.count(1))
                wait(dve, z_ready, i.plus(-1).count(1))
                nc.vector.tensor_tensor(ot[:, :, :, :].rearrange("p t g q -> p (t g q)"), B[0], rd[:, :],
                                        ALU.mult).then_inc(o_done, 1)

            def norms(i):
                wait(dve, newton, i.plus(0).count(NEWTON))
                for t in range(TT):
                    wait(dve, squared, i.count(2, t + 1))
                    nc.vector.reduce_sum(rs[:, 32 * t:32 * t + 32], sq[:, t, :].rearrange("p (h e) -> p h e", e=DIM),
                                         AX_X).then_inc(sum_done, 1)

            def variances(i):
                wait(dve, g_ready, i.count(1))
                wait(dve, newton, i.plus(-1).count(NEWTON))
                nc.vector.reduce_sum(gs[:, :, :], E[:, 0:4 * CT].rearrange("p (c h s) -> p c s h", h=2, s=2),
                                     AX_X).then_inc(gn_chain, 1)
                wait(dve, gn_chain, i.count(4, 1))
                nc.vector.tensor_scalar(minus_mean[:, :], gs[:, :, 0], -1.0, None, ALU.mult).then_inc(gn_chain, 1)
                nc.vector.tensor_tensor(gm[:, :], gs[:, :, 0], gs[:, :, 0], ALU.mult).then_inc(gn_chain, 1)
                wait(dve, gn_chain, i.count(4, 3))
                nc.vector.scalar_tensor_tensor(out=rs[:, 64:66], in0=gs[:, :, 1], scalar=EPS, in1=gm[:, :],
                                               op0=ALU.add, op1=ALU.subtract).then_inc(gn_chain, 1)

            def seeds(i):
                wait(dve, sum_done, i.plus(-1).count(2))
                if i.among(images):
                    wait(dve, gn_chain, i.count(4))
                wait(dve, xh_done, i.plus(-1).count(4))
                wait(dve, qkn_done, i.plus(-2).count(2))
                nc.vector.tensor_scalar(rs[:, :], rs[:, :], NORM_MIN * NORM_MIN, None, ALU.max).then_inc(rs_ready, 1)
                wait(dve, rs_ready, i.count(4, 1))
                nc.vector.tensor_scalar(rs_half[:, :], rs[:, :], -0.5, None, ALU.mult).then_inc(rs_ready, 1)
                nc.vector.tensor_scalar(rs_bits[:, :], rs[:, :].bitcast(I32), 1, None,
                                        ALU.logical_shift_right).then_inc(rs_ready, 1)
                wait(dve, rs_ready, i.count(4, 3))
                nc.vector.tensor_scalar(rs_y[:, :].bitcast(I32), rs_bits[:, :], -1.0, RSQRT_SEED, ALU.mult,
                                        ALU.add).then_inc(rs_ready, 1)

            def take_max(i):
                for n in range(4):
                    t, g = divmod(n, CT)
                    wait(dve, max_ready, i.count(4, n + 1))
                    if n == 0:
                        wait(dve, c_turned, i.plus(-1).count(1))
                    nc.vector.reduce_max(cm[:, t, g * TILE_HEADS:(g + 1) * TILE_HEADS],
                                         B[n % 2].rearrange("p (h k) -> p h k", k=WTOK), AX_X).then_inc(max_done, 1)

            def unit_qk(i):
                wait(dve, newton, i.plus(1).count(NEWTON))
                wait(dve, turned, i.plus(-1).count(2))
                for t in range(TT):
                    nc.vector.tensor_tensor(qkn[:, t, :].rearrange("p (h e) -> p h e", e=DIM),
                                            A[t][:].rearrange("p (h e) -> p h e", e=DIM),
                                            rs_y[:, 32 * t:32 * t + 32].unsqueeze(2).to_broadcast([P, 32, DIM]),
                                            ALU.mult).then_inc(qkn_done, 1)

            def residual(i):
                wait(dve, z_out, i.count(2))
                for r0, rn, rd_ in ((0, 12, 4), (12, 4, 0)):
                    for c0, cn, cd in ((0, 12, 4), (12, 4, 0)):
                        def part(ap, row, c):
                            return ap.rearrange("p c (i j) -> p c i j", j=SIDE)[:, :, row:row + rn, c:c + cn]
                        old = X[:, bass.ds(i.index(1), 1), :, :].rearrange("p i c t -> p (i c) t")
                        new = X[:, bass.ds(i.index(), 1), :, :].rearrange("p i c t -> p (i c) t")
                        nc.vector.tensor_tensor(part(new, rd_, cd), part(old, r0, c0), part(zb[:, :, :], r0, c0),
                                                ALU.add).then_inc(x1_done, 1)

            def stats_next(i):
                wait_alone(dve, x1_done, i.count(4))
                for c in range(CT):
                    nc.vector.bn_stats(stats2[:, bass.ds(i.index(), 1), c, :].rearrange("p i s -> p (i s)"),
                                       X[:, bass.ds(i.index(), 1), c, :].rearrange("p i t -> p (i t)"))

            def cast(i):
                wait(dve, qk_out, i.count(2))
                wait(dve, kx_in[1 - i.k], i.plus(-1).dmas(TILE_HEADS))
                wait(dve, max_ready, i.plus(-1).count(4))
                nc.vector.tensor_copy(qkb[:, :, :].rearrange("p n t -> p (n t)"),
                                      qk[i.k][:, :, :].rearrange("p n t -> p (n t)")).then_inc(cast_done, 1)

            def stats_first(i):
                wait_alone(dve, x_in[i.k], i.dmas(1))
                wait_alone(dve, g_ready, i.plus(-1).count(1))
                for c in range(CT):
                    nc.vector.bn_stats(bn[:, c, :], X[:, bass.ds(i.index(1), 1), c, :]
                                       .rearrange("p i t -> p (i t)")).then_inc(stats, 1)
                half = bn[:, :, :].rearrange("p c (h s) -> p (c h) s", s=3)
                wait(dve, stats, i.count(4, 2))
                nc.vector.tensor_tensor(mm[:, :], half[:, :, 1], half[:, :, 1], ALU.mult).then_inc(stats, 1)
                wait(dve, stats, i.count(4, 3))
                nc.vector.scalar_tensor_tensor(out=half[:, :, 2], in0=half[:, :, 2], scalar=2.0 / TOKENS, in1=mm[:, :],
                                               op0=ALU.mult, op1=ALU.add).then_inc(stats, 1)

            pipeline(dve, images, [(outputs, -1), (norms, 2), (variances, 3), (seeds, 3, 1), (take_max, 1),
                                   (unit_qk, 2), (residual, -1), (stats_next, -1), (cast, 2),
                                   (stats_first, 4)], LAGS)

        @block.gpsimd
        def _(pool):
            def roots(i):
                n = 0
                wait(pool, rs_ready, i.count(4))
                for step in range(3):
                    nc.gpsimd.tensor_tensor(rs_t[:, :], rs_y[:, :], rs_y[:, :], ALU.mult).then_inc(newton, 1)
                    wait(pool, newton, i.count(NEWTON, n + 1))
                    nc.gpsimd.tensor_tensor(rs_t[:, :], rs_t[:, :], rs_half[:, :], ALU.mult).then_inc(newton, 1)
                    wait(pool, newton, i.count(NEWTON, n + 2))
                    nc.gpsimd.tensor_tensor(rs_t[:, :], rs_t[:, :], three_halves[:, :].to_broadcast([P, 66]),
                                            ALU.add).then_inc(newton, 1)
                    wait(pool, newton, i.count(NEWTON, n + 3))
                    nc.gpsimd.tensor_tensor(rs_y[:, :], rs_y[:, :], rs_t[:, :], ALU.mult).then_inc(newton, 1)
                    n += 4
                    wait(pool, newton, i.count(NEWTON, n))
                q_part = rs_y[:, 0:64].rearrange("p (t n h) -> p t n h", t=TT, n=2)[:, :, 0, :]
                nc.gpsimd.tensor_tensor(q_part, q_part, scale[:, :].unsqueeze(1).to_broadcast([P, TT, HEADS]),
                                        ALU.mult).then_inc(newton, 1)
                nc.gpsimd.tensor_tensor(shift[:, :], minus_mean[:, :], rs_y[:, 64:66], ALU.mult).then_inc(newton, 1)

            def add_bias(i, t):
                wait(pool, exp_done, i.count(2, t + 1))
                both = prob[i.k][:, t, :, :]
                nc.gpsimd.tensor_tensor(both, both, ebias[:, :, :], ALU.mult).then_inc(biased, 1)

            pipeline(pool, images, [(roots, 3, 1), (lambda i: add_bias(i, 0), 0), (lambda i: add_bias(i, 1), 0)], LAGS)


class Part:

    def __init__(self, block, head, heads, start, size):
        self.block, self.head, self.heads, self.start, self.size = block, head, heads, start, size
        self.cols = slice(start, start + size)
        self.which = slice(head, head + heads)
        self.tile = head // TILE_HEADS
        self.ahead = self.tile == 1
        self.diagonal = block * P - start


SCORES = ([Part(0, h, 2, 0, TOKENS) for h in range(0, 8, 2)] + [Part(1, h, 4, P, P) for h in range(0, 8, 4)]
          + [Part(0, h, 4, 0, P) for h in range(8, 16, 4)] + [Part(1, h, 2, 0, TOKENS) for h in range(8, 16, 2)])
MAXIMA = ([Part(0, h, 4, 0, P) for h in range(0, 8, 4)] + [Part(1, h, 2, 0, TOKENS) for h in range(0, 8, 2)]
          + [Part(0, h, 2, 0, TOKENS) for h in range(8, 16, 2)] + [Part(1, h, 4, P, P) for h in range(8, 16, 4)])
ROUNDS = len(SCORES) // 2


def layer1(nc, ctx, images, out, given, scratch, X, stats2, probs, qx, kx, xh, qk, qkb, ident, gavg, A, C, E):
    def sb(name, shape, dt=F32):
        return ctx.enter_context(nc.sbuf_tensor(name, shape, dt))

    def sem(name):
        return ctx.enter_context(nc.semaphore(name))

    wqk = sb("wqk1", [P, CT, 2 * CH])
    wv = sb("wv1", [P, CT, CH])
    wo = sb("wo1", [P, CT, CH])
    identb = sb("identb", [P, P], BF16)
    below = sb("below", [P, P], BF16)
    above = sb("above", [P, P], BF16)
    ones = sb("ones", [COL + 1, P], BF16)
    row_maxima = sb("row_max", [COL + 1, HEADS, TOKENS], BF16)
    row_max = [row_maxima[COL * k:COL * k + 1, :, :] for k in range(2)]
    cm = sb("cm1", [P, TT, HEADS])
    ct = [sb(f"ct1{k}", [HEADS, TOKENS], BF16) for k in range(2)]
    va = [sb(f"va{k}", [P, TT, HEADS, COL]) for k in range(2)]
    ots = sb("ots", [P, QUADS, TOKENS])
    rdn = sb("rdn", [P, TT * HEADS])
    on = sb("on", [P, TT, CH])
    rows = sb("rows", [P, TT, CH])
    of = sb("of", [P, CT, TOKENS])
    n_stat = images * CT
    gs = probs[0][:, 0:2 * n_stat].rearrange("p (n s) -> p n s", s=2)
    gm, rs, rs_half, rs_t = (probs[0][:, (2 + n) * n_stat:(3 + n) * n_stat] for n in range(4))
    rs_bits = probs[0][:, 6 * n_stat:7 * n_stat].bitcast(I32)
    mm = probs[0][:, 7 * n_stat:9 * n_stat]
    rs_y = sb("rs1_y", [P, images, CT])
    shift = sb("shift1", [P, images, CT])
    flat_y = rs_y[:, :, :].rearrange("p i c -> p (i c)")

    c_in, z_in, sum_in, g_ready, var, newton = (sem(n) for n in ("c_in1", "z_in1", "sum_in", "g_ready1", "var1", "newton1"))
    loads = [(wqk, given["wqk1"]), (wv, given["wv1"]), (wo, given["wo1"]), (identb, given["identb"]), (below, given["below"]),
             (above, given["above"])]
    with nc.Block() as block:
        @block.sync
        def _(sp):
            for dst, src in loads:
                sp.dma_start(dst[:], src).then_inc(c_in, 16)
            sp.wait_ge(c_in, 16 * len(loads))

        @block.vector
        def _(dve):
            half = stats2[:, :, :, :].rearrange("p i c (h s) -> p (i c h) s", s=3)
            nc.vector.tensor_tensor(mm, half[:, :, 1], half[:, :, 1], ALU.mult).then_inc(var, 1)
            dve.wait_ge(var, 1)
            nc.vector.scalar_tensor_tensor(out=half[:, :, 2], in0=half[:, :, 2], scalar=2.0 / TOKENS, in1=mm,
                                           op0=ALU.mult, op1=ALU.add).then_inc(sum_in, 1)
            dve.wait_ge(g_ready, 1)
            nc.vector.reduce_sum(gs[:, :, :], E[:, 0:4 * n_stat].rearrange("p (n h s) -> p n s h", h=2, s=2),
                                 AX_X).then_inc(var, 1)
            dve.wait_ge(var, 2)
            nc.vector.tensor_tensor(gm[:, :], gs[:, :, 0], gs[:, :, 0], ALU.mult).then_inc(var, 1)
            dve.wait_ge(var, 3)
            nc.vector.scalar_tensor_tensor(out=rs[:, :], in0=gs[:, :, 1], scalar=EPS, in1=gm[:, :],
                                           op0=ALU.add, op1=ALU.subtract).then_inc(var, 1)
            dve.wait_ge(var, 4)
            nc.vector.tensor_scalar(rs_half[:, :], rs[:, :], -0.5, None, ALU.mult).then_inc(var, 1)
            nc.vector.tensor_scalar(rs_bits[:, :], rs[:, :].bitcast(I32), 1, None,
                                    ALU.logical_shift_right).then_inc(var, 1)
            dve.wait_ge(var, 6)
            nc.vector.tensor_scalar(flat_y.bitcast(I32), rs_bits[:, :], -1.0, RSQRT_SEED, ALU.mult,
                                    ALU.add).then_inc(var, 1)
            dve.wait_ge(var, 7)
            for step in range(3):
                nc.vector.tensor_tensor(rs_t[:, :], flat_y, flat_y, ALU.mult).then_inc(newton, 1)
                dve.wait_ge(newton, 3 * step + 1)
                nc.vector.tensor_tensor(rs_t[:, :], rs_t[:, :], rs_half[:, :], ALU.mult).then_inc(newton, 1)
                dve.wait_ge(newton, 3 * step + 2)
                nc.vector.scalar_tensor_tensor(out=flat_y, in0=rs_t[:, :], scalar=1.5, in1=flat_y,
                                               op0=ALU.add, op1=ALU.mult).then_inc(newton, 1)
                dve.wait_ge(newton, 3 * step + 3)
            nc.vector.scalar_tensor_tensor(out=shift[:, :, :].rearrange("p i c -> p (i c)"), in0=gs[:, :, 0],
                                           scalar=-1.0, in1=flat_y, op0=ALU.mult, op1=ALU.mult).then_inc(newton, 1)
            dve.wait_ge(newton, 10)

        @block.tensor
        def _(pe):
            pe.wait_ge(sum_in, 1)
            nc.tensor.matmul(E[:, 0:4 * n_stat], gavg[:, :],
                             stats2[:, :, :, :].rearrange("p i c (h s) -> p (i c h) s", s=3)[:, :, 1:3],
                             start=True, stop=True).then_inc(g_ready, 1)

        @block.gpsimd
        def _(pool):
            for k in range(2):
                nc.gpsimd.memset(va[k][:], 0.0).then_inc(z_in, 1)
            pool.wait_ge(z_in, 2)
            for k in range(2):
                nc.gpsimd.memset(va[k][:, :, :, DIM:DIM + 1], 1.0).then_inc(z_in, 1)
            nc.gpsimd.memset(ones[:], 1.0).then_inc(z_in, 1)
            pool.wait_ge(z_in, 5)

    kx_in, qx_in, c_row, stored, loaded, y_out = (
        [sem(f"{n}{k}") for k in range(2)] for n in ("l1_kx_in", "l1_qx_in", "l1_c_row", "stored", "loaded", "y_out"))
    pv_done, proj_q, proj_k, proj_v, max_ready, s_ready, turned, c_turned, f_turned, z_ready = (
        sem("l1_" + n) for n in ("pv_done", "proj_q", "proj_k", "proj_v", "max_ready", "s_ready", "turned", "c_turned",
                                 "f_turned", "z_ready"))
    exp_done, ot_out, f_out, v_out, qk_out, c_out, xh_done = (
        sem("l1_" + n) for n in ("exp_done", "ot_out", "f_out", "v_out", "qk_out", "c_out", "xh_done"))
    max_done, y_done, cast_done, r_done, on_done = (
        sem("l1_" + n) for n in ("max_done", "y_done", "cast_done", "r_done", "on_done"))
    LAGS = (-2, 3)

    with nc.Block() as block:
        @block.sync
        def _(sp):
            def spread(i, dst, src, done):
                for h in range(TILE_HEADS):
                    at = slice(h * DIM, (h + 1) * DIM)
                    sp.dma_start(dst[at, h::TILE_HEADS, :], src[at, :, :]).then_inc(done, 16)

            def spread_k(i):
                wait_alone(sp, cast_done, i.count(1))
                wait_alone(sp, max_ready, i.plus(-1).count(ROUNDS))
                spread(i, kx, qkb[:, 2:4, :], kx_in[i.k])

            def spread_q(i):
                wait_alone(sp, qk_out, i.count(2))
                wait_alone(sp, s_ready, i.plus(-2).count(ROUNDS))
                spread(i, qx[i.k], qk[i.k][:, 0:2, :], qx_in[i.k])

            def row_c(i):
                wait_alone(sp, c_out, i.count(1))
                wait_alone(sp, s_ready, i.plus(-2).count(ROUNDS))
                sp.dma_start(row_max[i.k][:, :, :], ct[i.k][:, :]).then_inc(c_row[i.k], 16)

            def regroup(i):
                wait_alone(sp, on_done, i.count(1))
                wait_alone(sp, loaded[i.k], i.plus(-2).dmas(1))
                for t in range(TT):
                    sp.dma_start(scratch[i.k, :, t * P:(t + 1) * P, :].rearrange("h p e -> p h e"),
                                 on[:, t, :].rearrange("p (h e) -> p h e", h=HEADS)).then_inc(stored[i.k], 16)

            def fetch(i):
                wait_alone(sp, stored[i.k], i.dmas(TT))
                wait_alone(sp, f_turned, i.plus(-1).count(1))
                sp.dma_start(rows[:, :, :],
                             scratch[i.k].rearrange("h n e -> (h n e)").rearrange("(t p f) -> p t f", p=P, f=CH)
                             ).then_inc(loaded[i.k], 16)

            def store(i):
                wait_alone(sp, y_done, i.count(1))
                wait_alone(sp, y_out[i.k], i.plus(-2).dmas(1))
                sp.dma_start(out.rearrange("(c p) i t -> p c i t", p=P)[:, :, bass.ds(i.index(), 1), :]
                             .rearrange("p c i t -> p c (i t)"),
                             X[:, bass.ds(i.index(), 1), :, :].rearrange("p i c t -> p c (i t)")).then_inc(y_out[i.k], 16)

            pipeline(sp, images, [(store, -2), (row_c, 1), (spread_k, 2), (regroup, -1), (fetch, -1),
                                  (spread_q, 2)], LAGS)
            for k in range(2):
                sp.wait_ge(y_out[k], 16 * ((images + 1 - k) // 2))

        @block.tensor
        def _(pe):
            def scores(i, rnd):
                if rnd == 0:
                    wait(pe, qx_in[i.k], i.dmas(TILE_HEADS))
                    wait(pe, exp_done, i.plus(-1).count(ROUNDS))
                    wait(pe, on_done, i.plus(-2).count(1))
                else:
                    wait(pe, exp_done, i.count(ROUNDS, rnd))
                for stage in range(3):
                    if stage == 2 and rnd == 0:
                        wait(pe, c_row[i.k], i.dmas(1))
                    for b in range(2):
                        s = SCORES[2 * rnd + b]
                        bank = C[0][:, b * 512:(b + 1) * 512].rearrange("p (h q) -> p h q", h=s.heads)
                        if stage == 0:
                            nc.tensor.matmul(bank, qk[i.k][:, 2 + s.tile, s.block * P:(s.block + 1) * P],
                                             qx[i.k][:, s.which, s.cols], start=True, stop=False, skip_group_check=True)
                        elif stage == 1:
                            mask = (above if s.ahead else below)[:, :].unsqueeze(1).to_broadcast([P, s.heads, P])
                            nc.tensor.matmul(bank[:, :, s.diagonal:s.diagonal + P], identb[:, :], mask,
                                             start=False, stop=False, skip_group_check=True)
                        else:
                            last = nc.tensor.matmul(bank, ones[COL * i.k:COL * i.k + 1, :], row_max[i.k][:, s.which, s.cols],
                                                    start=False, stop=True, skip_group_check=True)
                last.then_inc(s_ready, 1)

            def maxima(i, rnd):
                if rnd == 0:
                    wait(pe, kx_in[i.k], i.dmas(TILE_HEADS))
                    wait(pe, max_done, i.plus(-1).count(ROUNDS))
                else:
                    wait(pe, max_done, i.count(ROUNDS, rnd))
                for b in range(2):
                    s = MAXIMA[2 * rnd + b]
                    bank = C[1][:, b * 512:(b + 1) * 512].rearrange("p (h k) -> p h k", h=s.heads)
                    nc.tensor.matmul(bank, qkb[:, s.tile, s.block * P:(s.block + 1) * P],
                                     kx[:, s.which, s.cols], start=True, stop=False, skip_group_check=True)
                    mask = (below if s.ahead else above)[:, :].unsqueeze(1).to_broadcast([P, s.heads, P])
                    last = nc.tensor.matmul(bank[:, :, s.diagonal:s.diagonal + P], identb[:, :], mask,
                                            start=False, stop=True, skip_group_check=True)
                last.then_inc(max_ready, 1)

            def weigh(i, g):
                if g == 0:
                    wait(pe, exp_done, i.count(ROUNDS))
                    wait(pe, v_out, i.count(1))
                    wait(pe, ot_out, i.plus(-1).count(2))
                    if i.plus(2).among(images):
                        wait(pe, qk_out, i.plus(2).count(2))
                for part in range(2):
                    for c in range(QUADS):
                        h = g * QUADS + c
                        block = part if g < 2 else 1 - part
                        n = next(n for n, s in enumerate(SCORES) if s.block == block and s.head <= h < s.head + s.heads)
                        s = SCORES[n]
                        at = 512 * n + (h - s.head) * s.size
                        to = (g % 2) * TOKENS + s.start
                        last = nc.tensor.matmul(A[g // 2][COL * c:COL * (c + 1), to:to + s.size], va[i.k][:, block, h, :],
                                                probs[i.k][:, at:at + s.size], start=(part == 0), stop=(part == 1),
                                                tile_position=(0, COL * c), skip_group_check=True)
                last.then_inc(pv_done, 1)

            def project_qk(i, n):
                if n == 0:
                    wait(pe, xh_done, i.count(2))
                wait(pe, ot_out, i.plus(-3).count(2, n + 1))
                if n == 0:
                    wait(pe, qk_out, i.plus(-1).count(2))
                for o in range(CT):
                    for c in range(CT):
                        last = nc.tensor.matmul(A[n][:, o * TOKENS:(o + 1) * TOKENS],
                                                wqk[:, c, n * CH + o * P:n * CH + (o + 1) * P], xh[i.k][:, c, :],
                                                start=(c == 0), stop=(c == CT - 1))
                last.then_inc(proj_k if n else proj_q, 1)

            def project_v(i):
                wait(pe, xh_done, i.count(2))
                wait(pe, v_out, i.plus(-1).count(1))
                for t in range(TT):
                    for c in range(CT):
                        last = nc.tensor.matmul(A[2][:, t * CH:(t + 1) * CH], xh[i.k][:, c, t * P:(t + 1) * P],
                                                wv[:, c, :], start=(c == 0), stop=(c == CT - 1))
                last.then_inc(proj_v, 1)

            def turn_c(i):
                wait(pe, max_done, i.count(ROUNDS))
                wait(pe, y_done, i.plus(-3).count(1))
                for t in range(TT):
                    last = nc.tensor.transpose(E[0:HEADS, t * P:(t + 1) * P], cm[:, t, :], ident[:, :])
                last.then_inc(c_turned, 1)

            def turn(i):
                wait(pe, ot_out, i.count(2))
                wait(pe, on_done, i.plus(-1).count(1))
                if i.plus(1).among(images):
                    wait(pe, exp_done, i.plus(1).count(ROUNDS))
                for t in range(TT):
                    for g in range(QUADS):
                        last = nc.tensor.transpose(C[0][:, t * 512 + g * P:t * 512 + (g + 1) * P],
                                                   ots[:, g, t * P:(t + 1) * P], ident[:, :])
                last.then_inc(turned, 1)

            def turn_rows(i):
                wait(pe, loaded[i.k], i.dmas(1))
                wait(pe, y_done, i.plus(-1).count(1))
                if i.plus(2).among(images):
                    wait(pe, c_out, i.plus(2).count(1))
                for t in range(TT):
                    for f in range(CT):
                        last = nc.tensor.transpose(E[:, f * TOKENS + t * P:f * TOKENS + (t + 1) * P],
                                                   rows[:, t, f * P:(f + 1) * P], ident[:, :])
                last.then_inc(f_turned, 1)

            def output(i):
                wait(pe, f_out, i.count(1))
                for o in range(CT):
                    for f in range(CT):
                        last = nc.tensor.matmul(E[:, o * TOKENS:(o + 1) * TOKENS], wo[:, f, o * P:(o + 1) * P],
                                                of[:, f, :], start=(f == 0), stop=(f == CT - 1))
                last.then_inc(z_ready, 1)

            def S(rnd):
                return lambda i: scores(i, rnd), 0

            def M(rnd):
                return lambda i: maxima(i, rnd), 1

            def W(g):
                return lambda i: weigh(i, g), -1

            pipeline(pe, images, [S(0), W(0), S(1), W(1), S(2), M(0), W(2), S(3), M(1), W(3), (turn_rows, -2), S(4),
                                  M(2), (output, -2), S(5), M(3), (project_v, 1), M(4),
                                  (lambda i: project_qk(i, 0), 2), M(5), (lambda i: project_qk(i, 1), 2),
                                  (turn_c, 1), (turn, -1)], LAGS)

        @block.scalar
        def _(act):
            def exponent(i, rnd):
                wait(act, s_ready, i.count(ROUNDS, rnd + 1))
                if rnd == 0:
                    wait(act, pv_done, i.plus(-2).count(QUADS))
                nc.scalar.activation(probs[i.k][:, rnd * 1024:(rnd + 1) * 1024], C[0][:, :], ACT.Exp).then_inc(exp_done, 1)

            def copy_outputs(i, n):
                wait(act, pv_done, i.count(QUADS, 2 * n + 2))
                wait(act, turned, i.plus(-1).count(1))
                nc.scalar.activation(ots[:, 2 * n:2 * n + 2, :].rearrange("p g q -> p (g q)"), A[n][:, :],
                                     ACT.Copy).then_inc(ot_out, 1)

            def copy_rows(i):
                wait(act, f_turned, i.count(1))
                wait(act, z_ready, i.plus(-1).count(1))
                nc.scalar.activation(of[:, :, :].rearrange("p f t -> p (f t)"), E[:, :], ACT.Copy).then_inc(f_out, 1)

            def copy_v(i):
                wait(act, proj_v, i.count(1))
                wait(act, pv_done, i.plus(-2).count(QUADS))
                nc.scalar.activation(va[i.k][:, :, :, 0:DIM].rearrange("p t h e -> p (t h) e"),
                                     A[2][:, :].rearrange("p (n e) -> p n e", e=DIM), ACT.Copy).then_inc(v_out, 1)

            def copy_qk(i, n):
                wait(act, proj_k if n else proj_q, i.count(1))
                if n == 0:
                    wait(act, qx_in[i.k], i.plus(-2).dmas(TILE_HEADS))
                    wait(act, s_ready, i.plus(-2).count(ROUNDS))
                    wait(act, cast_done, i.plus(-2).count(1))
                nc.scalar.activation(qk[i.k][:, 2 * n:2 * n + 2, :].rearrange("p o t -> p (o t)"), A[n][:, :],
                                     ACT.Copy, scale=1.0 if n else DIM ** -0.5).then_inc(qk_out, 1)

            def copy_c(i):
                wait(act, c_turned, i.count(1))
                wait(act, c_row[i.k], i.plus(-2).dmas(1))
                nc.scalar.activation(ct[i.k][:, :], E[0:HEADS, 0:TOKENS], ACT.Copy, scale=-1.0).then_inc(c_out, 1)

            def normalize(i):
                wait(act, proj_v, i.plus(-2).count(1))
                wait(act, proj_k, i.plus(-2).count(1))
                for c in range(CT):
                    nc.scalar.activation(xh[i.k][:, c, :], X[:, bass.ds(i.index(), 1), c, :].rearrange("p i t -> p (i t)"),
                                         ACT.Identity,
                                         bias=shift[:, bass.ds(i.index(), 1), c],
                                         scale=rs_y[:, bass.ds(i.index(), 1), c]).then_inc(xh_done, 1)

            def X_(rnd):
                return lambda i: exponent(i, rnd), 0

            pipeline(act, images, [X_(0), X_(1), (lambda i: copy_outputs(i, 0), -1), X_(2), X_(3),
                                   (lambda i: copy_outputs(i, 1), -1), (copy_rows, -2), X_(4), X_(5), (copy_v, 1),
                                   (lambda i: copy_qk(i, 0), 2), (lambda i: copy_qk(i, 1), 2), (copy_c, 1),
                                   (normalize, 3)], LAGS)

        @block.vector
        def _(dve):
            def take_max(i, rnd):
                s = MAXIMA[2 * rnd]
                wait(dve, max_ready, i.count(ROUNDS, rnd + 1))
                if rnd == 0:
                    wait(dve, c_turned, i.plus(-1).count(1))
                nc.vector.reduce_max(cm[:, s.block, s.head:s.head + 2 * s.heads],
                                     C[1][:, :].rearrange("p (h k) -> p h k", k=s.size), AX_X).then_inc(max_done, 1)

            def residual(i):
                wait(dve, z_ready, i.count(1))
                x = X[:, bass.ds(i.index(), 1), :, :].rearrange("p i c t -> p (i c t)")
                nc.vector.tensor_tensor(x, E[:, :], x, ALU.add).then_inc(y_done, 1)

            def cast(i):
                wait(dve, qk_out, i.count(2))
                wait(dve, kx_in[1 - i.k], i.plus(-1).dmas(TILE_HEADS))
                wait(dve, max_ready, i.plus(-1).count(ROUNDS))
                nc.vector.tensor_copy(qkb[:, :, :].rearrange("p n t -> p (n t)"),
                                      qk[i.k][:, :, :].rearrange("p n t -> p (n t)")).then_inc(cast_done, 1)

            def divide(i):
                wait(dve, turned, i.count(1))
                wait(dve, stored[1 - i.k], i.plus(-1).dmas(TT))
                heads = C[0][:, :].rearrange("p (n e) -> p n e", e=COL)
                nc.vector.reciprocal(rdn[:, :], heads[:, :, DIM]).then_inc(r_done, 1)
                wait(dve, r_done, i.count(1))
                nc.vector.tensor_tensor(on[:, :, :].rearrange("p t (h e) -> p (t h) e", e=DIM), heads[:, :, 0:DIM],
                                        rdn[:, :].unsqueeze(2).to_broadcast([P, TT * HEADS, DIM]),
                                        ALU.mult).then_inc(on_done, 1)

            def R(rnd):
                return lambda i: take_max(i, rnd), 1

            pipeline(dve, images, [R(0), R(1), R(2), (residual, -2), R(3), R(4), R(5), (cast, 2), (divide, -1)], LAGS)


def lay_out(x, L0_conv_Wq, L0_conv_Wk, L0_conv_Wv, L0_conv_bv, L0_conv_Wo, L0_conv_bo, L0_conv_logit_scale,
            L0_conv_cpb_w1, L0_conv_cpb_b1, L0_conv_cpb_w2, L1_conv_Wq_lb, L1_conv_Wk_lb, L1_conv_Wv_lb,
            L1_conv_Wq_la, L1_conv_Wk_la, L1_conv_Wv_la, L1_conv_Wo):
    bfloat16 = mybir.dt.np(BF16)

    def rows(*weights):
        t = np.concatenate([np.asarray(a).reshape(-1, CH).T for a in weights], axis=1)
        return t.reshape(CT, P, -1).transpose(1, 0, 2)

    def column(a):
        return np.asarray(a).reshape(CT, P).T

    images = x.shape[0]
    rolled = np.roll(np.asarray(x), (-SHIFT, -SHIFT), axis=(1, 2)).reshape(images, TOKENS, CH)
    wo = rows(L0_conv_Wo)
    by_head = np.asarray(L0_conv_Wo).T.reshape(QUADS, QUADS, DIM, CH)
    wop = np.zeros((QUADS, 2, DIM, 2, QUADS, CH), wo.dtype)
    for ww in range(2):
        wop[:, ww, :, ww] = by_head.transpose(1, 2, 0, 3)
    queries, keys = window_rows()
    aux_q = np.zeros((5, HEADS, TOKENS), np.float32)
    aux_q[0:4] = queries[:, None, :]
    ones_win = np.zeros((2, WTOK, 2, DIM), np.float32)
    for ww in range(2):
        ones_win[ww, :, ww] = 1.0
    return {
        "xr": rolled.transpose(2, 0, 1),
        "wqk0": rows(L0_conv_Wq, L0_conv_Wk), "wv0": rows(L0_conv_Wv), "wo0": wo,
        "wop0": wop.reshape(P, 2, QUADS, CH), "bv0": column(L0_conv_bv), "bo0": column(L0_conv_bo),
        "scale0": np.broadcast_to(np.asarray(L0_conv_logit_scale).reshape(1, HEADS), (P, HEADS)),
        "cpb_w1": np.asarray(L0_conv_cpb_w1).T, "cpb_b1": np.asarray(L0_conv_cpb_b1).reshape(HIDDEN, 1),
        "cpb_w2": np.asarray(L0_conv_cpb_w2).T, "points": relative_points(),
        "ident": np.eye(P, dtype=np.float32),
        "gavg": np.kron(np.eye(P // GROUP), np.full((GROUP, GROUP), 0.5 / GROUP)).astype(np.float32),
        "ones_win": ones_win.reshape(P, COL),
        "aux_k": np.concatenate([keys, np.ones((1, TOKENS), np.float32)]).astype(bfloat16),
        "aux_q": aux_q.astype(bfloat16),
        "wqk1": rows(L1_conv_Wq_lb, L1_conv_Wq_la, L1_conv_Wk_lb, L1_conv_Wk_la),
        "wv1": rows(L1_conv_Wv_lb, L1_conv_Wv_la), "wo1": rows(L1_conv_Wo),
        "identb": np.eye(P).astype(bfloat16),
        "below": (np.tril(np.ones((P, P)), -1) * MASKED).astype(bfloat16),
        "above": (np.triu(np.ones((P, P)), 1) * MASKED).astype(bfloat16),
    }


def kernel(**inputs):
    import concourse.bacc as bacc
    from concourse.bass_utils import run_bass_kernel_spmd

    arrays = {"in_" + n: np.ascontiguousarray(a) for n, a in lay_out(**inputs).items()}
    images = inputs["x"].shape[0]
    nc = bacc.Bacc("TRN2", target_bir_lowering=False, num_devices=1)
    ins = {n[3:]: nc.dram_tensor(n, a.shape, mybir.dt.from_np(a.dtype), kind="ExternalInput").ap()
           for n, a in arrays.items()}
    out = nc.dram_tensor("out", (CH, images, TOKENS), F32, kind="ExternalOutput").ap()
    build_network(nc, ins.pop("xr"), out, ins)
    got = run_bass_kernel_spmd(nc, [arrays], core_ids=[0]).results[0]["out"]
    return np.ascontiguousarray(got.transpose(1, 2, 0)).reshape(images, SIDE, SIDE, CH)
```

```python
import math
from contextlib import ExitStack

import numpy as np

import concourse.bass as bass
from concourse import mybir

F32 = mybir.dt.float32
BF16 = mybir.dt.bfloat16
I32 = mybir.dt.int32
ALU = mybir.AluOpType
ACT = mybir.ActivationFunctionType
AX_X = mybir.AxisListType.X

P = 128
SIDE = 16
TOKENS = SIDE * SIDE
WIN = 8
WTOK = WIN * WIN
SHIFT = 4
CH = 256
CT = CH // P
HEADS = 16
DIM = CH // HEADS
TILE_HEADS = P // DIM
GROUP = CH // 32
TT = TOKENS // P
COL = 32
QUADS = P // COL
HIDDEN = 128
PARTS = 3
PART_OF_Q = (0, 0, 0, 1, 1, 2)
PART_OF_K = (0, 1, 2, 0, 1, 0)
STACK = len(PART_OF_Q) * DIM
STACK_DMAS = 2 * len(PART_OF_Q)
MASKS = 4
LOG100 = math.log(100.0)
EPS = 1e-5
NORM_MIN = 1e-12
MASKED = -1e30
RSQRT_SEED = 1597463007.0


class Image:

    def __init__(self, pair, offset):
        self.pair, self.offset = pair, offset
        self.k = offset % 2

    def plus(self, n):
        return Image(self.pair, self.offset + n)

    def among(self, images):
        return not isinstance(self.pair, int) or self.pair * 2 + self.offset < images

    def index(self, n=0):
        return self.pair * 2 + (self.offset + n)

    def count(self, per, n=None):
        return self.pair * (2 * per) + (self.offset * per + (per if n is None else n))

    def dmas(self, n):
        return self.pair * (16 * n) + 16 * n * (self.offset // 2 + 1)


def wait(eng, sem, value):
    if not (isinstance(value, int) and value <= 0):
        eng.wait_ge(sem, value)


def wait_alone(eng, sem, value):
    if not (isinstance(value, int) and value <= 0):
        eng.wait_ge(sem, value)
        if not isinstance(value, int):
            eng.nop(nofuse=True)


def pipeline(eng, images, stages, lags):
    low, high = lags
    first_pair = (2 - low + 1) // 2
    last_pair = (images - 1 - high - 1) // 2
    pairs = range(first_pair, last_pair + 1)

    def step(s):
        for stage, lag, *past in stages:
            if 0 <= s + lag < images + len(past):
                stage(Image(0, s + lag))

    if len(pairs) < 2:
        for s in range(-high, images - low):
            step(s)
        return
    for s in range(-high, 2 * pairs[0]):
        step(s)
    with eng.Fori(pairs[0], pairs[-1] + 1) as pair:
        for k in range(2):
            for stage, lag, *_ in stages:
                stage(Image(pair, k + lag))
    for s in range(2 * pairs[-1] + 2, images - low):
        step(s)


def keep_parts(sp, i, parts, split_parts, split_out):
    sp.dma_start(split_parts[i.k].rearrange("n p s -> p n s"),
                 parts[:, :, :, :, :].rearrange("p n a z t -> p n (a z t)")).then_inc(split_out[i.k], 16)


def stack_parts(sp, i, split_parts, stack, stacked):
    src = split_parts[i.k].rearrange("n (h e) (a z t) -> e (n h) a z t", e=DIM, a=PARTS, z=2)
    for z, part_of in ((0, PART_OF_Q), (1, PART_OF_K)):
        for slot, part in enumerate(part_of):
            sp.dma_start(stack[i.k][slot * DIM:(slot + 1) * DIM, z, :, :],
                         src[:, :, part, z, :]).then_inc(stacked[i.k], 16)


def window_rows():
    t, ww, rr, c = np.meshgrid(np.arange(2), np.arange(2), np.arange(WIN), np.arange(WIN), indexing="ij")
    right, left = (ww == 1) & (c >= WIN - SHIFT), (ww == 1) & (c < WIN - SHIFT)
    low, high = (t == 1) & (rr >= WIN - SHIFT), (t == 1) & (rr < WIN - SHIFT)
    queries = np.stack([right, left, low, high]).reshape(4, TOKENS).astype(np.float32) * MASKED
    keys = np.stack([left, right, high, low]).reshape(4, TOKENS).astype(np.float32)
    return queries, keys


def relative_points():
    rows, cols = np.meshgrid(np.arange(WIN), np.arange(WIN), indexing="ij")
    at = np.stack([rows.ravel(), cols.ravel()]).astype(np.float32)
    rel = (at[:, :, None] - at[:, None, :]) / np.float32(WIN - 1) * np.float32(8.0)
    rel = np.sign(rel) * np.log2(np.abs(rel) + np.float32(1.0)) / np.float32(3.0)
    return rel.astype(np.float32).reshape(2, WTOK * WTOK)


def build_network(nc, xr, out, given):
    images = xr.shape[1]
    scratch = nc.dram_tensor("scratch_heads", [2, HEADS, TOKENS, DIM], F32).ap()
    split_parts = nc.dram_tensor("scratch_parts", [2, CT, P, PARTS * 2 * TOKENS], BF16).ap()

    with ExitStack() as shared:
        def sb(name, shape, dt=F32, ctx=shared):
            return ctx.enter_context(nc.sbuf_tensor(name, shape, dt))

        X = sb("X", [P, images + 1, CT, TOKENS])
        stats2 = sb("stats2", [P, images, CT, 6])
        probs = [sb(f"probs{k}", [P, 6144]) for k in range(2)]
        stack = [sb(f"stack{k}", [P, 2, HEADS, TOKENS], BF16) for k in range(2)]
        xh = [sb(f"xh{k}", [P, CT, TOKENS]) for k in range(2)]
        parts = sb("parts", [P, CT, PARTS, 2, TOKENS], BF16)
        rest = [sb(f"rest{n}", [P, 2 * TOKENS]) for n in range(2)]
        ident = sb("ident", [P, P])
        gavg = sb("gavg", [P, P])
        A = [shared.enter_context(nc.psum_tensor(f"psA{n}", [P, 512], F32)) for n in range(3)]
        C = [shared.enter_context(nc.psum_tensor(f"psC{n}", [P, 1024], F32)) for n in range(2)]
        E = shared.enter_context(nc.psum_tensor("psE", [P, 512], F32))
        B = [C[1][:, 0:512], C[1][:, 512:1024]]

        with ExitStack() as ctx:
            layer0(nc, ctx, images, xr, given, X, stats2, probs, xh, parts, rest, stack, split_parts, ident, gavg, A, B, C, E)
        with ExitStack() as ctx:
            layer1(nc, ctx, images, out, given, scratch, X, stats2, probs, xh, parts, rest, stack, split_parts, ident, gavg, A, C, E)


def layer0(nc, ctx, images, xr, given, X, stats2, probs, xh, parts, rest, stack, split_parts, ident, gavg, A, B, C, E):
    def sb(name, shape, dt=F32):
        return ctx.enter_context(nc.sbuf_tensor(name, shape, dt))

    def sem(name):
        return ctx.enter_context(nc.semaphore(name))

    prob = [p[:, 0:TT * HEADS * WTOK].rearrange("p (t h q) -> p t h q", t=TT, h=HEADS) for p in probs]
    sq = probs[0][:, 2048:3072].rearrange("p (t c) -> p t c", t=TT)
    qkn = probs[0][:, 3072:4096].rearrange("p (t c) -> p t c", t=TT)
    zb = probs[1][:, 2048:2560].rearrange("p (c t) -> p c t", c=CT)
    rd = probs[1][:, 2560:3072]
    wop = probs[1][:, 3072:5120].rearrange("p (ww g o) -> p ww g o", ww=2, g=QUADS)
    wqk = probs[1][:, 5120:6144].rearrange("p (c o) -> p c o", c=CT)
    hidden = probs[0][:, 0:WTOK * WTOK]
    e_bias = [probs[1][:, n * 1024:(n + 1) * 1024] for n in range(3)]
    wo = xh[0]
    wv = sb("wv0", [P, CT, CH])
    bv = sb("bv0", [P, CT])
    bo = sb("bo0", [P, CT])
    bz = sb("bz0", [P, CT])
    scale = sb("scale0", [P, HEADS])
    ones_win = sb("ones_win", [P, COL])
    pt = stack[1][0:2, :, :, :].rearrange("p z h t -> p (z h t)").bitcast(F32)
    w1 = sb("cpb_w1", [2, HIDDEN])
    b1 = sb("cpb_b1", [HIDDEN, 1])
    w2 = sb("cpb_w2", [HIDDEN, HEADS])
    ebias = sb("ebias", [P, HEADS, WTOK])
    rs = sb("rs", [P, 66])
    rs_bits = sb("rs_bits", [P, 66], I32)
    rs_y = sb("rs_y", [P, 66])
    rs_t = sb("rs_t", [P, 66])
    shift = sb("shift", [P, CT])
    bn = sb("bn", [P, CT, 6])
    mm = sb("mm", [P, 2 * CT])
    gs = sb("gs", [P, CT, 2])
    gm = sb("gm", [P, CT])
    cm = sb("cm", [P, TT, HEADS])
    ct = [sb(f"ct{k}", [HEADS, TOKENS], BF16) for k in range(2)]
    vw = [sb(f"vw{k}", [P, TT, HEADS, 2, DIM]) for k in range(2)]
    ot = sb("ot", [P, TT, QUADS, WTOK])

    c_in, p_hid, a_hid, p_tab, a_tab, d_tab, a_tab2, tab_in, z_in, p_bz, d_bz = (
        sem(n) for n in ("c_in", "p_hid", "a_hid", "p_tab", "a_tab", "d_tab", "a_tab2", "tab_in", "z_in",
                         "p_bz", "d_bz"))
    loads = [(ident, given["ident"]), (gavg, given["gavg"]), (ones_win, given["ones_win"]), (pt, given["points"]),
             (w1, given["cpb_w1"]), (b1, given["cpb_b1"]), (w2, given["cpb_w2"]), (wqk, given["wqk0"]), (wv, given["wv0"]),
             (wo, given["wo0"]), (wop, given["wop0"]), (bv, given["bv0"]), (bo, given["bo0"]), (scale, given["scale0"])]
    aux = slice(STACK, STACK + MASKS + 1)
    loads += [(stack[k][aux, :, :, :], given["aux"]) for k in range(2)]

    with nc.Block() as block:
        @block.sync
        def _(sp):
            for dst, src in loads:
                sp.dma_start(dst if isinstance(dst, bass.AP) else dst[:], src).then_inc(c_in, 16)
            sp.wait_ge(a_tab2, 1)
            sp.dma_start(ebias[WTOK:P, :, :], ebias[0:WTOK, :, :]).then_inc(tab_in, 16)
            sp.wait_ge(tab_in, 16)

        @block.gpsimd
        def _(pool):
            for k in range(2):
                nc.gpsimd.memset(vw[k][:], 0.0)
            nc.gpsimd.memset(rs[:], 1.0).then_inc(z_in, 1)
            pool.wait_ge(z_in, 1)

        @block.tensor
        def _(pe):
            pe.wait_ge(c_in, 16 * len(loads))
            for n in range(8):
                if n >= 3:
                    pe.wait_ge(a_hid, n - 2)
                nc.tensor.matmul(A[n % 3][:], w1[:], pt[:, 512 * n:512 * n + 512],
                                 start=True, stop=True).then_inc(p_hid, 1)
            pe.wait_ge(a_hid, 8)
            for q in range(WTOK):
                last = nc.tensor.matmul(C[0][0:WTOK, q * HEADS:(q + 1) * HEADS],
                                        hidden[:, q * WTOK:(q + 1) * WTOK], w2[:], start=True, stop=True)
            last.then_inc(p_tab, 1)
            for o in range(CT):
                for c in range(CT):
                    last = nc.tensor.matmul(E[:, o:o + 1], wo[:, c, o * P:(o + 1) * P], bv[:, c:c + 1],
                                            start=(c == 0), stop=(c == CT - 1))
            last.then_inc(p_bz, 1)

        @block.scalar
        def _(act):
            for n in range(8):
                act.wait_ge(p_hid, n + 1)
                nc.scalar.activation(hidden[:, 512 * n:512 * n + 512], A[n % 3][:], ACT.Relu,
                                     bias=b1[:, 0:1]).then_inc(a_hid, 1)
            act.wait_ge(p_tab, 1)
            nc.scalar.activation(e_bias[0][0:WTOK, :], C[0][0:WTOK, :], ACT.Exp, scale=-1.0).then_inc(a_tab, 1)
            act.wait_ge(d_tab, 2)
            nc.scalar.activation(ebias[0:WTOK, :, :].rearrange("p h q -> p q h"),
                                 e_bias[2][0:WTOK, :].rearrange("p (q h) -> p q h", h=HEADS),
                                 ACT.Exp, scale=16.0).then_inc(a_tab2, 1)
            act.wait_ge(d_bz, 2)
            nc.scalar.activation(scale[:], scale[:], ACT.Exp).then_inc(a_tab2, 1)

        @block.vector
        def _(dve):
            dve.wait_ge(a_tab, 1)
            nc.vector.tensor_scalar(e_bias[1][0:WTOK, :], e_bias[0][0:WTOK, :], 1.0, None,
                                    ALU.add).then_inc(d_tab, 1)
            dve.wait_ge(d_tab, 1)
            nc.vector.reciprocal(e_bias[2][0:WTOK, :], e_bias[1][0:WTOK, :]).then_inc(d_tab, 1)
            dve.wait_ge(p_bz, 1)
            nc.vector.tensor_tensor(bz[:], E[:, 0:CT], bo[:], ALU.add).then_inc(d_bz, 1)
            nc.vector.tensor_scalar(scale[:], scale[:], LOG100, None, ALU.min).then_inc(d_bz, 1)

    x_in = [sem(f"x_in{k}") for k in range(2)]
    split_out = [sem(f"split_out{k}") for k in range(2)]
    stacked = [sem(f"stacked{k}") for k in range(2)]
    c_row = [sem(f"c_row{k}") for k in range(2)]
    pv_done, proj_qk, proj_v, max_ready, s_ready, z_ready, turned, c_turned, g_ready = (
        sem(n) for n in ("pv_done", "proj_qk", "proj_v", "max_ready", "s_ready", "z_ready", "turned",
                         "c_turned", "g_ready"))
    squared, exp_done, z_out, high_out, mid_out, c_out, xh_done, v_out = (
        sem(n) for n in ("squared", "exp_done", "z_out", "high_out", "mid_out", "c_out", "xh_done", "v_out"))
    r_done, o_done, sum_done, gn_chain, rs_ready, max_done, qkn_done, x1_done, rest_out, stats = (
        sem(n) for n in ("r_done", "o_done", "sum_done", "gn_chain", "rs_ready", "max_done", "qkn_done",
                         "x1_done", "rest_out", "stats"))
    newton, biased, low_out, sums_done = (sem(n) for n in ("newton", "biased", "low_out", "sums_done"))
    LAGS = (-1, 6)
    NEWTON = 11

    def by_kind(ap):
        return ap[:, :].rearrange("p (z n t) -> p n z t", z=2, n=CT)

    def by_tile(ap):
        return ap[:, :].rearrange("p (n z t) -> p n z t", n=CT, z=2)

    def tile_parts(part, t):
        return parts[:, :, part, :, t * P:(t + 1) * P]

    def win(t, ww):
        return slice(t * P + ww * WTOK, t * P + (ww + 1) * WTOK)

    with nc.Block() as block:
        @block.sync
        def _(sp):
            def load(i):
                wait_alone(sp, stats, i.plus(-2).count(4, 1))
                src = xr.rearrange("(c p) i t -> p c i t", p=P)[:, :, bass.ds(i.index(), 1), :]
                sp.dma_start(X[:, bass.ds(i.index(1), 1), :, :].rearrange("p i c t -> p c (i t)"),
                             src.rearrange("p c i t -> p c (i t)")).then_inc(x_in[i.k], 16)

            def keep_split(i):
                wait_alone(sp, low_out, i.count(2))
                wait_alone(sp, stacked[i.k], i.plus(-2).dmas(STACK_DMAS))
                keep_parts(sp, i, parts, split_parts, split_out)

            def stack_up(i):
                wait_alone(sp, split_out[i.k], i.dmas(1))
                wait_alone(sp, s_ready, i.plus(-2).count(2))
                stack_parts(sp, i, split_parts, stack, stacked)

            pipeline(sp, images, [(load, 6), (keep_split, 2), (stack_up, 2)], LAGS)

        @block.tensor
        def _(pe):
            def weigh(i):
                wait(pe, biased, i.count(2))
                wait(pe, v_out, i.count(2))
                if i.plus(1).among(images):
                    wait(pe, max_done, i.plus(1).count(4))
                for c in range(QUADS):
                    nc.tensor.matmul(B[1][COL * c:COL * c + COL, :].rearrange("p (t g q) -> p t g q", t=TT, g=QUADS),
                                     ones_win[:, :], prob[i.k][:, :, c::QUADS, :], start=True, stop=True,
                                     tile_position=(0, COL * c)).then_inc(sums_done, 1)
                for t in range(TT):
                    for g in range(QUADS):
                        for c in range(QUADS):
                            h = g * QUADS + c
                            at = (t * QUADS + g) * WTOK
                            last = nc.tensor.matmul(B[0][COL * c:COL * c + COL, at:at + WTOK], vw[i.k][:, t, h, :, :],
                                                    prob[i.k][:, t, h, :], start=True, stop=True,
                                                    tile_position=(0, COL * c))
                last.then_inc(pv_done, 1)

            def project(i):
                wait(pe, xh_done, i.count(4))
                wait(pe, rest_out, i.plus(-1).count(2))
                for t in range(TT):
                    for c in range(CT):
                        last = nc.tensor.matmul(A[t][:], xh[i.k][:, c, t * P:(t + 1) * P], wqk[:, c, :],
                                                start=(c == 0), stop=(c == CT - 1))
                    last.then_inc(proj_qk, 1)

            def project_v(i):
                wait(pe, c_out, i.plus(-1).count(1))
                for t in range(TT):
                    for c in range(CT):
                        last = nc.tensor.matmul(A[2][:, t * CH:(t + 1) * CH], xh[i.k][:, c, t * P:(t + 1) * P],
                                                wv[:, c, :], start=(c == 0), stop=(c == CT - 1))
                last.then_inc(proj_v, 1)

            def maxima(i, n):
                t, g = divmod(n, CT)
                if n == 0:
                    wait(pe, stacked[i.k], i.dmas(STACK_DMAS))
                if n < 2:
                    wait(pe, o_done, i.plus(-2).count(1))
                else:
                    wait(pe, max_done, i.count(4, n - 1))
                rows = slice(0, STACK + MASKS)
                for h in range(TILE_HEADS):
                    for ww in range(2):
                        last = nc.tensor.matmul(B[n % 2][WTOK * ww:WTOK * (ww + 1), h * WTOK:(h + 1) * WTOK],
                                                stack[i.k][rows, 0, g * TILE_HEADS + h, win(t, ww)],
                                                stack[i.k][rows, 1, g * TILE_HEADS + h, win(t, ww)],
                                                start=True, stop=True, skip_group_check=True)
                last.then_inc(max_ready, 1)

            def scores(i, t):
                wait(pe, c_row[i.k], i.dmas(1))
                wait(pe, exp_done, i.count(2, t - 1 + 1) if t else i.plus(-1).count(2))
                rows = slice(0, STACK + MASKS + 1)
                for h in range(HEADS):
                    for ww in range(2):
                        last = nc.tensor.matmul(C[0][WTOK * ww:WTOK * (ww + 1), h * WTOK:(h + 1) * WTOK],
                                                stack[i.k][rows, 1, h, win(t, ww)], stack[i.k][rows, 0, h, win(t, ww)],
                                                start=True, stop=True, skip_group_check=True)
                last.then_inc(s_ready, 1)

            def output(i):
                wait(pe, o_done, i.count(1))
                if i.plus(4).among(images):
                    wait(pe, gn_chain, i.plus(4).count(3, 1))
                wait(pe, z_out, i.plus(-1).count(2))
                for o in range(CT):
                    for ww in range(2):
                        dst = E[:, o * TOKENS:(o + 1) * TOKENS].rearrange("p (t rr ww c) -> p ww t rr c", t=TT, rr=WIN, ww=2)
                        for g in range(QUADS):
                            last = nc.tensor.matmul(dst[:, ww], wop[:, ww, g, o * P:(o + 1) * P],
                                                    ot[:, :, g, :].rearrange("p t (rr c) -> p t rr c", rr=WIN),
                                                    start=(g == 0), stop=(g == QUADS - 1))
                last.then_inc(z_ready, 1)

            def turn(i):
                for t in range(TT):
                    wait(pe, qkn_done, i.count(2, t + 1))
                    for n in range(4):
                        last = nc.tensor.transpose(A[t][:, n * P:(n + 1) * P], qkn[:, t, n * P:(n + 1) * P],
                                                   ident[:, :])
                    last.then_inc(turned, 1)

            def turn_c(i):
                wait(pe, max_done, i.count(4))
                wait(pe, v_out, i.count(2))
                for t in range(TT):
                    last = nc.tensor.transpose(A[2][0:HEADS, t * P:(t + 1) * P], cm[:, t, :], ident[:, :])
                last.then_inc(c_turned, 1)

            def groups(i):
                wait(pe, stats, i.count(4))
                wait(pe, z_out, i.plus(-5).count(2))
                nc.tensor.matmul(E[:, 0:4 * CT], gavg[:, :], bn[:, :, :].rearrange("p c (h s) -> p (c h) s", s=3)[:, :, 1:3],
                                 start=True, stop=True).then_inc(g_ready, 1)

            def M(n):
                return lambda i: maxima(i, n), 1

            pipeline(pe, images, [(weigh, -1), (lambda i: scores(i, 0), 0), (project_v, 1),
                                  (lambda i: scores(i, 1), 0), (output, -1), M(0), M(1), (turn, 2), M(2),
                                  M(3), (groups, 4), (project, 3), (turn_c, 1)], LAGS)

        @block.scalar
        def _(act):
            def square(i):
                wait(act, sum_done, i.plus(-1).count(2))
                for t in range(TT):
                    wait(act, proj_qk, i.count(2, t + 1))
                    nc.scalar.activation(sq[:, t, :], A[t][:], ACT.Square).then_inc(squared, 1)

            def copy_v(i):
                wait(act, proj_v, i.count(1))
                wait(act, pv_done, i.plus(-2).count(1))
                for ww in range(2):
                    rows = slice(ww * WTOK, (ww + 1) * WTOK)
                    nc.scalar.activation(vw[i.k][rows, :, :, ww, :],
                                         A[2][rows, :].rearrange("p (t h e) -> p t h e", t=TT, h=HEADS),
                                         ACT.Copy).then_inc(v_out, 1)

            def exponent(i, t):
                wait(act, s_ready, i.count(2, t + 1))
                wait(act, pv_done, i.plus(-2).count(1))
                nc.scalar.activation(prob[i.k][:, t, :, :].rearrange("p h q -> p (h q)"), C[0][:, :],
                                     ACT.Exp).then_inc(exp_done, 1)

            def copy_z(i):
                wait(act, z_ready, i.count(1))
                wait(act, x1_done, i.plus(-1).count(4))
                for o in range(CT):
                    nc.scalar.activation(zb[:, o, :], E[:, o * TOKENS:(o + 1) * TOKENS], ACT.Identity,
                                         bias=bz[:, o:o + 1]).then_inc(z_out, 1)

            def split_high(i, t):
                wait(act, turned, i.count(2, t + 1))
                if t == 0:
                    wait(act, split_out[1 - i.k], i.plus(-1).dmas(1))
                nc.scalar.activation(tile_parts(0, t), by_kind(A[t]), ACT.Copy).then_inc(high_out, 1)

            def split_middle(i, t):
                wait(act, rest_out, i.count(2, t + 1))
                nc.scalar.activation(tile_parts(1, t), by_tile(rest[t]), ACT.Copy).then_inc(mid_out, 1)

            def copy_c(i):
                wait(act, c_turned, i.count(1))
                wait(act, c_row[i.k], i.plus(-2).dmas(1))
                nc.scalar.activation(ct[i.k][:, :], A[2][0:HEADS, 0:TOKENS], ACT.Copy, scale=-1.0).then_inc(c_out, 1)

            def row_c(i):
                wait(act, c_out, i.count(1))
                wait(act, s_ready, i.plus(-2).count(2))
                act.dma_start(stack[i.k][STACK + MASKS:STACK + MASKS + 1, 0, :, :], ct[i.k][:, :]).then_inc(c_row[i.k], 16)

            def normalize(i):
                wait(act, newton, i.count(NEWTON))
                wait(act, proj_v, i.plus(-2).count(1))
                for c in range(CT):
                    src = X[:, bass.ds(i.index(1), 1), c, :].rearrange("p i (t rr ww c) -> p (i t) rr ww c", t=TT, rr=WIN, ww=2)
                    dst = xh[i.k][:, c, :].rearrange("p (t ww rr c) -> p t rr ww c", t=TT, ww=2, rr=WIN)
                    for ww in range(2):
                        nc.scalar.activation(dst[:, :, :, ww, :], src[:, :, :, ww, :], ACT.Identity,
                                             bias=shift[:, c:c + 1], scale=rs_y[:, 64 + c:65 + c]).then_inc(xh_done, 1)

            pipeline(act, images, [(lambda i: exponent(i, 0), 0), (copy_v, 1), (lambda i: exponent(i, 1), 0),
                                   (normalize, 3), (copy_z, -1), (lambda i: split_high(i, 0), 2),
                                   (lambda i: split_high(i, 1), 2), (lambda i: split_middle(i, 0), 2),
                                   (lambda i: split_middle(i, 1), 2), (square, 3), (copy_c, 1), (row_c, 1)], LAGS)

        @block.vector
        def _(dve):
            def outputs(i):
                wait(dve, sums_done, i.count(QUADS))
                wait(dve, o_done, i.plus(-1).count(1))
                nc.vector.reciprocal(rd[:, :], B[1]).then_inc(r_done, 1)
                wait(dve, pv_done, i.count(1))
                wait(dve, r_done, i.count(1))
                wait(dve, z_ready, i.plus(-1).count(1))
                nc.vector.tensor_tensor(ot[:, :, :, :].rearrange("p t g q -> p (t g q)"), B[0], rd[:, :],
                                        ALU.mult).then_inc(o_done, 1)

            def norms(i):
                wait(dve, newton, i.plus(0).count(NEWTON))
                for t in range(TT):
                    wait(dve, squared, i.count(2, t + 1))
                    nc.vector.reduce_sum(rs[:, 32 * t:32 * t + 32], sq[:, t, :].rearrange("p (h e) -> p h e", e=DIM),
                                         AX_X).then_inc(sum_done, 1)

            def variances(i):
                wait(dve, g_ready, i.count(1))
                wait(dve, newton, i.plus(-1).count(NEWTON))
                nc.vector.reduce_sum(gs[:, :, :], E[:, 0:4 * CT].rearrange("p (c h s) -> p c s h", h=2, s=2),
                                     AX_X).then_inc(gn_chain, 1)
                wait(dve, gn_chain, i.count(3, 1))
                nc.vector.tensor_tensor(gm[:, :], gs[:, :, 0], gs[:, :, 0], ALU.mult).then_inc(gn_chain, 1)
                wait(dve, gn_chain, i.count(3, 2))
                nc.vector.scalar_tensor_tensor(out=rs[:, 64:66], in0=gs[:, :, 1], scalar=EPS, in1=gm[:, :],
                                               op0=ALU.add, op1=ALU.subtract).then_inc(gn_chain, 1)

            def seeds(i):
                wait(dve, sum_done, i.plus(-1).count(2))
                if i.among(images):
                    wait(dve, gn_chain, i.count(3))
                wait(dve, xh_done, i.plus(-1).count(4))
                wait(dve, qkn_done, i.plus(-2).count(2))
                nc.vector.tensor_scalar(rs[:, :], rs[:, :], NORM_MIN * NORM_MIN, None, ALU.max).then_inc(rs_ready, 1)
                wait(dve, rs_ready, i.count(3, 1))
                nc.vector.tensor_scalar(rs_bits[:, :], rs[:, :].bitcast(I32), 1, None,
                                        ALU.logical_shift_right).then_inc(rs_ready, 1)
                wait(dve, rs_ready, i.count(3, 2))
                nc.vector.tensor_scalar(rs_y[:, :].bitcast(I32), rs_bits[:, :], -1.0, RSQRT_SEED, ALU.mult,
                                        ALU.add).then_inc(rs_ready, 1)

            def roots(i):
                wait(dve, rs_ready, i.count(3))
                for step in range(3):
                    if step:
                        wait(dve, newton, i.count(NEWTON, 3 * step))
                    nc.vector.scalar_tensor_tensor(out=rs_t[:, :], in0=rs_y[:, :], scalar=-0.5, in1=rs_y[:, :],
                                                   op0=ALU.mult, op1=ALU.mult).then_inc(newton, 1)
                    wait(dve, newton, i.count(NEWTON, 3 * step + 1))
                    nc.vector.tensor_tensor(rs_t[:, :], rs_t[:, :], rs[:, :], ALU.mult).then_inc(newton, 1)
                    wait(dve, newton, i.count(NEWTON, 3 * step + 2))
                    nc.vector.scalar_tensor_tensor(out=rs_y[:, :], in0=rs_t[:, :], scalar=1.5, in1=rs_y[:, :],
                                                   op0=ALU.add, op1=ALU.mult).then_inc(newton, 1)
                wait(dve, newton, i.count(NEWTON, 9))
                q_part = rs_y[:, 0:64].rearrange("p (t n h) -> p t n h", t=TT, n=2)[:, :, 0, :]
                nc.vector.tensor_tensor(q_part, q_part, scale[:, :].unsqueeze(1).to_broadcast([P, TT, HEADS]),
                                        ALU.mult).then_inc(newton, 1)
                nc.vector.scalar_tensor_tensor(out=shift[:, :], in0=gs[:, :, 0], scalar=-1.0, in1=rs_y[:, 64:66],
                                               op0=ALU.mult, op1=ALU.mult).then_inc(newton, 1)

            def take_max(i, n):
                t, g = divmod(n, CT)
                wait(dve, max_ready, i.count(4, n + 1))
                if n == 0:
                    wait(dve, c_turned, i.plus(-1).count(1))
                nc.vector.reduce_max(cm[:, t, g * TILE_HEADS:(g + 1) * TILE_HEADS],
                                     B[n % 2].rearrange("p (h k) -> p h k", k=WTOK), AX_X).then_inc(max_done, 1)

            def unit_qk(i):
                wait(dve, newton, i.plus(1).count(NEWTON))
                wait(dve, turned, i.plus(-1).count(2))
                for t in range(TT):
                    nc.vector.tensor_tensor(qkn[:, t, :].rearrange("p (h e) -> p h e", e=DIM),
                                            A[t][:].rearrange("p (h e) -> p h e", e=DIM),
                                            rs_y[:, 32 * t:32 * t + 32].unsqueeze(2).to_broadcast([P, 32, DIM]),
                                            ALU.mult).then_inc(qkn_done, 1)

            def stats_next(i):
                wait_alone(dve, x1_done, i.count(4))
                for c in range(CT):
                    nc.vector.bn_stats(stats2[:, bass.ds(i.index(), 1), c, :].rearrange("p i s -> p (i s)"),
                                       X[:, bass.ds(i.index(), 1), c, :].rearrange("p i t -> p (i t)"))

            def take_high(i, t):
                wait(dve, high_out, i.count(2, t + 1))
                wait(dve, low_out, i.plus(-1).count(2, t + 1))
                nc.vector.tensor_tensor(by_tile(rest[t]), by_kind(A[t]), tile_parts(0, t), ALU.subtract).then_inc(rest_out, 1)

            def stats_first(i):
                wait_alone(dve, x_in[i.k], i.dmas(1))
                wait_alone(dve, g_ready, i.plus(-1).count(1))
                for c in range(CT):
                    nc.vector.bn_stats(bn[:, c, :], X[:, bass.ds(i.index(1), 1), c, :]
                                       .rearrange("p i t -> p (i t)")).then_inc(stats, 1)
                half = bn[:, :, :].rearrange("p c (h s) -> p (c h) s", s=3)
                wait(dve, stats, i.count(4, 2))
                nc.vector.tensor_tensor(mm[:, :], half[:, :, 1], half[:, :, 1], ALU.mult).then_inc(stats, 1)
                wait(dve, stats, i.count(4, 3))
                nc.vector.scalar_tensor_tensor(out=half[:, :, 2], in0=half[:, :, 2], scalar=2.0 / TOKENS, in1=mm[:, :],
                                               op0=ALU.mult, op1=ALU.add).then_inc(stats, 1)

            def R(n):
                return lambda i: take_max(i, n), 1

            pipeline(dve, images, [(variances, 3), (norms, 2), (outputs, -1), (seeds, 3, 1), (roots, 3, 1), (unit_qk, 2),
                                   (stats_first, 4), R(0), R(1), (lambda i: take_high(i, 0), 2),
                                   (lambda i: take_high(i, 1), 2), R(2), R(3), (stats_next, -1)], LAGS)

        @block.gpsimd
        def _(pool):
            def add_bias(i, t):
                wait(pool, exp_done, i.count(2, t + 1))
                both = prob[i.k][:, t, :, :]
                nc.gpsimd.tensor_tensor(both, both, ebias[:, :, :], ALU.mult).then_inc(biased, 1)

            def residual(i):
                wait(pool, z_out, i.count(2))
                for r0, rn, rd_ in ((0, 12, 4), (12, 4, 0)):
                    for c0, cn, cd in ((0, 12, 4), (12, 4, 0)):
                        def part(ap, row, c):
                            return ap.rearrange("p c (i j) -> p c i j", j=SIDE)[:, :, row:row + rn, c:c + cn]
                        old = X[:, bass.ds(i.index(1), 1), :, :].rearrange("p i c t -> p (i c) t")
                        new = X[:, bass.ds(i.index(), 1), :, :].rearrange("p i c t -> p (i c) t")
                        nc.gpsimd.tensor_tensor(part(new, rd_, cd), part(old, r0, c0), part(zb[:, :, :], r0, c0),
                                                ALU.add).then_inc(x1_done, 1)

            def split_low(i, t):
                wait(pool, mid_out, i.count(2, t + 1))
                if t == 0:
                    wait(pool, split_out[1 - i.k], i.plus(-1).dmas(1))
                nc.gpsimd.tensor_tensor(tile_parts(2, t), by_tile(rest[t]), tile_parts(1, t), ALU.subtract).then_inc(low_out, 1)

            pipeline(pool, images, [(lambda i: add_bias(i, 0), 0), (lambda i: add_bias(i, 1), 0), (residual, -1),
                                    (lambda i: split_low(i, 0), 2), (lambda i: split_low(i, 1), 2)], LAGS)


class Part:

    def __init__(self, block, head, heads, start, size):
        self.block, self.head, self.heads, self.start, self.size = block, head, heads, start, size
        self.cols = slice(start, start + size)
        self.which = slice(head, head + heads)
        self.tile = head // TILE_HEADS
        self.ahead = self.tile == 1
        self.diagonal = block * P - start


SCORES = ([Part(0, h, 2, 0, TOKENS) for h in range(0, 8, 2)] + [Part(1, h, 4, P, P) for h in range(0, 8, 4)]
          + [Part(0, h, 4, 0, P) for h in range(8, 16, 4)] + [Part(1, h, 2, 0, TOKENS) for h in range(8, 16, 2)])
MAXIMA = ([Part(0, h, 4, 0, P) for h in range(0, 8, 4)] + [Part(1, h, 2, 0, TOKENS) for h in range(0, 8, 2)]
          + [Part(0, h, 2, 0, TOKENS) for h in range(8, 16, 2)] + [Part(1, h, 4, P, P) for h in range(8, 16, 4)])
ROUNDS = len(SCORES) // 2


def layer1(nc, ctx, images, out, given, scratch, X, stats2, probs, xh, parts, rest, stack, split_parts, ident, gavg, A, C, E):
    def sb(name, shape, dt=F32):
        return ctx.enter_context(nc.sbuf_tensor(name, shape, dt))

    def sem(name):
        return ctx.enter_context(nc.semaphore(name))

    def by_tile(ap):
        return ap[:, :].rearrange("p (t n) -> p t n", t=CT)

    wqk = sb("wqk1", [P, CT, 2 * CH])
    wv = sb("wv1", [P, CT, CH])
    wo = sb("wo1", [P, CT, CH])
    identb = sb("identb", [P, P], BF16)
    below = sb("below", [P, P], BF16)
    above = sb("above", [P, P], BF16)
    cm = sb("cm1", [P, TT, HEADS])
    ct = [sb(f"ct1{k}", [HEADS, TOKENS], BF16) for k in range(2)]
    va = [sb(f"va{k}", [P, TT, HEADS, COL]) for k in range(2)]
    ots = sb("ots", [P, QUADS, TOKENS])
    rdn = sb("rdn", [P, TT * HEADS])
    on = sb("on", [P, TT, CH])
    rows = sb("rows", [P, TT, CH])
    of = sb("of", [P, CT, TOKENS])
    n_stat = images * CT
    gs = probs[0][:, 0:2 * n_stat].rearrange("p (n s) -> p n s", s=2)
    gm, rs, rs_half, rs_t = (probs[0][:, (2 + n) * n_stat:(3 + n) * n_stat] for n in range(4))
    rs_bits = probs[0][:, 6 * n_stat:7 * n_stat].bitcast(I32)
    mm = probs[0][:, 7 * n_stat:9 * n_stat]
    rs_y = sb("rs1_y", [P, images, CT])
    shift = sb("shift1", [P, images, CT])
    flat_y = rs_y[:, :, :].rearrange("p i c -> p (i c)")

    c_in, z_in, sum_in, g_ready, var, newton = (sem(n) for n in ("c_in1", "z_in1", "sum_in", "g_ready1", "var1", "newton1"))
    loads = [(wqk, given["wqk1"]), (wv, given["wv1"]), (wo, given["wo1"]), (identb, given["identb"]), (below, given["below"]),
             (above, given["above"])]
    with nc.Block() as block:
        @block.sync
        def _(sp):
            for dst, src in loads:
                sp.dma_start(dst[:], src).then_inc(c_in, 16)
            for k in range(2):
                sp.dma_start(stack[k][STACK:STACK + 1, 1, :, :],
                             stack[k][STACK + MASKS:STACK + MASKS + 1, 1, :, :]).then_inc(c_in, 16)
            sp.wait_ge(c_in, 16 * (len(loads) + 2))

        @block.vector
        def _(dve):
            half = stats2[:, :, :, :].rearrange("p i c (h s) -> p (i c h) s", s=3)
            nc.vector.tensor_tensor(mm, half[:, :, 1], half[:, :, 1], ALU.mult).then_inc(var, 1)
            dve.wait_ge(var, 1)
            nc.vector.scalar_tensor_tensor(out=half[:, :, 2], in0=half[:, :, 2], scalar=2.0 / TOKENS, in1=mm,
                                           op0=ALU.mult, op1=ALU.add).then_inc(sum_in, 1)
            dve.wait_ge(g_ready, 1)
            nc.vector.reduce_sum(gs[:, :, :], E[:, 0:4 * n_stat].rearrange("p (n h s) -> p n s h", h=2, s=2),
                                 AX_X).then_inc(var, 1)
            dve.wait_ge(var, 2)
            nc.vector.tensor_tensor(gm[:, :], gs[:, :, 0], gs[:, :, 0], ALU.mult).then_inc(var, 1)
            dve.wait_ge(var, 3)
            nc.vector.scalar_tensor_tensor(out=rs[:, :], in0=gs[:, :, 1], scalar=EPS, in1=gm[:, :],
                                           op0=ALU.add, op1=ALU.subtract).then_inc(var, 1)
            dve.wait_ge(var, 4)
            nc.vector.tensor_scalar(rs_half[:, :], rs[:, :], -0.5, None, ALU.mult).then_inc(var, 1)
            nc.vector.tensor_scalar(rs_bits[:, :], rs[:, :].bitcast(I32), 1, None,
                                    ALU.logical_shift_right).then_inc(var, 1)
            dve.wait_ge(var, 6)
            nc.vector.tensor_scalar(flat_y.bitcast(I32), rs_bits[:, :], -1.0, RSQRT_SEED, ALU.mult,
                                    ALU.add).then_inc(var, 1)
            dve.wait_ge(var, 7)
            for step in range(3):
                nc.vector.tensor_tensor(rs_t[:, :], flat_y, flat_y, ALU.mult).then_inc(newton, 1)
                dve.wait_ge(newton, 3 * step + 1)
                nc.vector.tensor_tensor(rs_t[:, :], rs_t[:, :], rs_half[:, :], ALU.mult).then_inc(newton, 1)
                dve.wait_ge(newton, 3 * step + 2)
                nc.vector.scalar_tensor_tensor(out=flat_y, in0=rs_t[:, :], scalar=1.5, in1=flat_y,
                                               op0=ALU.add, op1=ALU.mult).then_inc(newton, 1)
                dve.wait_ge(newton, 3 * step + 3)
            nc.vector.scalar_tensor_tensor(out=shift[:, :, :].rearrange("p i c -> p (i c)"), in0=gs[:, :, 0],
                                           scalar=-1.0, in1=flat_y, op0=ALU.mult, op1=ALU.mult).then_inc(newton, 1)
            dve.wait_ge(newton, 10)

        @block.tensor
        def _(pe):
            pe.wait_ge(sum_in, 1)
            nc.tensor.matmul(E[:, 0:4 * n_stat], gavg[:, :],
                             stats2[:, :, :, :].rearrange("p i c (h s) -> p (i c h) s", s=3)[:, :, 1:3],
                             start=True, stop=True).then_inc(g_ready, 1)

        @block.gpsimd
        def _(pool):
            for k in range(2):
                nc.gpsimd.memset(va[k][:], 0.0).then_inc(z_in, 1)
            pool.wait_ge(z_in, 2)
            for k in range(2):
                nc.gpsimd.memset(va[k][:, :, :, DIM:DIM + 1], 1.0).then_inc(z_in, 1)
            pool.wait_ge(z_in, 4)

    split_out, stacked, c_row, stored, loaded, y_out = (
        [sem(f"{n}{k}") for k in range(2)] for n in ("l1_split_out", "l1_stacked", "l1_c_row", "stored", "loaded", "y_out"))
    pv_done, proj_q, proj_k, proj_v, max_ready, s_ready, turned, c_turned, f_turned, z_ready = (
        sem("l1_" + n) for n in ("pv_done", "proj_q", "proj_k", "proj_v", "max_ready", "s_ready", "turned", "c_turned",
                                 "f_turned", "z_ready"))
    exp_done, ot_out, f_out, v_out, high_out, mid_out, c_out, xh_done = (
        sem("l1_" + n) for n in ("exp_done", "ot_out", "f_out", "v_out", "high_out", "mid_out", "c_out", "xh_done"))
    max_done, y_done, rest_out, low_out, r_done, on_done = (
        sem("l1_" + n) for n in ("max_done", "y_done", "rest_out", "low_out", "r_done", "on_done"))
    LAGS = (-2, 3)

    with nc.Block() as block:
        @block.sync
        def _(sp):
            def keep_split(i):
                wait_alone(sp, low_out, i.count(2))
                wait_alone(sp, stacked[i.k], i.plus(-2).dmas(STACK_DMAS))
                keep_parts(sp, i, parts, split_parts, split_out)

            def stack_up(i):
                wait_alone(sp, split_out[i.k], i.dmas(1))
                wait_alone(sp, s_ready, i.plus(-2).count(ROUNDS))
                stack_parts(sp, i, split_parts, stack, stacked)

            def regroup(i):
                wait_alone(sp, on_done, i.count(1))
                wait_alone(sp, loaded[i.k], i.plus(-2).dmas(1))
                for t in range(TT):
                    sp.dma_start(scratch[i.k, :, t * P:(t + 1) * P, :].rearrange("h p e -> p h e"),
                                 on[:, t, :].rearrange("p (h e) -> p h e", h=HEADS)).then_inc(stored[i.k], 16)

            def fetch(i):
                wait_alone(sp, stored[i.k], i.dmas(TT))
                wait_alone(sp, f_turned, i.plus(-1).count(1))
                sp.dma_start(rows[:, :, :],
                             scratch[i.k].rearrange("h n e -> (h n e)").rearrange("(t p f) -> p t f", p=P, f=CH)
                             ).then_inc(loaded[i.k], 16)

            def store(i):
                wait_alone(sp, y_done, i.count(1))
                wait_alone(sp, y_out[i.k], i.plus(-2).dmas(1))
                sp.dma_start(out.rearrange("(c p) i t -> p c i t", p=P)[:, :, bass.ds(i.index(), 1), :]
                             .rearrange("p c i t -> p c (i t)"),
                             X[:, bass.ds(i.index(), 1), :, :].rearrange("p i c t -> p c (i t)")).then_inc(y_out[i.k], 16)

            pipeline(sp, images, [(keep_split, 2), (stack_up, 2), (store, -2), (regroup, -1), (fetch, -1)], LAGS)
            for k in range(2):
                sp.wait_ge(y_out[k], 16 * ((images + 1 - k) // 2))

        @block.tensor
        def _(pe):
            def scores(i, rnd):
                if rnd == 0:
                    wait(pe, c_row[i.k], i.dmas(1))
                    wait(pe, exp_done, i.plus(-1).count(ROUNDS))
                    wait(pe, on_done, i.plus(-2).count(1))
                else:
                    wait(pe, exp_done, i.count(ROUNDS, rnd))
                for b in range(2):
                    s = SCORES[2 * rnd + b]
                    bank = C[0][:, b * 512:(b + 1) * 512].rearrange("p (h q) -> p h q", h=s.heads)
                    for n in range(s.heads):
                        nc.tensor.matmul(bank[:, n, :], stack[i.k][0:STACK + 1, 1, s.head + n, s.block * P:(s.block + 1) * P],
                                         stack[i.k][0:STACK + 1, 0, s.head + n, s.cols], start=(n == 0), stop=False,
                                         skip_group_check=True)
                    mask = (above if s.ahead else below)[:, :].unsqueeze(1).to_broadcast([P, s.heads, P])
                    last = nc.tensor.matmul(bank[:, :, s.diagonal:s.diagonal + P], identb[:, :], mask,
                                            start=False, stop=True, skip_group_check=True)
                last.then_inc(s_ready, 1)

            def maxima(i, rnd):
                if rnd == 0:
                    wait(pe, stacked[i.k], i.dmas(STACK_DMAS))
                    wait(pe, max_done, i.plus(-1).count(ROUNDS))
                else:
                    wait(pe, max_done, i.count(ROUNDS, rnd))
                for b in range(2):
                    s = MAXIMA[2 * rnd + b]
                    bank = C[1][:, b * 512:(b + 1) * 512].rearrange("p (h k) -> p h k", h=s.heads)
                    for n in range(s.heads):
                        nc.tensor.matmul(bank[:, n, :], stack[i.k][0:STACK, 0, s.head + n, s.block * P:(s.block + 1) * P],
                                         stack[i.k][0:STACK, 1, s.head + n, s.cols], start=(n == 0), stop=False,
                                         skip_group_check=True)
                    mask = (below if s.ahead else above)[:, :].unsqueeze(1).to_broadcast([P, s.heads, P])
                    last = nc.tensor.matmul(bank[:, :, s.diagonal:s.diagonal + P], identb[:, :], mask,
                                            start=False, stop=True, skip_group_check=True)
                last.then_inc(max_ready, 1)

            def weigh(i, g):
                if g == 0:
                    wait(pe, exp_done, i.count(ROUNDS))
                    wait(pe, v_out, i.count(1))
                    wait(pe, ot_out, i.plus(-1).count(2))
                if g % 2 == 0:
                    n = g // 2
                    if i.plus(2 + n).among(images):
                        wait(pe, rest_out, i.plus(2 + n).count(2, n + 1))
                for part in range(2):
                    for c in range(QUADS):
                        h = g * QUADS + c
                        block = part if g < 2 else 1 - part
                        n = next(n for n, s in enumerate(SCORES) if s.block == block and s.head <= h < s.head + s.heads)
                        s = SCORES[n]
                        at = 512 * n + (h - s.head) * s.size
                        to = (g % 2) * TOKENS + s.start
                        last = nc.tensor.matmul(A[g // 2][COL * c:COL * (c + 1), to:to + s.size], va[i.k][:, block, h, :],
                                                probs[i.k][:, at:at + s.size], start=(part == 0), stop=(part == 1),
                                                tile_position=(0, COL * c), skip_group_check=True)
                last.then_inc(pv_done, 1)

            def project_qk(i, n):
                if n == 0:
                    wait(pe, xh_done, i.count(2))
                wait(pe, ot_out, i.plus(-3 - n).count(2, n + 1))
                if n == 0:
                    wait(pe, rest_out, i.plus(-1).count(2))
                for o in range(CT):
                    for c in range(CT):
                        last = nc.tensor.matmul(A[n][:, o * TOKENS:(o + 1) * TOKENS],
                                                wqk[:, c, n * CH + o * P:n * CH + (o + 1) * P], xh[i.k][:, c, :],
                                                start=(c == 0), stop=(c == CT - 1))
                last.then_inc(proj_k if n else proj_q, 1)

            def project_v(i):
                wait(pe, xh_done, i.count(2))
                wait(pe, v_out, i.plus(-1).count(1))
                for t in range(TT):
                    for c in range(CT):
                        last = nc.tensor.matmul(A[2][:, t * CH:(t + 1) * CH], xh[i.k][:, c, t * P:(t + 1) * P],
                                                wv[:, c, :], start=(c == 0), stop=(c == CT - 1))
                last.then_inc(proj_v, 1)

            def turn_c(i):
                wait(pe, max_done, i.count(ROUNDS))
                wait(pe, y_done, i.plus(-3).count(1))
                for t in range(TT):
                    last = nc.tensor.transpose(E[0:HEADS, t * P:(t + 1) * P], cm[:, t, :], ident[:, :])
                last.then_inc(c_turned, 1)

            def turn(i):
                wait(pe, ot_out, i.count(2))
                wait(pe, on_done, i.plus(-1).count(1))
                if i.plus(1).among(images):
                    wait(pe, exp_done, i.plus(1).count(ROUNDS))
                for t in range(TT):
                    for g in range(QUADS):
                        last = nc.tensor.transpose(C[0][:, t * 512 + g * P:t * 512 + (g + 1) * P],
                                                   ots[:, g, t * P:(t + 1) * P], ident[:, :])
                last.then_inc(turned, 1)

            def turn_rows(i):
                wait(pe, loaded[i.k], i.dmas(1))
                wait(pe, y_done, i.plus(-1).count(1))
                if i.plus(2).among(images):
                    wait(pe, c_out, i.plus(2).count(1))
                for t in range(TT):
                    for f in range(CT):
                        last = nc.tensor.transpose(E[:, f * TOKENS + t * P:f * TOKENS + (t + 1) * P],
                                                   rows[:, t, f * P:(f + 1) * P], ident[:, :])
                last.then_inc(f_turned, 1)

            def output(i):
                wait(pe, f_out, i.count(1))
                for o in range(CT):
                    for f in range(CT):
                        last = nc.tensor.matmul(E[:, o * TOKENS:(o + 1) * TOKENS], wo[:, f, o * P:(o + 1) * P],
                                                of[:, f, :], start=(f == 0), stop=(f == CT - 1))
                last.then_inc(z_ready, 1)

            def S(rnd):
                return lambda i: scores(i, rnd), 0

            def M(rnd):
                return lambda i: maxima(i, rnd), 1

            def W(g):
                return lambda i: weigh(i, g), -1

            pipeline(pe, images, [W(0), W(1), S(0), (lambda i: project_qk(i, 0), 2), S(1), (lambda i: project_qk(i, 1), 2),
                                  S(2), M(0), S(3), W(2), M(1), S(4), W(3), M(2), S(5), (turn_rows, -2), M(3),
                                  (output, -2), M(4), (turn, -1), M(5), (turn_c, 1), (project_v, 1)], LAGS)

        @block.scalar
        def _(act):
            def exponent(i, rnd):
                wait(act, s_ready, i.count(ROUNDS, rnd + 1))
                if rnd == 0:
                    wait(act, pv_done, i.plus(-2).count(QUADS))
                nc.scalar.activation(probs[i.k][:, rnd * 1024:(rnd + 1) * 1024], C[0][:, :], ACT.Exp).then_inc(exp_done, 1)

            def copy_outputs(i, n):
                wait(act, pv_done, i.count(QUADS, 2 * n + 2))
                wait(act, turned, i.plus(-1).count(1))
                nc.scalar.activation(ots[:, 2 * n:2 * n + 2, :].rearrange("p g q -> p (g q)"), A[n][:, :],
                                     ACT.Copy).then_inc(ot_out, 1)

            def copy_rows(i):
                wait(act, f_turned, i.count(1))
                wait(act, z_ready, i.plus(-1).count(1))
                nc.scalar.activation(of[:, :, :].rearrange("p f t -> p (f t)"), E[:, :], ACT.Copy).then_inc(f_out, 1)

            def copy_v(i):
                wait(act, proj_v, i.count(1))
                wait(act, pv_done, i.plus(-2).count(QUADS))
                nc.scalar.activation(va[i.k][:, :, :, 0:DIM].rearrange("p t h e -> p (t h) e"),
                                     A[2][:, :].rearrange("p (n e) -> p n e", e=DIM), ACT.Copy).then_inc(v_out, 1)

            def split_high(i, n):
                wait(act, proj_k if n else proj_q, i.count(1))
                if n == 0:
                    wait(act, split_out[1 - i.k], i.plus(-1).dmas(1))
                nc.scalar.activation(parts[:, :, 0, n, :], by_tile(A[n]), ACT.Copy,
                                     scale=1.0 if n else DIM ** -0.5).then_inc(high_out, 1)

            def split_middle(i, n):
                wait(act, rest_out, i.count(2, n + 1))
                nc.scalar.activation(parts[:, :, 1, n, :], by_tile(rest[n]), ACT.Copy).then_inc(mid_out, 1)

            def copy_c(i):
                wait(act, c_turned, i.count(1))
                wait(act, c_row[i.k], i.plus(-2).dmas(1))
                nc.scalar.activation(ct[i.k][:, :], E[0:HEADS, 0:TOKENS], ACT.Copy, scale=-1.0).then_inc(c_out, 1)

            def row_c(i):
                wait(act, c_out, i.count(1))
                wait(act, s_ready, i.plus(-2).count(ROUNDS))
                act.dma_start(stack[i.k][STACK:STACK + 1, 0, :, :], ct[i.k][:, :]).then_inc(c_row[i.k], 16)

            def normalize(i):
                wait(act, proj_v, i.plus(-2).count(1))
                wait(act, proj_k, i.plus(-2).count(1))
                for c in range(CT):
                    nc.scalar.activation(xh[i.k][:, c, :], X[:, bass.ds(i.index(), 1), c, :].rearrange("p i t -> p (i t)"),
                                         ACT.Identity,
                                         bias=shift[:, bass.ds(i.index(), 1), c],
                                         scale=rs_y[:, bass.ds(i.index(), 1), c]).then_inc(xh_done, 1)

            def X_(rnd):
                return lambda i: exponent(i, rnd), 0

            pipeline(act, images, [(lambda i: copy_outputs(i, 0), -1), X_(0), (lambda i: split_high(i, 0), 2), X_(1),
                                   (lambda i: split_high(i, 1), 2), X_(2), (lambda i: split_middle(i, 0), 2), X_(3),
                                   (lambda i: split_middle(i, 1), 2), X_(4), (lambda i: copy_outputs(i, 1), -1), X_(5),
                                   (copy_rows, -2), (copy_c, 1), (row_c, 1), (normalize, 3), (copy_v, 1)], LAGS)

        @block.vector
        def _(dve):
            def take_max(i, rnd):
                s = MAXIMA[2 * rnd]
                wait(dve, max_ready, i.count(ROUNDS, rnd + 1))
                if rnd == 0:
                    wait(dve, c_turned, i.plus(-1).count(1))
                nc.vector.reduce_max(cm[:, s.block, s.head:s.head + 2 * s.heads],
                                     C[1][:, :].rearrange("p (h k) -> p h k", k=s.size), AX_X).then_inc(max_done, 1)

            def residual(i):
                wait(dve, z_ready, i.count(1))
                x = X[:, bass.ds(i.index(), 1), :, :].rearrange("p i c t -> p (i c t)")
                nc.vector.tensor_tensor(x, E[:, :], x, ALU.add).then_inc(y_done, 1)

            def take_high(i, n):
                wait(dve, high_out, i.count(2, n + 1))
                wait(dve, low_out, i.plus(-1).count(2, n + 1))
                nc.vector.scalar_tensor_tensor(out=by_tile(rest[n]), in0=by_tile(A[n]), scalar=1.0 if n else DIM ** -0.5,
                                               in1=parts[:, :, 0, n, :], op0=ALU.mult,
                                               op1=ALU.subtract).then_inc(rest_out, 1)

            def divide(i):
                wait(dve, turned, i.count(1))
                wait(dve, stored[1 - i.k], i.plus(-1).dmas(TT))
                heads = C[0][:, :].rearrange("p (n e) -> p n e", e=COL)
                nc.vector.reciprocal(rdn[:, :], heads[:, :, DIM]).then_inc(r_done, 1)
                wait(dve, r_done, i.count(1))
                nc.vector.tensor_tensor(on[:, :, :].rearrange("p t (h e) -> p (t h) e", e=DIM), heads[:, :, 0:DIM],
                                        rdn[:, :].unsqueeze(2).to_broadcast([P, TT * HEADS, DIM]),
                                        ALU.mult).then_inc(on_done, 1)

            def R(rnd):
                return lambda i: take_max(i, rnd), 1

            pipeline(dve, images, [(lambda i: take_high(i, 0), 2), (lambda i: take_high(i, 1), 2), R(0), R(1), R(2), R(3),
                                   (residual, -2), R(4), (divide, -1), R(5)], LAGS)

        @block.gpsimd
        def _(pool):
            def split_low(i, n):
                wait(pool, mid_out, i.count(2, n + 1))
                if n == 0:
                    wait(pool, split_out[1 - i.k], i.plus(-1).dmas(1))
                nc.gpsimd.tensor_tensor(parts[:, :, 2, n, :], by_tile(rest[n]), parts[:, :, 1, n, :],
                                        ALU.subtract).then_inc(low_out, 1)

            pipeline(pool, images, [(lambda i: split_low(i, 0), 2), (lambda i: split_low(i, 1), 2)], LAGS)


def lay_out(x, L0_conv_Wq, L0_conv_Wk, L0_conv_Wv, L0_conv_bv, L0_conv_Wo, L0_conv_bo, L0_conv_logit_scale,
            L0_conv_cpb_w1, L0_conv_cpb_b1, L0_conv_cpb_w2, L1_conv_Wq_lb, L1_conv_Wk_lb, L1_conv_Wv_lb,
            L1_conv_Wq_la, L1_conv_Wk_la, L1_conv_Wv_la, L1_conv_Wo):
    bfloat16 = mybir.dt.np(BF16)

    def rows(*weights):
        t = np.concatenate([np.asarray(a).reshape(-1, CH).T for a in weights], axis=1)
        return t.reshape(CT, P, -1).transpose(1, 0, 2)

    def column(a):
        return np.asarray(a).reshape(CT, P).T

    images = x.shape[0]
    rolled = np.roll(np.asarray(x), (-SHIFT, -SHIFT), axis=(1, 2)).reshape(images, TOKENS, CH)
    wo = rows(L0_conv_Wo)
    by_head = np.asarray(L0_conv_Wo).T.reshape(QUADS, QUADS, DIM, CH)
    wop = np.zeros((QUADS, 2, DIM, 2, QUADS, CH), wo.dtype)
    for ww in range(2):
        wop[:, ww, :, ww] = by_head.transpose(1, 2, 0, 3)
    queries, keys = window_rows()
    aux = np.zeros((MASKS + 1, 2, HEADS, TOKENS), np.float32)
    aux[0:MASKS, 0], aux[0:MASKS, 1], aux[MASKS, 1] = queries[:, None, :], keys[:, None, :], 1.0
    ones_win = np.zeros((2, WTOK, 2, DIM), np.float32)
    for ww in range(2):
        ones_win[ww, :, ww] = 1.0
    return {
        "xr": rolled.transpose(2, 0, 1),
        "wqk0": rows(L0_conv_Wq, L0_conv_Wk), "wv0": rows(L0_conv_Wv), "wo0": wo,
        "wop0": wop.reshape(P, 2, QUADS, CH), "bv0": column(L0_conv_bv), "bo0": column(L0_conv_bo),
        "scale0": np.broadcast_to(np.asarray(L0_conv_logit_scale).reshape(1, HEADS), (P, HEADS)),
        "cpb_w1": np.asarray(L0_conv_cpb_w1).T, "cpb_b1": np.asarray(L0_conv_cpb_b1).reshape(HIDDEN, 1),
        "cpb_w2": np.asarray(L0_conv_cpb_w2).T, "points": relative_points(),
        "ident": np.eye(P, dtype=np.float32),
        "gavg": np.kron(np.eye(P // GROUP), np.full((GROUP, GROUP), 0.5 / GROUP)).astype(np.float32),
        "ones_win": ones_win.reshape(P, COL),
        "aux": aux.astype(bfloat16),
        "wqk1": rows(L1_conv_Wq_lb, L1_conv_Wq_la, L1_conv_Wk_lb, L1_conv_Wk_la),
        "wv1": rows(L1_conv_Wv_lb, L1_conv_Wv_la), "wo1": rows(L1_conv_Wo),
        "identb": np.eye(P).astype(bfloat16),
        "below": (np.tril(np.ones((P, P)), -1) * MASKED).astype(bfloat16),
        "above": (np.triu(np.ones((P, P)), 1) * MASKED).astype(bfloat16),
    }


def kernel(**inputs):
    import concourse.bacc as bacc
    from concourse.bass_utils import run_bass_kernel_spmd

    arrays = {"in_" + n: np.ascontiguousarray(a) for n, a in lay_out(**inputs).items()}
    images = inputs["x"].shape[0]
    nc = bacc.Bacc("TRN2", target_bir_lowering=False, num_devices=1)
    ins = {n[3:]: nc.dram_tensor(n, a.shape, mybir.dt.from_np(a.dtype), kind="ExternalInput").ap()
           for n, a in arrays.items()}
    out = nc.dram_tensor("out", (CH, images, TOKENS), F32, kind="ExternalOutput").ap()
    build_network(nc, ins.pop("xr"), out, ins)
    got = run_bass_kernel_spmd(nc, [arrays], core_ids=[0]).results[0]["out"]
    return np.ascontiguousarray(got.transpose(1, 2, 0)).reshape(images, SIDE, SIDE, CH)
```

```python
import math
from contextlib import ExitStack

import numpy as np

import concourse.bass as bass
from concourse import mybir

F32 = mybir.dt.float32
BF16 = mybir.dt.bfloat16
I32 = mybir.dt.int32
ALU = mybir.AluOpType
ACT = mybir.ActivationFunctionType
AX_X = mybir.AxisListType.X

P = 128
SIDE = 16
TOKENS = SIDE * SIDE
WIN = 8
WTOK = WIN * WIN
HALF = WTOK // 2
SHIFT = 4
CH = 256
CT = CH // P
HEADS = 16
DIM = CH // HEADS
TILE_HEADS = P // DIM
GROUP = CH // 32
TT = TOKENS // P
COL = 32
QUADS = P // COL
HIDDEN = 128
PARTS = 3
PART_OF_Q = (0, 0, 0, 1, 1, 2)
PART_OF_K = (0, 1, 2, 0, 1, 0)
STACK = len(PART_OF_Q) * DIM
STACK_DMAS = 2 * len(PART_OF_Q)
MASKS = 4
LOG100 = math.log(100.0)
EPS = 1e-5
NORM_MIN = 1e-12
MASKED = -1e30
RSQRT_SEED = 1597463007.0


class Image:

    def __init__(self, pair, offset):
        self.pair, self.offset = pair, offset
        self.k = offset % 2

    def plus(self, n):
        return Image(self.pair, self.offset + n)

    def among(self, images):
        return not isinstance(self.pair, int) or self.pair * 2 + self.offset < images

    def index(self, n=0):
        return self.pair * 2 + (self.offset + n)

    def count(self, per, n=None):
        return self.pair * (2 * per) + (self.offset * per + (per if n is None else n))

    def dmas(self, n):
        return self.pair * (16 * n) + 16 * n * (self.offset // 2 + 1)


def wait(eng, sem, value):
    if not (isinstance(value, int) and value <= 0):
        eng.wait_ge(sem, value)


def wait_alone(eng, sem, value):
    if not (isinstance(value, int) and value <= 0):
        eng.wait_ge(sem, value)
        if not isinstance(value, int):
            eng.nop(nofuse=True)


def pipeline(eng, images, stages, lags, once=(None, None)):
    low, high = lags
    first_pair = (2 - low + 1) // 2
    last_pair = (images - 1 - high - 1) // 2
    pairs = range(first_pair, last_pair + 1)

    def step(s):
        if s == once[0]:
            once[1]()
        for stage, lag, *past in stages:
            if 0 <= s + lag < images + len(past):
                stage(Image(0, s + lag))

    if len(pairs) < 2:
        for s in range(-high, images - low):
            step(s)
        return
    for s in range(-high, 2 * pairs[0]):
        step(s)
    with eng.Fori(pairs[0], pairs[-1] + 1) as pair:
        for k in range(2):
            for stage, lag, *_ in stages:
                stage(Image(pair, k + lag))
    for s in range(2 * pairs[-1] + 2, images - low):
        step(s)


def keep_parts(sp, i, parts, split_parts, split_out):
    sp.dma_start(split_parts[i.k].rearrange("n p s -> p n s"),
                 parts[:, :, :, :, :].rearrange("p n a z t -> p n (a z t)")).then_inc(split_out[i.k], 16)


def stack_parts(sp, i, split_parts, stack, stacked):
    src = split_parts[i.k].rearrange("n (h e) (a z t) -> e (n h) a z t", e=DIM, a=PARTS, z=2)
    for z, part_of in ((0, PART_OF_Q), (1, PART_OF_K)):
        for slot, part in enumerate(part_of):
            sp.dma_start(stack[i.k][slot * DIM:(slot + 1) * DIM, z, :, :],
                         src[:, :, part, z, :]).then_inc(stacked[i.k], 16)


def window_rows():
    t, ww, rr, c = np.meshgrid(np.arange(2), np.arange(2), np.arange(WIN), np.arange(WIN), indexing="ij")
    right, left = (ww == 1) & (c >= WIN - SHIFT), (ww == 1) & (c < WIN - SHIFT)
    low, high = (t == 1) & (rr >= WIN - SHIFT), (t == 1) & (rr < WIN - SHIFT)
    queries = np.stack([right, left, low, high]).reshape(4, TOKENS).astype(np.float32) * MASKED
    keys = np.stack([left, right, high, low]).reshape(4, TOKENS).astype(np.float32)
    return queries, keys


def relative_points():
    rows, cols = np.meshgrid(np.arange(WIN), np.arange(WIN), indexing="ij")
    at = np.stack([rows.ravel(), cols.ravel()]).astype(np.float32)
    rel = (at[:, :, None] - at[:, None, :]) / np.float32(WIN - 1) * np.float32(8.0)
    rel = np.sign(rel) * np.log2(np.abs(rel) + np.float32(1.0)) / np.float32(3.0)
    return rel.astype(np.float32).reshape(2, 2, HALF, WTOK).transpose(0, 2, 1, 3).reshape(2, WTOK * WTOK)


def build_network(nc, xr, out, given):
    images = xr.shape[1]
    scratch = nc.dram_tensor("scratch_heads", [2, HEADS, TOKENS, DIM], F32).ap()
    split_parts = nc.dram_tensor("scratch_parts", [2, CT, P, PARTS * 2 * TOKENS], BF16).ap()

    with ExitStack() as shared:
        def sb(name, shape, dt=F32, ctx=shared):
            return ctx.enter_context(nc.sbuf_tensor(name, shape, dt))

        X = sb("X", [P, images + 1, CT, TOKENS])
        stats2 = sb("stats2", [P, images, CT, 6])
        probs = [sb(f"probs{k}", [P, 6144]) for k in range(2)]
        stack = [sb(f"stack{k}", [P, 2, HEADS, TOKENS], BF16) for k in range(2)]
        xh = [sb(f"xh{k}", [P, CT, TOKENS]) for k in range(2)]
        parts = sb("parts", [P, CT, PARTS, 2, TOKENS], BF16)
        rest = [sb(f"rest{n}", [P, 2 * TOKENS]) for n in range(2)]
        ident = sb("ident", [P, P])
        gavg = sb("gavg", [P, P])
        A = [shared.enter_context(nc.psum_tensor(f"psA{n}", [P, 512], F32)) for n in range(3)]
        C = [shared.enter_context(nc.psum_tensor(f"psC{n}", [P, 1024], F32)) for n in range(2)]
        E = shared.enter_context(nc.psum_tensor("psE", [P, 512], F32))
        B = [C[1][:, 0:512], C[1][:, 512:1024]]

        with ExitStack() as ctx:
            layer0(nc, ctx, images, xr, given, X, stats2, probs, xh, parts, rest, stack, split_parts, ident, gavg, A, B, C, E)
        with ExitStack() as ctx:
            layer1(nc, ctx, images, out, given, scratch, X, stats2, probs, xh, parts, rest, stack, split_parts, ident, gavg, A, C, E)


def layer0(nc, ctx, images, xr, given, X, stats2, probs, xh, parts, rest, stack, split_parts, ident, gavg, A, B, C, E):
    def sb(name, shape, dt=F32):
        return ctx.enter_context(nc.sbuf_tensor(name, shape, dt))

    def sem(name):
        return ctx.enter_context(nc.semaphore(name))

    prob = [p[:, 0:TT * HEADS * WTOK].rearrange("p (t h q) -> p t h q", t=TT, h=HEADS) for p in probs]
    sq = probs[0][:, 2048:3072].rearrange("p (t c) -> p t c", t=TT)
    qkn = probs[0][:, 3072:4096].rearrange("p (t c) -> p t c", t=TT)
    zb = probs[1][:, 2048:2560].rearrange("p (c t) -> p c t", c=CT)
    rd = probs[1][:, 2560:3072]
    wop = probs[1][:, 3072:5120].rearrange("p (ww g o) -> p ww g o", ww=2, g=QUADS)
    wqk = probs[1][:, 5120:6144].rearrange("p (c o) -> p c o", c=CT)
    hidden = [p[:, 0:WTOK * WTOK // 2] for p in probs]
    wo = xh[0]
    wv = sb("wv0", [P, CT, CH])
    bv = sb("bv0", [P, CT])
    bo = sb("bo0", [P, CT])
    bz = sb("bz0", [P, CT])
    scale = sb("scale0", [P, HEADS])
    ones_win = sb("ones_win", [P, COL])
    pt = stack[1][0:2, :, :, :].rearrange("p z h t -> p (z h t)").bitcast(F32)
    w1 = sb("cpb_w1", [2, HIDDEN])
    b1 = sb("cpb_b1", [HIDDEN, 1])
    w2 = sb("cpb_w2", [HIDDEN, HEADS])
    ebias = sb("ebias", [P, HEADS, WTOK])
    rs = sb("rs", [P, 66])
    rs_bits = sb("rs_bits", [P, 66], I32)
    rs_y = sb("rs_y", [P, 66])
    rs_t = sb("rs_t", [P, 66])
    shift = sb("shift", [P, CT])
    bn = sb("bn", [P, CT, 6])
    mm = sb("mm", [P, 2 * CT])
    gs = sb("gs", [P, CT, 2])
    gm = sb("gm", [P, CT])
    cm = sb("cm", [P, TT, HEADS])
    ct = [sb(f"ct{k}", [HEADS, TOKENS], BF16) for k in range(2)]
    vw = [sb(f"vw{k}", [P, TT, HEADS, 2, DIM]) for k in range(2)]
    ot = sb("ot", [P, TT, QUADS, WTOK])
    table = ot[:, :, :, :].rearrange("p t g q -> p (t g q)")

    x_in = [sem(f"x_in{k}") for k in range(2)]
    split_out = [sem(f"split_out{k}") for k in range(2)]
    stacked = [sem(f"stacked{k}") for k in range(2)]
    c_row = [sem(f"c_row{k}") for k in range(2)]
    pv_done, proj_qk, proj_v, max_ready, s_ready, z_ready, turned, c_turned, g_ready = (
        sem(n) for n in ("pv_done", "proj_qk", "proj_v", "max_ready", "s_ready", "z_ready", "turned",
                         "c_turned", "g_ready"))
    squared, exp_done, z_out, high_out, mid_out, c_out, xh_done, v_out = (
        sem(n) for n in ("squared", "exp_done", "z_out", "high_out", "mid_out", "c_out", "xh_done", "v_out"))
    r_done, o_done, sum_done, gn_chain, rs_ready, max_done, qkn_done, x1_done, rest_out, stats = (
        sem(n) for n in ("r_done", "o_done", "sum_done", "gn_chain", "rs_ready", "max_done", "qkn_done",
                         "x1_done", "rest_out", "stats"))
    newton, biased, low_out, sums_done = (sem(n) for n in ("newton", "biased", "low_out", "sums_done"))
    LAGS = (-1, 6)
    NEWTON = 11

    def by_kind(ap):
        return ap[:, :].rearrange("p (z n t) -> p n z t", z=2, n=CT)

    def by_tile(ap):
        return ap[:, :].rearrange("p (n z t) -> p n z t", n=CT, z=2)

    def tile_parts(part, t):
        return parts[:, :, part, :, t * P:(t + 1) * P]

    def win(t, ww):
        return slice(t * P + ww * WTOK, t * P + (ww + 1) * WTOK)

    c_net, c_in, p_hid, a_hid, p_tab, a_tab, d_tab, a_tab2, tab_in, z_in, p_bz, d_scale, a_scale, d_bz = (
        sem(n) for n in ("c_net", "c_in", "p_hid", "a_hid", "p_tab", "a_tab", "d_tab", "a_tab2", "tab_in", "z_in",
                         "p_bz", "d_scale", "a_scale", "d_bz"))
    net = [(pt, given["points"]), (w1, given["cpb_w1"]), (b1, given["cpb_b1"]), (w2, given["cpb_w2"]),
           (scale, given["scale0"]), (bv, given["bv0"]), (bo, given["bo0"]), (wo, given["wo0"])]
    aux = slice(STACK, STACK + MASKS + 1)
    others = [(gavg, given["gavg"]), (wqk, given["wqk0"]), (ident, given["ident"]), (wv, given["wv0"]),
              (ones_win, given["ones_win"]), (wop, given["wop0"])]
    others += [(stack[k][aux, :, :, :], given["aux"]) for k in range(2)]
    TABLE_STEP = -2

    with nc.Block() as block:
        @block.sync
        def _(sp):
            for group, done in ((net, c_net), (others, c_in)):
                for dst, src in group:
                    sp.dma_start(dst if isinstance(dst, bass.AP) else dst[:], src).then_inc(done, 16)

            def load(i):
                wait_alone(sp, stats, i.plus(-2).count(4, 1))
                src = xr.rearrange("(c p) i t -> p c i t", p=P)[:, :, bass.ds(i.index(), 1), :]
                sp.dma_start(X[:, bass.ds(i.index(1), 1), :, :].rearrange("p i c t -> p c (i t)"),
                             src.rearrange("p c i t -> p c (i t)")).then_inc(x_in[i.k], 16)

            def keep_split(i):
                wait_alone(sp, low_out, i.count(2))
                wait_alone(sp, stacked[i.k], i.plus(-2).dmas(STACK_DMAS))
                keep_parts(sp, i, parts, split_parts, split_out)

            def stack_up(i):
                wait_alone(sp, split_out[i.k], i.dmas(1))
                wait_alone(sp, s_ready, i.plus(-2).count(2))
                stack_parts(sp, i, split_parts, stack, stacked)

            pipeline(sp, images, [(load, 6), (keep_split, 2), (stack_up, 2)], LAGS)

        @block.tensor
        def _(pe):
            pe.wait_ge(c_net, 16 * len(net))
            for o in range(CT):
                for c in range(CT):
                    last = nc.tensor.matmul(E[:, o:o + 1], wo[:, c, o * P:(o + 1) * P], bv[:, c:c + 1],
                                            start=(c == 0), stop=(c == CT - 1))
            last.then_inc(p_bz, 1)
            for n in range(8):
                if n >= 3:
                    pe.wait_ge(a_hid, n - 2)
                nc.tensor.matmul(A[n % 3][:], w1[:], pt[:, 512 * n:512 * n + 512],
                                 start=True, stop=True).then_inc(p_hid, 1)
            pe.wait_ge(a_hid, 8)
            pe.wait_ge(d_bz, 1)
            pe.wait_ge(c_in, 16 * len(others))

            def bias_outputs():
                for q in range(HALF):
                    part, at = divmod(q * P, WTOK * WTOK // 2)
                    last = nc.tensor.matmul(C[0][:, q * HEADS:(q + 1) * HEADS],
                                            hidden[part][:, at:at + P], w2[:], start=True, stop=True)
                last.then_inc(p_tab, 1)

            def weigh(i):
                wait(pe, biased, i.count(2))
                wait(pe, v_out, i.count(2))
                if i.plus(1).among(images):
                    wait(pe, max_done, i.plus(1).count(4))
                for c in range(QUADS):
                    nc.tensor.matmul(B[1][COL * c:COL * c + COL, :].rearrange("p (t g q) -> p t g q", t=TT, g=QUADS),
                                     ones_win[:, :], prob[i.k][:, :, c::QUADS, :], start=True, stop=True,
                                     tile_position=(0, COL * c)).then_inc(sums_done, 1)
                for t in range(TT):
                    for g in range(QUADS):
                        for c in range(QUADS):
                            h = g * QUADS + c
                            at = (t * QUADS + g) * WTOK
                            last = nc.tensor.matmul(B[0][COL * c:COL * c + COL, at:at + WTOK], vw[i.k][:, t, h, :, :],
                                                    prob[i.k][:, t, h, :], start=True, stop=True,
                                                    tile_position=(0, COL * c))
                last.then_inc(pv_done, 1)

            def project(i, t):
                if t == 0:
                    wait(pe, xh_done, i.count(4))
                wait(pe, rest_out, i.plus(-1).count(2, t + 1))
                for c in range(CT):
                    last = nc.tensor.matmul(A[t][:], xh[i.k][:, c, t * P:(t + 1) * P], wqk[:, c, :],
                                            start=(c == 0), stop=(c == CT - 1))
                last.then_inc(proj_qk, 1)

            def project_v(i):
                wait(pe, c_out, i.plus(-1).count(1))
                for t in range(TT):
                    for c in range(CT):
                        last = nc.tensor.matmul(A[2][:, t * CH:(t + 1) * CH], xh[i.k][:, c, t * P:(t + 1) * P],
                                                wv[:, c, :], start=(c == 0), stop=(c == CT - 1))
                last.then_inc(proj_v, 1)

            def maxima(i, n):
                t, g = divmod(n, CT)
                if n == 0:
                    wait(pe, stacked[i.k], i.dmas(STACK_DMAS))
                if n < 2:
                    wait(pe, o_done, i.plus(-2).count(1))
                else:
                    wait(pe, max_done, i.count(4, n - 1))
                rows = slice(0, STACK + MASKS)
                for h in range(TILE_HEADS):
                    for ww in range(2):
                        last = nc.tensor.matmul(B[n % 2][WTOK * ww:WTOK * (ww + 1), h * WTOK:(h + 1) * WTOK],
                                                stack[i.k][rows, 0, g * TILE_HEADS + h, win(t, ww)],
                                                stack[i.k][rows, 1, g * TILE_HEADS + h, win(t, ww)],
                                                start=True, stop=True, skip_group_check=True)
                last.then_inc(max_ready, 1)

            def scores(i, t):
                wait(pe, c_row[i.k], i.dmas(1))
                wait(pe, exp_done, i.count(2, t) if t else i.plus(-1).count(2))
                rows = slice(0, STACK + MASKS + 1)
                for h in range(HEADS):
                    for ww in range(2):
                        last = nc.tensor.matmul(C[0][WTOK * ww:WTOK * (ww + 1), h * WTOK:(h + 1) * WTOK],
                                                stack[i.k][rows, 1, h, win(t, ww)], stack[i.k][rows, 0, h, win(t, ww)],
                                                start=True, stop=True, skip_group_check=True)
                last.then_inc(s_ready, 1)

            def output(i):
                wait(pe, o_done, i.count(1))
                if i.plus(4).among(images):
                    wait(pe, gn_chain, i.plus(4).count(3, 1))
                wait(pe, z_out, i.plus(-1).count(2))
                for o in range(CT):
                    for ww in range(2):
                        dst = E[:, o * TOKENS:(o + 1) * TOKENS].rearrange("p (t rr ww c) -> p ww t rr c", t=TT, rr=WIN, ww=2)
                        for g in range(QUADS):
                            last = nc.tensor.matmul(dst[:, ww], wop[:, ww, g, o * P:(o + 1) * P],
                                                    ot[:, :, g, :].rearrange("p t (rr c) -> p t rr c", rr=WIN),
                                                    start=(g == 0), stop=(g == QUADS - 1))
                last.then_inc(z_ready, 1)

            def turn(i):
                for t in range(TT):
                    wait(pe, qkn_done, i.count(2, t + 1))
                    for n in range(4):
                        last = nc.tensor.transpose(A[t][:, n * P:(n + 1) * P], qkn[:, t, n * P:(n + 1) * P],
                                                   ident[:, :])
                    last.then_inc(turned, 1)

            def turn_c(i):
                wait(pe, max_done, i.count(4))
                wait(pe, v_out, i.count(2))
                for t in range(TT):
                    last = nc.tensor.transpose(A[2][0:HEADS, t * P:(t + 1) * P], cm[:, t, :], ident[:, :])
                last.then_inc(c_turned, 1)

            def groups(i):
                wait(pe, stats, i.count(4))
                wait(pe, z_out, i.plus(-5).count(2))
                nc.tensor.matmul(E[:, 0:4 * CT], gavg[:, :], bn[:, :, :].rearrange("p c (h s) -> p (c h) s", s=3)[:, :, 1:3],
                                 start=True, stop=True).then_inc(g_ready, 1)

            def M(n):
                return lambda i: maxima(i, n), 1

            pipeline(pe, images, [(weigh, -1), (lambda i: scores(i, 0), 0), (project_v, 1),
                                  (lambda i: scores(i, 1), 0), (output, -1), (turn, 2), M(0), M(1),
                                  (lambda i: project(i, 0), 3), (groups, 4), M(2), M(3), (lambda i: project(i, 1), 3),
                                  (turn_c, 1)], LAGS, once=(TABLE_STEP, bias_outputs))

        @block.scalar
        def _(act):
            act.wait_ge(d_scale, 1)
            nc.scalar.activation(scale[:], scale[:], ACT.Exp).then_inc(a_scale, 1)
            for n in range(8):
                act.wait_ge(p_hid, n + 1)
                nc.scalar.activation(hidden[n // 4][:, 512 * (n % 4):512 * (n % 4) + 512], A[n % 3][:], ACT.Relu,
                                     bias=b1[:, 0:1]).then_inc(a_hid, 1)
            act.wait_ge(z_in, 1)
            act.wait_ge(d_bz, 1)

            def finish_table():
                act.wait_ge(p_tab, 1)
                nc.scalar.activation(table, C[0][:, 0:512], ACT.Exp, scale=-1.0).then_inc(a_tab, 1)
                act.wait_ge(d_tab, 2)
                for half in range(2):
                    own = slice(half * WTOK, (half + 1) * WTOK)
                    nc.scalar.activation(ebias[own, :, half * HALF:(half + 1) * HALF].rearrange("p h q -> p q h"),
                                         table[own, :].rearrange("p (q h) -> p q h", h=HEADS),
                                         ACT.Exp, scale=16.0).then_inc(a_tab2, 1)
                act.wait_ge(a_tab2, 2)
                for half in range(2):
                    own, other = slice(half * WTOK, (half + 1) * WTOK), slice((1 - half) * WTOK, (2 - half) * WTOK)
                    queries = slice(half * HALF, (half + 1) * HALF)
                    act.dma_start(ebias[other, :, queries], ebias[own, :, queries]).then_inc(tab_in, 16)

            def square(i):
                wait(act, sum_done, i.plus(-1).count(2))
                for t in range(TT):
                    wait(act, proj_qk, i.count(2, t + 1))
                    nc.scalar.activation(sq[:, t, :], A[t][:], ACT.Square).then_inc(squared, 1)

            def copy_v(i):
                wait(act, proj_v, i.count(1))
                wait(act, pv_done, i.plus(-2).count(1))
                for ww in range(2):
                    rows = slice(ww * WTOK, (ww + 1) * WTOK)
                    nc.scalar.activation(vw[i.k][rows, :, :, ww, :],
                                         A[2][rows, :].rearrange("p (t h e) -> p t h e", t=TT, h=HEADS),
                                         ACT.Copy).then_inc(v_out, 1)

            def exponent(i, t):
                wait(act, s_ready, i.count(2, t + 1))
                wait(act, pv_done, i.plus(-2).count(1))
                nc.scalar.activation(prob[i.k][:, t, :, :].rearrange("p h q -> p (h q)"), C[0][:, :],
                                     ACT.Exp).then_inc(exp_done, 1)

            def copy_z(i):
                wait(act, z_ready, i.count(1))
                wait(act, x1_done, i.plus(-1).count(4))
                for o in range(CT):
                    nc.scalar.activation(zb[:, o, :], E[:, o * TOKENS:(o + 1) * TOKENS], ACT.Identity,
                                         bias=bz[:, o:o + 1]).then_inc(z_out, 1)

            def split_high(i, t):
                wait(act, turned, i.count(2, t + 1))
                if t == 0:
                    wait(act, split_out[1 - i.k], i.plus(-1).dmas(1))
                nc.scalar.activation(tile_parts(0, t), by_kind(A[t]), ACT.Copy).then_inc(high_out, 1)

            def split_middle(i, t):
                wait(act, rest_out, i.count(2, t + 1))
                nc.scalar.activation(tile_parts(1, t), by_tile(rest[t]), ACT.Copy).then_inc(mid_out, 1)

            def copy_c(i):
                wait(act, c_turned, i.count(1))
                wait(act, c_row[i.k], i.plus(-2).dmas(1))
                nc.scalar.activation(ct[i.k][:, :], A[2][0:HEADS, 0:TOKENS], ACT.Copy, scale=-1.0).then_inc(c_out, 1)

            def row_c(i):
                wait(act, c_out, i.count(1))
                wait(act, s_ready, i.plus(-2).count(2))
                act.dma_start(stack[i.k][STACK + MASKS:STACK + MASKS + 1, 0, :, :], ct[i.k][:, :]).then_inc(c_row[i.k], 16)

            def normalize(i):
                wait(act, newton, i.count(NEWTON))
                wait(act, proj_v, i.plus(-2).count(1))
                for c in range(CT):
                    src = X[:, bass.ds(i.index(1), 1), c, :].rearrange("p i (t rr ww c) -> p (i t) rr ww c", t=TT, rr=WIN, ww=2)
                    dst = xh[i.k][:, c, :].rearrange("p (t ww rr c) -> p t rr ww c", t=TT, ww=2, rr=WIN)
                    for ww in range(2):
                        nc.scalar.activation(dst[:, :, :, ww, :], src[:, :, :, ww, :], ACT.Identity,
                                             bias=shift[:, c:c + 1], scale=rs_y[:, 64 + c:65 + c]).then_inc(xh_done, 1)

            pipeline(act, images, [(lambda i: exponent(i, 0), 0), (copy_v, 1), (lambda i: exponent(i, 1), 0),
                                   (normalize, 3), (copy_z, -1), (lambda i: split_high(i, 0), 2),
                                   (lambda i: split_high(i, 1), 2), (lambda i: split_middle(i, 0), 2),
                                   (lambda i: split_middle(i, 1), 2), (square, 3), (copy_c, 1), (row_c, 1)], LAGS,
                     once=(TABLE_STEP, finish_table))

        @block.vector
        def _(dve):
            dve.wait_ge(c_net, 16 * len(net))
            nc.vector.tensor_scalar(scale[:], scale[:], LOG100, None, ALU.min).then_inc(d_scale, 1)
            dve.wait_ge(p_bz, 1)
            nc.vector.tensor_tensor(bz[:], E[:, 0:CT], bo[:], ALU.add).then_inc(d_bz, 1)
            dve.wait_ge(z_in, 1)
            dve.wait_ge(a_scale, 1)

            def invert_table():
                dve.wait_ge(a_tab, 1)
                nc.vector.tensor_scalar(table, table, 1.0, None, ALU.add).then_inc(d_tab, 1)
                dve.wait_ge(d_tab, 1)
                nc.vector.reciprocal(table, table).then_inc(d_tab, 1)

            def outputs(i):
                wait(dve, sums_done, i.count(QUADS))
                wait(dve, o_done, i.plus(-1).count(1))
                nc.vector.reciprocal(rd[:, :], B[1]).then_inc(r_done, 1)
                wait(dve, pv_done, i.count(1))
                wait(dve, r_done, i.count(1))
                wait(dve, z_ready, i.plus(-1).count(1))
                nc.vector.tensor_tensor(ot[:, :, :, :].rearrange("p t g q -> p (t g q)"), B[0], rd[:, :],
                                        ALU.mult).then_inc(o_done, 1)

            def norms(i):
                wait(dve, newton, i.plus(0).count(NEWTON))
                for t in range(TT):
                    wait(dve, squared, i.count(2, t + 1))
                    nc.vector.reduce_sum(rs[:, 32 * t:32 * t + 32], sq[:, t, :].rearrange("p (h e) -> p h e", e=DIM),
                                         AX_X).then_inc(sum_done, 1)

            def variances(i):
                wait(dve, g_ready, i.count(1))
                wait(dve, newton, i.plus(-1).count(NEWTON))
                nc.vector.reduce_sum(gs[:, :, :], E[:, 0:4 * CT].rearrange("p (c h s) -> p c s h", h=2, s=2),
                                     AX_X).then_inc(gn_chain, 1)
                wait(dve, gn_chain, i.count(3, 1))
                nc.vector.tensor_tensor(gm[:, :], gs[:, :, 0], gs[:, :, 0], ALU.mult).then_inc(gn_chain, 1)
                wait(dve, gn_chain, i.count(3, 2))
                nc.vector.scalar_tensor_tensor(out=rs[:, 64:66], in0=gs[:, :, 1], scalar=EPS, in1=gm[:, :],
                                               op0=ALU.add, op1=ALU.subtract).then_inc(gn_chain, 1)

            def seeds(i):
                wait(dve, sum_done, i.plus(-1).count(2))
                if i.among(images):
                    wait(dve, gn_chain, i.count(3))
                wait(dve, xh_done, i.plus(-1).count(4))
                wait(dve, qkn_done, i.plus(-2).count(2))
                nc.vector.tensor_scalar(rs[:, :], rs[:, :], NORM_MIN * NORM_MIN, None, ALU.max).then_inc(rs_ready, 1)
                wait(dve, rs_ready, i.count(3, 1))
                nc.vector.tensor_scalar(rs_bits[:, :], rs[:, :].bitcast(I32), 1, None,
                                        ALU.logical_shift_right).then_inc(rs_ready, 1)
                wait(dve, rs_ready, i.count(3, 2))
                nc.vector.tensor_scalar(rs_y[:, :].bitcast(I32), rs_bits[:, :], -1.0, RSQRT_SEED, ALU.mult,
                                        ALU.add).then_inc(rs_ready, 1)

            def roots(i):
                wait(dve, rs_ready, i.count(3))
                for step in range(3):
                    if step:
                        wait(dve, newton, i.count(NEWTON, 3 * step))
                    nc.vector.scalar_tensor_tensor(out=rs_t[:, :], in0=rs_y[:, :], scalar=-0.5, in1=rs_y[:, :],
                                                   op0=ALU.mult, op1=ALU.mult).then_inc(newton, 1)
                    wait(dve, newton, i.count(NEWTON, 3 * step + 1))
                    nc.vector.tensor_tensor(rs_t[:, :], rs_t[:, :], rs[:, :], ALU.mult).then_inc(newton, 1)
                    wait(dve, newton, i.count(NEWTON, 3 * step + 2))
                    nc.vector.scalar_tensor_tensor(out=rs_y[:, :], in0=rs_t[:, :], scalar=1.5, in1=rs_y[:, :],
                                                   op0=ALU.add, op1=ALU.mult).then_inc(newton, 1)
                wait(dve, newton, i.count(NEWTON, 9))
                q_part = rs_y[:, 0:64].rearrange("p (t n h) -> p t n h", t=TT, n=2)[:, :, 0, :]
                nc.vector.tensor_tensor(q_part, q_part, scale[:, :].unsqueeze(1).to_broadcast([P, TT, HEADS]),
                                        ALU.mult).then_inc(newton, 1)
                nc.vector.scalar_tensor_tensor(out=shift[:, :], in0=gs[:, :, 0], scalar=-1.0, in1=rs_y[:, 64:66],
                                               op0=ALU.mult, op1=ALU.mult).then_inc(newton, 1)

            def take_max(i, n):
                t, g = divmod(n, CT)
                wait(dve, max_ready, i.count(4, n + 1))
                if n == 0:
                    wait(dve, c_turned, i.plus(-1).count(1))
                nc.vector.reduce_max(cm[:, t, g * TILE_HEADS:(g + 1) * TILE_HEADS],
                                     B[n % 2].rearrange("p (h k) -> p h k", k=WTOK), AX_X).then_inc(max_done, 1)

            def unit_qk(i):
                wait(dve, newton, i.plus(1).count(NEWTON))
                wait(dve, turned, i.plus(-1).count(2))
                for t in range(TT):
                    nc.vector.tensor_tensor(qkn[:, t, :].rearrange("p (h e) -> p h e", e=DIM),
                                            A[t][:].rearrange("p (h e) -> p h e", e=DIM),
                                            rs_y[:, 32 * t:32 * t + 32].unsqueeze(2).to_broadcast([P, 32, DIM]),
                                            ALU.mult).then_inc(qkn_done, 1)

            def stats_next(i):
                wait_alone(dve, x1_done, i.count(4))
                for c in range(CT):
                    nc.vector.bn_stats(stats2[:, bass.ds(i.index(), 1), c, :].rearrange("p i s -> p (i s)"),
                                       X[:, bass.ds(i.index(), 1), c, :].rearrange("p i t -> p (i t)"))

            def take_high(i, t):
                wait(dve, high_out, i.count(2, t + 1))
                wait(dve, low_out, i.plus(-1).count(2, t + 1))
                nc.vector.tensor_tensor(by_tile(rest[t]), by_kind(A[t]), tile_parts(0, t), ALU.subtract).then_inc(rest_out, 1)

            def stats_first(i):
                wait_alone(dve, x_in[i.k], i.dmas(1))
                wait_alone(dve, g_ready, i.plus(-1).count(1))
                for c in range(CT):
                    nc.vector.bn_stats(bn[:, c, :], X[:, bass.ds(i.index(1), 1), c, :]
                                       .rearrange("p i t -> p (i t)")).then_inc(stats, 1)
                half = bn[:, :, :].rearrange("p c (h s) -> p (c h) s", s=3)
                wait(dve, stats, i.count(4, 2))
                nc.vector.tensor_tensor(mm[:, :], half[:, :, 1], half[:, :, 1], ALU.mult).then_inc(stats, 1)
                wait(dve, stats, i.count(4, 3))
                nc.vector.scalar_tensor_tensor(out=half[:, :, 2], in0=half[:, :, 2], scalar=2.0 / TOKENS, in1=mm[:, :],
                                               op0=ALU.mult, op1=ALU.add).then_inc(stats, 1)

            def R(n):
                return lambda i: take_max(i, n), 1

            pipeline(dve, images, [(variances, 3), (norms, 2), (outputs, -1), (seeds, 3, 1), (roots, 3, 1), (unit_qk, 2),
                                   (stats_first, 4), (lambda i: take_high(i, 0), 2),
                                   (lambda i: take_high(i, 1), 2), R(0), R(1), R(2), R(3), (stats_next, -1)], LAGS,
                     once=(TABLE_STEP, invert_table))

        @block.gpsimd
        def _(pool):
            for k in range(2):
                nc.gpsimd.memset(vw[k][:], 0.0)
            nc.gpsimd.memset(rs[:], 1.0).then_inc(z_in, 1)
            pool.wait_ge(tab_in, 32)

            def add_bias(i, t):
                wait(pool, exp_done, i.count(2, t + 1))
                both = prob[i.k][:, t, :, :]
                nc.gpsimd.tensor_tensor(both, both, ebias[:, :, :], ALU.mult).then_inc(biased, 1)

            def residual(i):
                wait(pool, z_out, i.count(2))
                for r0, rn, rd_ in ((0, 12, 4), (12, 4, 0)):
                    for c0, cn, cd in ((0, 12, 4), (12, 4, 0)):
                        def part(ap, row, c):
                            return ap.rearrange("p c (i j) -> p c i j", j=SIDE)[:, :, row:row + rn, c:c + cn]
                        old = X[:, bass.ds(i.index(1), 1), :, :].rearrange("p i c t -> p (i c) t")
                        new = X[:, bass.ds(i.index(), 1), :, :].rearrange("p i c t -> p (i c) t")
                        nc.gpsimd.tensor_tensor(part(new, rd_, cd), part(old, r0, c0), part(zb[:, :, :], r0, c0),
                                                ALU.add).then_inc(x1_done, 1)

            def split_low(i, t):
                wait(pool, mid_out, i.count(2, t + 1))
                if t == 0:
                    wait(pool, split_out[1 - i.k], i.plus(-1).dmas(1))
                nc.gpsimd.tensor_tensor(tile_parts(2, t), by_tile(rest[t]), tile_parts(1, t), ALU.subtract).then_inc(low_out, 1)

            pipeline(pool, images, [(lambda i: add_bias(i, 0), 0), (lambda i: add_bias(i, 1), 0), (residual, -1),
                                    (lambda i: split_low(i, 0), 2), (lambda i: split_low(i, 1), 2)], LAGS)


class Part:

    def __init__(self, block, head, heads, start, size):
        self.block, self.head, self.heads, self.start, self.size = block, head, heads, start, size
        self.cols = slice(start, start + size)
        self.ahead = head >= TILE_HEADS
        self.diagonal = block * P - start


SCORES = ([Part(0, h, 2, 0, TOKENS) for h in range(0, 8, 2)] + [Part(1, h, 4, P, P) for h in range(0, 8, 4)]
          + [Part(0, h, 4, 0, P) for h in range(8, 16, 4)] + [Part(1, h, 2, 0, TOKENS) for h in range(8, 16, 2)])
MAXIMA = ([Part(0, h, 4, 0, P) for h in range(0, 8, 4)] + [Part(1, h, 2, 0, TOKENS) for h in range(0, 8, 2)]
          + [Part(0, h, 2, 0, TOKENS) for h in range(8, 16, 2)] + [Part(1, h, 4, P, P) for h in range(8, 16, 4)])
LOGIT_BANKS = len(SCORES)
MASKED_PARTS = ((0, 3), (4, 5), (6, 7), (8, 11))


def layer1(nc, ctx, images, out, given, scratch, X, stats2, probs, xh, parts, rest, stack, split_parts, ident, gavg, A, C, E):
    def sb(name, shape, dt=F32):
        return ctx.enter_context(nc.sbuf_tensor(name, shape, dt))

    def sem(name):
        return ctx.enter_context(nc.semaphore(name))

    def by_tile(ap):
        return ap[:, :].rearrange("p (t n) -> p t n", t=CT)

    wqk = sb("wqk1", [P, CT, 2 * CH])
    wv = sb("wv1", [P, CT, CH])
    wo = sb("wo1", [P, CT, CH])
    identb = sb("identb", [P, P], BF16)
    below = sb("below", [P, P], BF16)
    above = sb("above", [P, P], BF16)
    cm = sb("cm1", [P, TT, HEADS])
    ct = [sb(f"ct1{k}", [HEADS, TOKENS], BF16) for k in range(2)]
    va = [sb(f"va{k}", [P, TT, HEADS, COL]) for k in range(2)]
    ots = sb("ots", [P, QUADS, TOKENS])
    rdn = sb("rdn", [P, TT * HEADS])
    on = sb("on", [P, TT, CH])
    rows = sb("rows", [P, TT, CH])
    of = sb("of", [P, CT, TOKENS])
    n_stat = images * CT
    gs = probs[0][:, 0:2 * n_stat].rearrange("p (n s) -> p n s", s=2)
    gm, rs, rs_half, rs_t = (probs[0][:, (2 + n) * n_stat:(3 + n) * n_stat] for n in range(4))
    rs_bits = probs[0][:, 6 * n_stat:7 * n_stat].bitcast(I32)
    mm = probs[0][:, 7 * n_stat:9 * n_stat]
    rs_y = sb("rs1_y", [P, images, CT])
    shift = sb("shift1", [P, images, CT])
    flat_y = rs_y[:, :, :].rearrange("p i c -> p (i c)")

    c_in, z_in, sum_in, g_ready, var, newton = (sem(n) for n in ("c_in1", "z_in1", "sum_in", "g_ready1", "var1", "newton1"))
    loads = [(wqk, given["wqk1"]), (wv, given["wv1"]), (wo, given["wo1"]), (identb, given["identb"]), (below, given["below"]),
             (above, given["above"])]
    with nc.Block() as block:
        @block.sync
        def _(sp):
            for dst, src in loads:
                sp.dma_start(dst[:], src).then_inc(c_in, 16)
            for k in range(2):
                sp.dma_start(stack[k][STACK:STACK + 1, 1, :, :],
                             stack[k][STACK + MASKS:STACK + MASKS + 1, 1, :, :]).then_inc(c_in, 16)
            sp.wait_ge(c_in, 16 * (len(loads) + 2))

        @block.vector
        def _(dve):
            half = stats2[:, :, :, :].rearrange("p i c (h s) -> p (i c h) s", s=3)
            nc.vector.tensor_tensor(mm, half[:, :, 1], half[:, :, 1], ALU.mult).then_inc(var, 1)
            dve.wait_ge(var, 1)
            nc.vector.scalar_tensor_tensor(out=half[:, :, 2], in0=half[:, :, 2], scalar=2.0 / TOKENS, in1=mm,
                                           op0=ALU.mult, op1=ALU.add).then_inc(sum_in, 1)
            dve.wait_ge(g_ready, 1)
            nc.vector.reduce_sum(gs[:, :, :], E[:, 0:4 * n_stat].rearrange("p (n h s) -> p n s h", h=2, s=2),
                                 AX_X).then_inc(var, 1)
            dve.wait_ge(var, 2)
            nc.vector.tensor_tensor(gm[:, :], gs[:, :, 0], gs[:, :, 0], ALU.mult).then_inc(var, 1)
            dve.wait_ge(var, 3)
            nc.vector.scalar_tensor_tensor(out=rs[:, :], in0=gs[:, :, 1], scalar=EPS, in1=gm[:, :],
                                           op0=ALU.add, op1=ALU.subtract).then_inc(var, 1)
            dve.wait_ge(var, 4)
            nc.vector.tensor_scalar(rs_half[:, :], rs[:, :], -0.5, None, ALU.mult).then_inc(var, 1)
            nc.vector.tensor_scalar(rs_bits[:, :], rs[:, :].bitcast(I32), 1, None,
                                    ALU.logical_shift_right).then_inc(var, 1)
            dve.wait_ge(var, 6)
            nc.vector.tensor_scalar(flat_y.bitcast(I32), rs_bits[:, :], -1.0, RSQRT_SEED, ALU.mult,
                                    ALU.add).then_inc(var, 1)
            dve.wait_ge(var, 7)
            for step in range(3):
                nc.vector.tensor_tensor(rs_t[:, :], flat_y, flat_y, ALU.mult).then_inc(newton, 1)
                dve.wait_ge(newton, 3 * step + 1)
                nc.vector.tensor_tensor(rs_t[:, :], rs_t[:, :], rs_half[:, :], ALU.mult).then_inc(newton, 1)
                dve.wait_ge(newton, 3 * step + 2)
                nc.vector.scalar_tensor_tensor(out=flat_y, in0=rs_t[:, :], scalar=1.5, in1=flat_y,
                                               op0=ALU.add, op1=ALU.mult).then_inc(newton, 1)
                dve.wait_ge(newton, 3 * step + 3)
            nc.vector.scalar_tensor_tensor(out=shift[:, :, :].rearrange("p i c -> p (i c)"), in0=gs[:, :, 0],
                                           scalar=-1.0, in1=flat_y, op0=ALU.mult, op1=ALU.mult).then_inc(newton, 1)
            dve.wait_ge(newton, 10)

        @block.tensor
        def _(pe):
            pe.wait_ge(sum_in, 1)
            nc.tensor.matmul(E[:, 0:4 * n_stat], gavg[:, :],
                             stats2[:, :, :, :].rearrange("p i c (h s) -> p (i c h) s", s=3)[:, :, 1:3],
                             start=True, stop=True).then_inc(g_ready, 1)

        @block.gpsimd
        def _(pool):
            for k in range(2):
                nc.gpsimd.memset(va[k][:], 0.0).then_inc(z_in, 1)
            pool.wait_ge(z_in, 2)
            for k in range(2):
                nc.gpsimd.memset(va[k][:, :, :, DIM:DIM + 1], 1.0).then_inc(z_in, 1)
            pool.wait_ge(z_in, 4)

    split_out, stacked, c_row, stored, loaded, y_out = (
        [sem(f"{n}{k}") for k in range(2)] for n in ("l1_split_out", "l1_stacked", "l1_c_row", "stored", "loaded", "y_out"))
    pv_done, proj_q, proj_k, proj_v, max_ready, s_ready, turned, c_turned, f_turned, z_ready = (
        sem("l1_" + n) for n in ("pv_done", "proj_q", "proj_k", "proj_v", "max_ready", "s_ready", "turned", "c_turned",
                                 "f_turned", "z_ready"))
    exp_done, ot_out, f_out, v_out, high_out, mid_out, c_out, xh_done = (
        sem("l1_" + n) for n in ("exp_done", "ot_out", "f_out", "v_out", "high_out", "mid_out", "c_out", "xh_done"))
    max_done, y_done, rest_out, low_out, r_done, on_done, masked = (
        sem("l1_" + n) for n in ("max_done", "y_done", "rest_out", "low_out", "r_done", "on_done", "masked"))
    LAGS = (-2, 3)

    with nc.Block() as block:
        @block.sync
        def _(sp):
            def keep_split(i):
                wait_alone(sp, low_out, i.count(2))
                wait_alone(sp, stacked[i.k], i.plus(-2).dmas(STACK_DMAS))
                keep_parts(sp, i, parts, split_parts, split_out)

            def stack_up(i):
                wait_alone(sp, split_out[i.k], i.dmas(1))
                wait_alone(sp, s_ready, i.plus(-2).count(LOGIT_BANKS))
                stack_parts(sp, i, split_parts, stack, stacked)

            def regroup(i):
                wait_alone(sp, on_done, i.count(1))
                wait_alone(sp, loaded[i.k], i.plus(-2).dmas(1))
                for t in range(TT):
                    sp.dma_start(scratch[i.k, :, t * P:(t + 1) * P, :].rearrange("h p e -> p h e"),
                                 on[:, t, :].rearrange("p (h e) -> p h e", h=HEADS)).then_inc(stored[i.k], 16)

            def fetch(i):
                wait_alone(sp, stored[i.k], i.dmas(TT))
                wait_alone(sp, f_turned, i.plus(-1).count(1))
                sp.dma_start(rows[:, :, :],
                             scratch[i.k].rearrange("h n e -> (h n e)").rearrange("(t p f) -> p t f", p=P, f=CH)
                             ).then_inc(loaded[i.k], 16)

            def store(i):
                wait_alone(sp, y_done, i.count(1))
                wait_alone(sp, y_out[i.k], i.plus(-2).dmas(1))
                sp.dma_start(out.rearrange("(c p) i t -> p c i t", p=P)[:, :, bass.ds(i.index(), 1), :]
                             .rearrange("p c i t -> p c (i t)"),
                             X[:, bass.ds(i.index(), 1), :, :].rearrange("p i c t -> p c (i t)")).then_inc(y_out[i.k], 16)

            pipeline(sp, images, [(keep_split, 2), (stack_up, 2), (store, -2), (regroup, -1), (fetch, -1)], LAGS)
            for k in range(2):
                sp.wait_ge(y_out[k], 16 * ((images + 1 - k) // 2))

        @block.tensor
        def _(pe):
            def scores(i, part):
                if part == 0:
                    wait(pe, c_row[i.k], i.dmas(1))
                if part < 2:
                    wait(pe, exp_done, i.plus(-1).count(LOGIT_BANKS))
                    wait(pe, on_done, i.plus(-2).count(1))
                else:
                    wait(pe, exp_done, i.count(LOGIT_BANKS, part - 1))
                s = SCORES[part]
                bank = C[0][:, part % 2 * 512:(part % 2 + 1) * 512].rearrange("p (h q) -> p h q", h=s.heads)
                for n in range(s.heads):
                    last = nc.tensor.matmul(bank[:, n, :], stack[i.k][0:STACK + 1, 1, s.head + n, s.block * P:(s.block + 1) * P],
                                            stack[i.k][0:STACK + 1, 0, s.head + n, s.cols], start=True, stop=True,
                                            skip_group_check=True)
                last.then_inc(s_ready, 1)

            def maxima(i, part):
                if part == 0:
                    wait(pe, stacked[i.k], i.dmas(STACK_DMAS))
                if part < 2:
                    wait(pe, max_done, i.plus(-1).count(LOGIT_BANKS))
                else:
                    wait(pe, max_done, i.count(LOGIT_BANKS, part - 1))
                s = MAXIMA[part]
                bank = C[1][:, part % 2 * 512:(part % 2 + 1) * 512].rearrange("p (h k) -> p h k", h=s.heads)
                for n in range(s.heads):
                    nc.tensor.matmul(bank[:, n, :], stack[i.k][0:STACK, 0, s.head + n, s.block * P:(s.block + 1) * P],
                                     stack[i.k][0:STACK, 1, s.head + n, s.cols], start=(n == 0), stop=False,
                                     skip_group_check=True)
                mask = (below if s.ahead else above)[:, :].unsqueeze(1).to_broadcast([P, s.heads, P])
                nc.tensor.matmul(bank[:, :, s.diagonal:s.diagonal + P], identb[:, :], mask,
                                 start=False, stop=True, skip_group_check=True).then_inc(max_ready, 1)

            def weigh(i, g):
                if g == 0:
                    wait(pe, masked, i.count(len(MASKED_PARTS)))
                    wait(pe, v_out, i.count(1))
                    wait(pe, ot_out, i.plus(-1).count(2))
                if g % 2 == 0:
                    n = g // 2
                    if i.plus(2 + n).among(images):
                        wait(pe, rest_out, i.plus(2 + n).count(2, 2 - n))
                for part in range(2):
                    for c in range(QUADS):
                        h = g * QUADS + c
                        block = part if g < 2 else 1 - part
                        n = next(n for n, s in enumerate(SCORES) if s.block == block and s.head <= h < s.head + s.heads)
                        s = SCORES[n]
                        at = 512 * n + (h - s.head) * s.size
                        to = (g % 2) * TOKENS + s.start
                        last = nc.tensor.matmul(A[g // 2][COL * c:COL * (c + 1), to:to + s.size], va[i.k][:, block, h, :],
                                                probs[i.k][:, at:at + s.size], start=(part == 0), stop=(part == 1),
                                                tile_position=(0, COL * c), skip_group_check=True)
                last.then_inc(pv_done, 1)

            def project_qk(i, n):
                if n == 0:
                    wait(pe, xh_done, i.count(2))
                wait(pe, ot_out, i.plus(-4 + n).count(2, 2 - n))
                if n == 0:
                    wait(pe, rest_out, i.plus(-1).count(2))
                for o in range(CT):
                    for c in range(CT):
                        last = nc.tensor.matmul(A[1 - n][:, o * TOKENS:(o + 1) * TOKENS],
                                                wqk[:, c, n * CH + o * P:n * CH + (o + 1) * P], xh[i.k][:, c, :],
                                                start=(c == 0), stop=(c == CT - 1))
                last.then_inc(proj_k if n else proj_q, 1)

            def project_v(i):
                wait(pe, xh_done, i.count(2))
                wait(pe, v_out, i.plus(-1).count(1))
                for t in range(TT):
                    for c in range(CT):
                        last = nc.tensor.matmul(A[2][:, t * CH:(t + 1) * CH], xh[i.k][:, c, t * P:(t + 1) * P],
                                                wv[:, c, :], start=(c == 0), stop=(c == CT - 1))
                last.then_inc(proj_v, 1)

            def turn_c(i):
                wait(pe, max_done, i.count(LOGIT_BANKS))
                wait(pe, y_done, i.plus(-3).count(1))
                for t in range(TT):
                    last = nc.tensor.transpose(E[0:HEADS, t * P:(t + 1) * P], cm[:, t, :], ident[:, :])
                last.then_inc(c_turned, 1)

            def turn(i):
                wait(pe, ot_out, i.count(2))
                wait(pe, on_done, i.plus(-1).count(1))
                if i.plus(1).among(images):
                    wait(pe, exp_done, i.plus(1).count(LOGIT_BANKS))
                for t in range(TT):
                    for g in range(QUADS):
                        last = nc.tensor.transpose(C[0][:, t * 512 + g * P:t * 512 + (g + 1) * P],
                                                   ots[:, g, t * P:(t + 1) * P], ident[:, :])
                last.then_inc(turned, 1)

            def turn_rows(i):
                wait(pe, loaded[i.k], i.dmas(1))
                wait(pe, y_done, i.plus(-1).count(1))
                if i.plus(2).among(images):
                    wait(pe, c_out, i.plus(2).count(1))
                for t in range(TT):
                    for f in range(CT):
                        last = nc.tensor.transpose(E[:, f * TOKENS + t * P:f * TOKENS + (t + 1) * P],
                                                   rows[:, t, f * P:(f + 1) * P], ident[:, :])
                last.then_inc(f_turned, 1)

            def output(i):
                wait(pe, f_out, i.count(1))
                for o in range(CT):
                    for f in range(CT):
                        last = nc.tensor.matmul(E[:, o * TOKENS:(o + 1) * TOKENS], wo[:, f, o * P:(o + 1) * P],
                                                of[:, f, :], start=(f == 0), stop=(f == CT - 1))
                last.then_inc(z_ready, 1)

            def S(part):
                return lambda i: scores(i, part), 0

            def M(part):
                return lambda i: maxima(i, part), 1

            def W(g):
                return lambda i: weigh(i, g), 0 if g < 2 else -1

            pipeline(pe, images, [(lambda i: project_qk(i, 0), 2), (lambda i: project_qk(i, 1), 2), S(0), S(1), M(0),
                                  M(1), S(2), S(3), W(2), M(2), M(3), S(4), S(5), W(3), M(4), M(5), S(6), S(7), M(6),
                                  (turn_rows, -2), M(7), S(8), S(9), M(8), S(10), S(11), (output, -2), M(9),
                                  (turn, -1), (project_v, 1), M(10), M(11), W(0), (turn_c, 1), W(1)], LAGS)

        @block.scalar
        def _(act):
            def exponent(i, part):
                wait(act, s_ready, i.count(LOGIT_BANKS, part + 1))
                if part == 0:
                    wait(act, pv_done, i.plus(-2).count(QUADS))
                nc.scalar.activation(probs[i.k][:, part * 512:(part + 1) * 512],
                                     C[0][:, part % 2 * 512:(part % 2 + 1) * 512], ACT.Exp).then_inc(exp_done, 1)

            def copy_outputs(i, n):
                wait(act, pv_done, i.count(QUADS, 2 * n + 2))
                wait(act, turned, i.plus(-1).count(1))
                nc.scalar.activation(ots[:, 2 * n:2 * n + 2, :].rearrange("p g q -> p (g q)"), A[n][:, :],
                                     ACT.Copy).then_inc(ot_out, 1)

            def copy_rows(i):
                wait(act, f_turned, i.count(1))
                wait(act, z_ready, i.plus(-1).count(1))
                nc.scalar.activation(of[:, :, :].rearrange("p f t -> p (f t)"), E[:, :], ACT.Copy).then_inc(f_out, 1)

            def copy_v(i):
                wait(act, proj_v, i.count(1))
                wait(act, pv_done, i.plus(-2).count(QUADS))
                nc.scalar.activation(va[i.k][:, :, :, 0:DIM].rearrange("p t h e -> p (t h) e"),
                                     A[2][:, :].rearrange("p (n e) -> p n e", e=DIM), ACT.Copy).then_inc(v_out, 1)

            def split_high(i, n):
                wait(act, proj_k if n else proj_q, i.count(1))
                if n == 0:
                    wait(act, split_out[1 - i.k], i.plus(-1).dmas(1))
                nc.scalar.activation(parts[:, :, 0, n, :], by_tile(A[1 - n]), ACT.Copy,
                                     scale=1.0 if n else DIM ** -0.5).then_inc(high_out, 1)

            def split_middle(i, n):
                wait(act, rest_out, i.count(2, n + 1))
                nc.scalar.activation(parts[:, :, 1, n, :], by_tile(rest[n]), ACT.Copy).then_inc(mid_out, 1)

            def copy_c(i):
                wait(act, c_turned, i.count(1))
                wait(act, c_row[i.k], i.plus(-2).dmas(1))
                nc.scalar.activation(ct[i.k][:, :], E[0:HEADS, 0:TOKENS], ACT.Copy, scale=-1.0).then_inc(c_out, 1)

            def row_c(i):
                wait(act, c_out, i.count(1))
                wait(act, s_ready, i.plus(-2).count(LOGIT_BANKS))
                act.dma_start(stack[i.k][STACK:STACK + 1, 0, :, :], ct[i.k][:, :]).then_inc(c_row[i.k], 16)

            def normalize(i):
                wait(act, proj_v, i.plus(-2).count(1))
                wait(act, proj_k, i.plus(-2).count(1))
                for c in range(CT):
                    nc.scalar.activation(xh[i.k][:, c, :], X[:, bass.ds(i.index(), 1), c, :].rearrange("p i t -> p (i t)"),
                                         ACT.Identity,
                                         bias=shift[:, bass.ds(i.index(), 1), c],
                                         scale=rs_y[:, bass.ds(i.index(), 1), c]).then_inc(xh_done, 1)

            def X_(part):
                return lambda i: exponent(i, part), 0

            pipeline(act, images, [(lambda i: copy_outputs(i, 0), -1), (lambda i: split_high(i, 0), 2),
                                   (lambda i: split_high(i, 1), 2), X_(0), X_(1), (lambda i: split_middle(i, 0), 2),
                                   X_(2), X_(3), (lambda i: split_middle(i, 1), 2), X_(4), X_(5),
                                   (lambda i: copy_outputs(i, 1), -1), X_(6), X_(7), (copy_rows, -2), X_(8), X_(9),
                                   X_(10), X_(11), (copy_v, 1), (normalize, 3), (copy_c, 1), (row_c, 1)], LAGS)

        @block.vector
        def _(dve):
            def take_max(i, part):
                s = MAXIMA[part]
                wait(dve, max_ready, i.count(LOGIT_BANKS, part + 1))
                if part == 0:
                    wait(dve, c_turned, i.plus(-1).count(1))
                nc.vector.reduce_max(cm[:, s.block, s.head:s.head + s.heads],
                                     C[1][:, part % 2 * 512:(part % 2 + 1) * 512].rearrange("p (h k) -> p h k", k=s.size),
                                     AX_X).then_inc(max_done, 1)

            def residual(i):
                wait(dve, z_ready, i.count(1))
                x = X[:, bass.ds(i.index(), 1), :, :].rearrange("p i c t -> p (i c t)")
                nc.vector.tensor_tensor(x, E[:, :], x, ALU.add).then_inc(y_done, 1)

            def take_high(i, n):
                wait(dve, high_out, i.count(2, n + 1))
                wait(dve, low_out, i.plus(-1).count(2, n + 1))
                nc.vector.scalar_tensor_tensor(out=by_tile(rest[n]), in0=by_tile(A[1 - n]), scalar=1.0 if n else DIM ** -0.5,
                                               in1=parts[:, :, 0, n, :], op0=ALU.mult,
                                               op1=ALU.subtract).then_inc(rest_out, 1)

            def divide(i):
                wait(dve, turned, i.count(1))
                wait(dve, stored[1 - i.k], i.plus(-1).dmas(TT))
                heads = C[0][:, :].rearrange("p (n e) -> p n e", e=COL)
                nc.vector.reciprocal(rdn[:, :], heads[:, :, DIM]).then_inc(r_done, 1)
                wait(dve, r_done, i.count(1))
                nc.vector.tensor_tensor(on[:, :, :].rearrange("p t (h e) -> p (t h) e", e=DIM), heads[:, :, 0:DIM],
                                        rdn[:, :].unsqueeze(2).to_broadcast([P, TT * HEADS, DIM]),
                                        ALU.mult).then_inc(on_done, 1)

            def R(part):
                return lambda i: take_max(i, part), 1

            pipeline(dve, images, [(lambda i: take_high(i, 0), 2), (lambda i: take_high(i, 1), 2), R(0), R(1), R(2), R(3),
                                   R(4), R(5), R(6), R(7), (residual, -2), R(8), R(9), (divide, -1), R(10), R(11)], LAGS)

        @block.gpsimd
        def _(pool):
            def mask(i, n):
                first, last = MASKED_PARTS[n]
                s = SCORES[first]
                wait_alone(pool, exp_done, i.count(LOGIT_BANKS, last + 1))
                weights = (probs[i.k][:, 512 * first:512 * (last + 1)]
                           .rearrange("p (h q) -> p h q", q=s.size)[:, :, s.diagonal:s.diagonal + P])
                sign = -1 if s.ahead else 1
                nc.gpsimd.affine_select(out=weights, in_=weights, compare_op=ALU.is_ge, fill=0.0, base=0,
                                        pattern=[[0, weights.shape[1]], [sign, P]],
                                        channel_multiplier=-sign).then_inc(masked, 1)

            def split_low(i, n):
                wait(pool, mid_out, i.count(2, n + 1))
                if n == 0:
                    wait(pool, split_out[1 - i.k], i.plus(-1).dmas(1))
                nc.gpsimd.tensor_tensor(parts[:, :, 2, n, :], by_tile(rest[n]), parts[:, :, 1, n, :],
                                        ALU.subtract).then_inc(low_out, 1)

            def K(n):
                return lambda i: mask(i, n), 0

            pipeline(pool, images, [K(0), (lambda i: split_low(i, 0), 2), K(1), (lambda i: split_low(i, 1), 2), K(2), K(3)],
                     LAGS)


def lay_out(x, L0_conv_Wq, L0_conv_Wk, L0_conv_Wv, L0_conv_bv, L0_conv_Wo, L0_conv_bo, L0_conv_logit_scale,
            L0_conv_cpb_w1, L0_conv_cpb_b1, L0_conv_cpb_w2, L1_conv_Wq_lb, L1_conv_Wk_lb, L1_conv_Wv_lb,
            L1_conv_Wq_la, L1_conv_Wk_la, L1_conv_Wv_la, L1_conv_Wo):
    bfloat16 = mybir.dt.np(BF16)

    def rows(*weights):
        t = np.concatenate([np.asarray(a).reshape(-1, CH).T for a in weights], axis=1)
        return t.reshape(CT, P, -1).transpose(1, 0, 2)

    def column(a):
        return np.asarray(a).reshape(CT, P).T

    images = x.shape[0]
    rolled = np.roll(np.asarray(x), (-SHIFT, -SHIFT), axis=(1, 2)).reshape(images, TOKENS, CH)
    wo = rows(L0_conv_Wo)
    by_head = np.asarray(L0_conv_Wo).T.reshape(QUADS, QUADS, DIM, CH)
    wop = np.zeros((QUADS, 2, DIM, 2, QUADS, CH), wo.dtype)
    for ww in range(2):
        wop[:, ww, :, ww] = by_head.transpose(1, 2, 0, 3)
    queries, keys = window_rows()
    aux = np.zeros((MASKS + 1, 2, HEADS, TOKENS), np.float32)
    aux[0:MASKS, 0], aux[0:MASKS, 1], aux[MASKS, 1] = queries[:, None, :], keys[:, None, :], 1.0
    ones_win = np.zeros((2, WTOK, 2, DIM), np.float32)
    for ww in range(2):
        ones_win[ww, :, ww] = 1.0
    return {
        "xr": rolled.transpose(2, 0, 1),
        "wqk0": rows(L0_conv_Wq, L0_conv_Wk), "wv0": rows(L0_conv_Wv), "wo0": wo,
        "wop0": wop.reshape(P, 2, QUADS, CH), "bv0": column(L0_conv_bv), "bo0": column(L0_conv_bo),
        "scale0": np.broadcast_to(np.asarray(L0_conv_logit_scale).reshape(1, HEADS), (P, HEADS)),
        "cpb_w1": np.asarray(L0_conv_cpb_w1).T, "cpb_b1": np.asarray(L0_conv_cpb_b1).reshape(HIDDEN, 1),
        "cpb_w2": np.asarray(L0_conv_cpb_w2).T, "points": relative_points(),
        "ident": np.eye(P, dtype=np.float32),
        "gavg": np.kron(np.eye(P // GROUP), np.full((GROUP, GROUP), 0.5 / GROUP)).astype(np.float32),
        "ones_win": ones_win.reshape(P, COL),
        "aux": aux.astype(bfloat16),
        "wqk1": rows(L1_conv_Wq_lb, L1_conv_Wq_la, L1_conv_Wk_lb, L1_conv_Wk_la),
        "wv1": rows(L1_conv_Wv_lb, L1_conv_Wv_la), "wo1": rows(L1_conv_Wo),
        "identb": np.eye(P).astype(bfloat16),
        "below": (np.tril(np.ones((P, P)), -1) * MASKED).astype(bfloat16),
        "above": (np.triu(np.ones((P, P)), 1) * MASKED).astype(bfloat16),
    }


def kernel(**inputs):
    import concourse.bacc as bacc
    from concourse.bass_utils import run_bass_kernel_spmd

    arrays = {"in_" + n: np.ascontiguousarray(a) for n, a in lay_out(**inputs).items()}
    images = inputs["x"].shape[0]
    nc = bacc.Bacc("TRN2", target_bir_lowering=False, num_devices=1)
    ins = {n[3:]: nc.dram_tensor(n, a.shape, mybir.dt.from_np(a.dtype), kind="ExternalInput").ap()
           for n, a in arrays.items()}
    out = nc.dram_tensor("out", (CH, images, TOKENS), F32, kind="ExternalOutput").ap()
    build_network(nc, ins.pop("xr"), out, ins)
    got = run_bass_kernel_spmd(nc, [arrays], core_ids=[0]).results[0]["out"]
    return np.ascontiguousarray(got.transpose(1, 2, 0)).reshape(images, SIDE, SIDE, CH)
```
